# Optimizing a Trainium2 kernel written in Bass

```python
import numpy as np
import jax
import jax.numpy as jnp

def _softmax(x, axis=-1):
    return jax.nn.softmax(x, axis=axis)

def _gelu(x):
    return jax.nn.gelu(x, approximate=True)

def _silu(x):
    return jax.nn.silu(x)

def _sigmoid(x):
    return jax.nn.sigmoid(x)

def _layernorm(x, axis=-1, eps=1e-05):
    m = jnp.mean(x, axis=axis, keepdims=True)
    v = jnp.var(x, axis=axis, keepdims=True)
    return (x - m) / jnp.sqrt(v + eps)

def _scatter_add(tgt, idx, src, axis=0):
    return tgt.at[idx].add(src)

def _segment_sum(src, seg, n):
    return jax.ops.segment_sum(src, seg, n)
kernel_name = 'mk_seq_preln_d2_jaxref_r8_9fd5c4'

def setup_inputs(seed: int=0):
    np.random.seed(seed)
    _w = jnp.asarray

    def _L0_attn_setup():
        import jax, jax.numpy as jnp
        import numpy as np
        H_SIZE = 256
        NUM_K_HEADS = 16
        NUM_V_HEADS = 32
        DK = 128
        DV = 128
        KEY_DIM = NUM_K_HEADS * DK
        VALUE_DIM = NUM_V_HEADS * DV
        CONV_DIM = 2 * KEY_DIM + VALUE_DIM
        KERNEL = 4
        EPS = 1e-06
        B, S = (2, 256)

        def _l2norm(x, eps=1e-06):
            return x * jax.lax.rsqrt(jnp.sum(x * x, axis=-1, keepdims=True) + eps)

        def _causal_conv(x, w):
            K = w.shape[-1]
            Sq = x.shape[1]
            xp = jnp.pad(x, ((0, 0), (K - 1, 0), (0, 0)))
            out = xp[:, 0:Sq, :] * w[None, None, :, 0]
            for j in range(1, K):
                out = out + xp[:, j:j + Sq, :] * w[None, None, :, j]
            return out

        def _forward(hidden_states, w_qkv, w_z, w_b, w_a, conv_w, dt_bias, A_log, norm_gamma, w_out):
            Bq, Sq, _ = hidden_states.shape
            mixed = hidden_states @ w_qkv
            z = (hidden_states @ w_z).reshape(Bq, Sq, NUM_V_HEADS, DV)
            b = hidden_states @ w_b
            a = hidden_states @ w_a
            mixed = jax.nn.silu(_causal_conv(mixed, conv_w))
            q, k, v = jnp.split(mixed, [KEY_DIM, 2 * KEY_DIM], axis=-1)
            q = q.reshape(Bq, Sq, NUM_K_HEADS, DK)
            k = k.reshape(Bq, Sq, NUM_K_HEADS, DK)
            v = v.reshape(Bq, Sq, NUM_V_HEADS, DV)
            nrep = NUM_V_HEADS // NUM_K_HEADS
            q = jnp.repeat(q, nrep, axis=2)
            k = jnp.repeat(k, nrep, axis=2)
            beta = jax.nn.sigmoid(b)
            g = -jnp.exp(A_log)[None, None, :] * jax.nn.softplus(a + dt_bias[None, None, :])
            qf = _l2norm(q.astype(jnp.float32)) * DK ** (-0.5)
            kf = _l2norm(k.astype(jnp.float32))
            vf = v.astype(jnp.float32)
            gf = g.astype(jnp.float32)
            bf = beta.astype(jnp.float32)

            def step(state, xs):
                q_t, k_t, v_t, g_t, b_t = xs
                state = state * jnp.exp(g_t)[..., None, None]
                kv = jnp.einsum('bhk,bhkv->bhv', k_t, state)
                delta = (v_t - kv) * b_t[..., None]
                state = state + jnp.einsum('bhk,bhv->bhkv', k_t, delta)
                out = jnp.einsum('bhk,bhkv->bhv', q_t, state)
                return (state, out)
            mv = lambda x: jnp.moveaxis(x, 1, 0)
            xs = (mv(qf), mv(kf), mv(vf), mv(gf), mv(bf))
            state0 = jnp.zeros((Bq, NUM_V_HEADS, DK, DV), jnp.float32)
            _, outs = jax.lax.scan(step, state0, xs)
            o = jnp.moveaxis(outs, 0, 1)
            o = o * jax.nn.silu(z.astype(jnp.float32))
            o = o * jax.lax.rsqrt(jnp.mean(o * o, axis=-1, keepdims=True) + EPS)
            o = o * norm_gamma
            o = o.reshape(Bq, Sq, VALUE_DIM).astype(hidden_states.dtype)
            return o @ w_out
        key = jax.random.key(seed)
        ks = jax.random.split(key, 8)
        w = lambda k, shape, s: jax.random.normal(k, shape, jnp.float32) * s
        return {'hidden_states': jax.random.normal(ks[0], (B, S, H_SIZE), jnp.float32), 'w_qkv': w(ks[1], (H_SIZE, CONV_DIM), 0.02), 'w_z': w(ks[2], (H_SIZE, VALUE_DIM), 0.02), 'w_b': w(ks[3], (H_SIZE, NUM_V_HEADS), 0.02), 'w_a': w(ks[4], (H_SIZE, NUM_V_HEADS), 0.02), 'conv_w': w(ks[5], (CONV_DIM, KERNEL), 0.2), 'dt_bias': jnp.ones((NUM_V_HEADS,), jnp.float32), 'A_log': jnp.zeros((NUM_V_HEADS,), jnp.float32), 'norm_gamma': jnp.ones((DV,), jnp.float32), 'w_out': w(ks[6], (VALUE_DIM, H_SIZE), 0.02)}
    _L0_attn_in = _L0_attn_setup()

    def _L0_ffn_setup():
        import jax, jax.numpy as jnp
        import numpy as np
        B, P = (32, 32)
        DIMS = [256, 512, 512, 256]
        key = jax.random.key(seed)
        ks = jax.random.split(key, 7)

        def lin(k, fan_out, fan_in):
            s = 1.0 / np.sqrt(fan_in)
            return jax.random.uniform(k, (fan_out, fan_in), jnp.float32, -s, s)
        return {'classifier_input': jax.random.normal(ks[0], (B, P, DIMS[0]), jnp.float32), 'W1': lin(ks[1], DIMS[1], DIMS[0]), 'b1': jax.random.uniform(ks[2], (DIMS[1],), jnp.float32, -0.02, 0.02), 'W2': lin(ks[3], DIMS[2], DIMS[1]), 'b2': jax.random.uniform(ks[4], (DIMS[2],), jnp.float32, -0.02, 0.02), 'W3': lin(ks[5], DIMS[3], DIMS[2]), 'b3': jax.random.uniform(ks[6], (DIMS[3],), jnp.float32, -0.02, 0.02)}
    _L0_ffn_in = _L0_ffn_setup()

    def _L1_attn_setup():
        import jax, jax.numpy as jnp
        import numpy as np
        IN_FEATURES = 256
        HEAD_NUM = 64
        D = IN_FEATURES // HEAD_NUM
        SCALE = float(np.sqrt(D))
        key = jax.random.key(seed)
        ks = jax.random.split(key, 9)
        F = IN_FEATURES
        x = jax.random.normal(ks[0], (4, 128, F), dtype=jnp.float32)
        w = lambda k: jax.random.normal(k, (F, F), dtype=jnp.float32) * 0.02
        b = lambda k: jax.random.normal(k, (F,), dtype=jnp.float32) * 0.01
        return {'x': x, 'Wq': w(ks[1]), 'bq': b(ks[2]), 'Wk': w(ks[3]), 'bk': b(ks[4]), 'Wv': w(ks[5]), 'bv': b(ks[6]), 'Wo': w(ks[7]), 'bo': b(ks[8])}
    _L1_attn_in = _L1_attn_setup()

    def _L1_ffn_setup():
        import jax, jax.numpy as jnp
        import numpy as np
        B, S, H = (2, 256, 256)
        E, K, F = (32, 4, 176)
        FS = 704
        EPS = 1e-06
        CAP = 128
        key = jax.random.key(seed)
        ks = jax.random.split(key, 10)
        s = 0.02
        return {'hidden_states': jax.random.normal(ks[0], (B, S, H), jnp.float32), 'w_norm': 1.0 + 0.02 * jax.random.normal(ks[1], (H,), jnp.float32), 'w_router': s * jax.random.normal(ks[2], (H, E), jnp.float32), 'w_gate': s * jax.random.normal(ks[3], (E, H, F), jnp.float32), 'w_up': s * jax.random.normal(ks[4], (E, H, F), jnp.float32), 'w_down': s * jax.random.normal(ks[5], (E, F, H), jnp.float32), 'sw_gate': s * jax.random.normal(ks[6], (H, FS), jnp.float32), 'sw_up': s * jax.random.normal(ks[7], (H, FS), jnp.float32), 'sw_down': s * jax.random.normal(ks[8], (FS, H), jnp.float32), 'w_shared_gate': s * jax.random.normal(ks[9], (H, 1), jnp.float32)}
    _L1_ffn_in = _L1_ffn_setup()
    _d = {'L0_attn_hidden_states': _L0_attn_in['hidden_states'], 'L0_attn_w_qkv': _L0_attn_in['w_qkv'], 'L0_attn_w_z': _L0_attn_in['w_z'], 'L0_attn_w_b': _L0_attn_in['w_b'], 'L0_attn_w_a': _L0_attn_in['w_a'], 'L0_attn_conv_w': _L0_attn_in['conv_w'], 'L0_attn_dt_bias': _L0_attn_in['dt_bias'], 'L0_attn_A_log': _L0_attn_in['A_log'], 'L0_attn_norm_gamma': _L0_attn_in['norm_gamma'], 'L0_attn_w_out': _L0_attn_in['w_out'], 'L0_ffn_W1': _L0_ffn_in['W1'], 'L0_ffn_b1': _L0_ffn_in['b1'], 'L0_ffn_W2': _L0_ffn_in['W2'], 'L0_ffn_b2': _L0_ffn_in['b2'], 'L0_ffn_W3': _L0_ffn_in['W3'], 'L0_ffn_b3': _L0_ffn_in['b3'], 'L1_attn_Wq': _L1_attn_in['Wq'], 'L1_attn_bq': _L1_attn_in['bq'], 'L1_attn_Wk': _L1_attn_in['Wk'], 'L1_attn_bk': _L1_attn_in['bk'], 'L1_attn_Wv': _L1_attn_in['Wv'], 'L1_attn_bv': _L1_attn_in['bv'], 'L1_attn_Wo': _L1_attn_in['Wo'], 'L1_attn_bo': _L1_attn_in['bo'], 'L1_ffn_w_norm': _L1_ffn_in['w_norm'], 'L1_ffn_w_router': _L1_ffn_in['w_router'], 'L1_ffn_w_gate': _L1_ffn_in['w_gate'], 'L1_ffn_w_up': _L1_ffn_in['w_up'], 'L1_ffn_w_down': _L1_ffn_in['w_down'], 'L1_ffn_sw_gate': _L1_ffn_in['sw_gate'], 'L1_ffn_sw_up': _L1_ffn_in['sw_up'], 'L1_ffn_sw_down': _L1_ffn_in['sw_down'], 'L1_ffn_w_shared_gate': _L1_ffn_in['w_shared_gate']}
    _x0 = _d['L0_attn_hidden_states']
    _d['L0_attn_hidden_states'] = jax.random.normal(jax.random.fold_in(jax.random.key(seed), 1), (1, 1024, 256), dtype=_x0.dtype)
    del _x0
    return _d

def reference(L0_attn_hidden_states, L0_attn_w_qkv, L0_attn_w_z, L0_attn_w_b, L0_attn_w_a, L0_attn_conv_w, L0_attn_dt_bias, L0_attn_A_log, L0_attn_norm_gamma, L0_attn_w_out, L0_ffn_W1, L0_ffn_b1, L0_ffn_W2, L0_ffn_b2, L0_ffn_W3, L0_ffn_b3, L1_attn_Wq, L1_attn_bq, L1_attn_Wk, L1_attn_bk, L1_attn_Wv, L1_attn_bv, L1_attn_Wo, L1_attn_bo, L1_ffn_w_norm, L1_ffn_w_router, L1_ffn_w_gate, L1_ffn_w_up, L1_ffn_w_down, L1_ffn_sw_gate, L1_ffn_sw_up, L1_ffn_sw_down, L1_ffn_w_shared_gate):

    def _L0_attn_ref(hidden_states, w_qkv, w_z, w_b, w_a, conv_w, dt_bias, A_log, norm_gamma, w_out):
        import jax, jax.numpy as jnp
        import numpy as np
        H_SIZE = 256
        NUM_K_HEADS = 16
        NUM_V_HEADS = 32
        DK = 128
        DV = 128
        KEY_DIM = NUM_K_HEADS * DK
        VALUE_DIM = NUM_V_HEADS * DV
        CONV_DIM = 2 * KEY_DIM + VALUE_DIM
        KERNEL = 4
        EPS = 1e-06
        B, S = (2, 256)

        def _l2norm(x, eps=1e-06):
            return x * jax.lax.rsqrt(jnp.sum(x * x, axis=-1, keepdims=True) + eps)

        def _causal_conv(x, w):
            K = w.shape[-1]
            Sq = x.shape[1]
            xp = jnp.pad(x, ((0, 0), (K - 1, 0), (0, 0)))
            out = xp[:, 0:Sq, :] * w[None, None, :, 0]
            for j in range(1, K):
                out = out + xp[:, j:j + Sq, :] * w[None, None, :, j]
            return out

        def _forward(hidden_states, w_qkv, w_z, w_b, w_a, conv_w, dt_bias, A_log, norm_gamma, w_out):
            Bq, Sq, _ = hidden_states.shape
            mixed = hidden_states @ w_qkv
            z = (hidden_states @ w_z).reshape(Bq, Sq, NUM_V_HEADS, DV)
            b = hidden_states @ w_b
            a = hidden_states @ w_a
            mixed = jax.nn.silu(_causal_conv(mixed, conv_w))
            q, k, v = jnp.split(mixed, [KEY_DIM, 2 * KEY_DIM], axis=-1)
            q = q.reshape(Bq, Sq, NUM_K_HEADS, DK)
            k = k.reshape(Bq, Sq, NUM_K_HEADS, DK)
            v = v.reshape(Bq, Sq, NUM_V_HEADS, DV)
            nrep = NUM_V_HEADS // NUM_K_HEADS
            q = jnp.repeat(q, nrep, axis=2)
            k = jnp.repeat(k, nrep, axis=2)
            beta = jax.nn.sigmoid(b)
            g = -jnp.exp(A_log)[None, None, :] * jax.nn.softplus(a + dt_bias[None, None, :])
            qf = _l2norm(q.astype(jnp.float32)) * DK ** (-0.5)
            kf = _l2norm(k.astype(jnp.float32))
            vf = v.astype(jnp.float32)
            gf = g.astype(jnp.float32)
            bf = beta.astype(jnp.float32)

            def step(state, xs):
                q_t, k_t, v_t, g_t, b_t = xs
                state = state * jnp.exp(g_t)[..., None, None]
                kv = jnp.einsum('bhk,bhkv->bhv', k_t, state)
                delta = (v_t - kv) * b_t[..., None]
                state = state + jnp.einsum('bhk,bhv->bhkv', k_t, delta)
                out = jnp.einsum('bhk,bhkv->bhv', q_t, state)
                return (state, out)
            mv = lambda x: jnp.moveaxis(x, 1, 0)
            xs = (mv(qf), mv(kf), mv(vf), mv(gf), mv(bf))
            state0 = jnp.zeros((Bq, NUM_V_HEADS, DK, DV), jnp.float32)
            _, outs = jax.lax.scan(step, state0, xs)
            o = jnp.moveaxis(outs, 0, 1)
            o = o * jax.nn.silu(z.astype(jnp.float32))
            o = o * jax.lax.rsqrt(jnp.mean(o * o, axis=-1, keepdims=True) + EPS)
            o = o * norm_gamma
            o = o.reshape(Bq, Sq, VALUE_DIM).astype(hidden_states.dtype)
            return o @ w_out
        return _forward(hidden_states, w_qkv, w_z, w_b, w_a, conv_w, dt_bias, A_log, norm_gamma, w_out)

    def _L0_ffn_ref(classifier_input, W1, b1, W2, b2, W3, b3):
        import jax, jax.numpy as jnp
        import numpy as np
        B, P = (32, 32)
        DIMS = [256, 512, 512, 256]
        x = classifier_input
        x = jax.nn.relu(jnp.einsum('bpd,hd->bph', x, W1) + b1)
        x = jax.nn.relu(jnp.einsum('bpd,hd->bph', x, W2) + b2)
        out = jnp.einsum('bpd,od->bpo', x, W3) + b3
        return out

    def _L1_attn_ref(x, Wq, bq, Wk, bk, Wv, bv, Wo, bo):
        import jax, jax.numpy as jnp
        import numpy as np
        IN_FEATURES = 256
        HEAD_NUM = 64
        D = IN_FEATURES // HEAD_NUM
        SCALE = float(np.sqrt(D))
        B, S, F = x.shape
        d = D
        h = F // d
        q = x @ Wq + bq
        k = x @ Wk + bk
        v = x @ Wv + bv

        def to_heads(t):
            return t.reshape(B, S, d, h).transpose(0, 2, 1, 3)
        q, k, v = (to_heads(q), to_heads(k), to_heads(v))
        scores = jnp.einsum('bdsh,bdth->bdst', q, k) / SCALE
        weights = jax.nn.softmax(scores, axis=-1)
        feats = jnp.einsum('bdst,bdth->bdsh', weights, v)
        feats = feats.transpose(0, 2, 1, 3).reshape(B, S, F)
        return feats @ Wo + bo

    def _L1_ffn_ref(hidden_states, w_norm, w_router, w_gate, w_up, w_down, sw_gate, sw_up, sw_down, w_shared_gate):
        import jax, jax.numpy as jnp
        import numpy as np
        B, S, H = (2, 256, 256)
        E, K, F = (32, 4, 176)
        FS = 704
        EPS = 1e-06
        CAP = 128
        inp = hidden_states
        xf = inp.astype(jnp.float32)
        var = jnp.mean(xf * xf, axis=-1, keepdims=True)
        x = (w_norm * (xf * jax.lax.rsqrt(var + EPS))).astype(inp.dtype)
        Bq, Sq, Hq = x.shape
        x = x.reshape(-1, Hq)
        T = Bq * Sq
        logits = x @ w_router
        probs = jax.nn.softmax(logits.astype(jnp.float32), axis=-1)
        w_topk, sel = jax.lax.top_k(probs, K)
        w_topk = w_topk.astype(x.dtype)
        flat_e = sel.reshape(-1)
        order = jnp.argsort(flat_e)
        sorted_e = flat_e[order]
        counts = jnp.zeros((E,), jnp.int32).at[flat_e].add(1)
        starts = jnp.cumsum(counts) - counts
        pos = jnp.arange(T * K) - starts[sorted_e]
        tok = order // K
        valid = pos < CAP
        dest = jnp.where(valid, pos, CAP)
        buf = jnp.zeros((E, CAP + 1, Hq), x.dtype).at[sorted_e, dest].set(x[tok])
        buf = buf[:, :CAP]
        g = jnp.einsum('ech,ehf->ecf', buf, w_gate)
        u = jnp.einsum('ech,ehf->ecf', buf, w_up)
        y = jnp.einsum('ecf,efh->ech', jax.nn.silu(g) * u, w_down)
        wv = w_topk.reshape(-1)[order] * valid.astype(x.dtype)
        gath = y[sorted_e, jnp.minimum(pos, CAP - 1)]
        out = jnp.zeros((T, Hq), x.dtype).at[tok].add(gath * wv[:, None])
        sh = jax.nn.silu(x @ sw_gate) * (x @ sw_up) @ sw_down
        sh = jax.nn.sigmoid(x @ w_shared_gate) * sh
        out = out + sh
        return inp + out.reshape(Bq, Sq, Hq)
    x = L0_attn_hidden_states
    x = x + _L0_attn_ref(_layernorm(x, axis=-1), L0_attn_w_qkv, L0_attn_w_z, L0_attn_w_b, L0_attn_w_a, L0_attn_conv_w, L0_attn_dt_bias, L0_attn_A_log, L0_attn_norm_gamma, L0_attn_w_out)
    x = x + _L0_ffn_ref(_layernorm(x, axis=-1), L0_ffn_W1, L0_ffn_b1, L0_ffn_W2, L0_ffn_b2, L0_ffn_W3, L0_ffn_b3)
    x = x + _L1_attn_ref(_layernorm(x, axis=-1), L1_attn_Wq, L1_attn_bq, L1_attn_Wk, L1_attn_bk, L1_attn_Wv, L1_attn_bv, L1_attn_Wo, L1_attn_bo)
    x = x + _L1_ffn_ref(_layernorm(x, axis=-1), L1_ffn_w_norm, L1_ffn_w_router, L1_ffn_w_gate, L1_ffn_w_up, L1_ffn_w_down, L1_ffn_sw_gate, L1_ffn_sw_up, L1_ffn_sw_down, L1_ffn_w_shared_gate)
    return x

_drawn_inputs = setup_inputs


def setup_inputs(seed=0):
    import zlib

    import numpy as np

    out = dict(_drawn_inputs(seed))
    spreads = {'L0_attn_dt_bias': (1.0, 0.6),
     'L0_attn_A_log': (0.0, 0.8),
     'L0_attn_norm_gamma': (1.0, 0.6)}
    factors = {'L0_attn_w_b': 6.219,
     'L0_attn_w_a': 8.0,
     'L0_ffn_b1': 8.0,
     'L0_ffn_b2': 8.0,
     'L0_ffn_b3': 4.746,
     'L1_attn_Wq': 8.0,
     'L1_attn_bq': 8.0,
     'L1_attn_Wk': 8.0,
     'L1_attn_bk': 8.0,
     'L1_attn_Wv': 6.36,
     'L1_attn_bv': 8.0,
     'L1_attn_Wo': 5.948,
     'L1_attn_bo': 5.937,
     'L1_ffn_w_norm': 8.0,
     'L1_ffn_w_router': 8.0,
     'L1_ffn_w_gate': 8.0,
     'L1_ffn_w_up': 8.0,
     'L1_ffn_w_down': 8.0,
     'L1_ffn_sw_gate': 8.0,
     'L1_ffn_sw_up': 8.0,
     'L1_ffn_sw_down': 8.0,
     'L1_ffn_w_shared_gate': 8.0}
    for name, (base, spread) in spreads.items():
        noise = np.random.default_rng([zlib.crc32(name.encode()), seed]).standard_normal(out[name].shape)
        drawn = base * np.exp(spread * noise) if base else spread * noise
        out[name] = jnp.asarray(drawn.astype(out[name].dtype))
    for name, factor in factors.items():
        out[name] = (out[name] * factor).astype(out[name].dtype)
    return out
```

```python
from contextlib import ExitStack

import concourse.bass as bass
from concourse import mybir

ALU = mybir.AluOpType
ACT = mybir.ActivationFunctionType
AX_X = mybir.AxisListType.X
F32 = mybir.dt.float32
U32 = mybir.dt.uint32

P = 128
T = 1024
D = 256
KD = D // P
NT = T // P
EPS_LN = 1e-5
EPS = 1e-6


class Alloc:

    psum_banks = None

    def __init__(self, nc, stack, stage, outer=None):
        self.nc, self.stack, self.stage, self.outer = nc, stack, stage, outer
        self.next_bank = 0
        self.sems = []

    def sb(self, name, shape, dtype=F32):
        return self.stack.enter_context(self.nc.sbuf_tensor(f"{self.stage}_{name}", shape, dtype))

    def psum(self, shape):
        first = self.next_bank
        self.next_bank += -(-int(shape[1] * (shape[2] if len(shape) > 2 else 1)) // 512)
        ap = self.psum_banks[:, first:self.next_bank].rearrange("p a b -> p (a b)")
        return ap.rearrange("p (a b) -> p a b", b=shape[2]) if len(shape) > 2 else ap

    def sem(self, name, stage=None):
        stage = stage or self.stage
        if self.outer:
            return self.outer.sem(name, stage)
        self.sems.append(self.stack.enter_context(self.nc.semaphore(f"{stage}_{name}")))
        return self.sems[-1]

    def clear_sems(self):
        with self.nc.Block() as block:
            @block.gpsimd
            def _(pool):
                for s in self.sems:
                    pool.sem_clear(s)


def bc_mid(ap, n):
    p, m = ap.shape
    return ap.unsqueeze(1).to_broadcast([p, n, m])


def bc_last(ap, n):
    p, m = ap.shape
    return ap.unsqueeze(2).to_broadcast([p, m, n])


def layernorm_transposed(nc, a, x, hT, ident, eps, prefetch=None, rms_weight=None, weight_ready=None, xn=None):
    rms = rms_weight is not None
    stats = a.sb("ln_stats", [P, NT, 6])
    mv = a.sb("ln_mv", [P, NT, 2])
    spread = a.sb("ln_spread", [P, NT])
    root = a.sb("ln_root", [P, NT])
    rstd = a.sb("ln_rstd", [P, NT])
    ln = a.sb("ln_out", [P, NT, D])
    rstd2 = a.sb("ln_rstd2", [P, NT]) if rms else None
    xn = xn if rms else ln
    flip = [a.psum([P, 4, P]) for i in range(4)]
    s_stats, s_mv, s_spread = a.sem("ln_stats_ready"), a.sem("ln_mv_ready"), a.sem("ln_spread_ready")
    s_root, s_rstd = a.sem("ln_root_ready"), a.sem("ln_rstd_ready")
    s_ln, s_x = a.sem("ln_ready"), a.sem("x_plus_ln")
    s_xn, s_flip, s_ht = a.sem("ln_xn_ready"), a.sem("ln_flipped"), a.sem("ln_ht_written")
    with nc.Block() as block:
        @block.sync
        def _(sp):
            if prefetch:
                prefetch(sp)

        @block.vector
        def _(dve):
            for t in range(NT):
                dve.bn_stats(stats[:, t], x[:, t]).then_inc(s_stats, 1)
            for t in range(NT):
                dve.wait_ge(s_stats, t + 1)
                dve.bn_aggr(mv[:, t], stats[:, t]).then_inc(s_mv, 1)
            dve.wait_ge(s_mv, NT)
            dve.tensor_scalar(spread[:], mv[:, :, 1], eps, None, ALU.add).then_inc(s_spread, 1)
            dve.wait_ge(s_root, 1)
            dve.reciprocal(rstd[:], root[:]).then_inc(s_rstd, 1)
            dve.wait_ge(s_rstd, 1)
            for t in range(NT):
                dve.tensor_scalar(ln[:, t], x[:, t], mv[:, t, 0:1], rstd[:, t:t + 1], ALU.subtract, ALU.mult).then_inc(s_ln, 1)
            if rms:
                dve.tensor_tensor(rstd2[:], rstd[:], rstd[:], ALU.mult).then_inc(s_rstd, 1)
                dve.wait_ge(s_rstd, 2)
                dve.tensor_tensor(rstd2[:], rstd2[:], mv[:, :, 1], ALU.mult).then_inc(s_rstd, 1)
                dve.wait_ge(s_rstd, 3)
                dve.tensor_scalar(spread[:], rstd2[:], EPS, None, ALU.add).then_inc(s_spread, 1)
                dve.wait_ge(s_ln, NT)
                dve.tensor_tensor(x[:], x[:], ln[:], ALU.add).then_inc(s_x, 1)
                dve.wait_ge(s_root, 2)
                dve.reciprocal(rstd2[:], root[:]).then_inc(s_rstd, 1)
                dve.wait_ge(s_rstd, 4)
                dve.wait_ge(weight_ready, 16)
                for t in range(NT):
                    dve.scalar_tensor_tensor(xn[:, t], ln[:, t], rstd2[:, t:t + 1], rms_weight[:], ALU.mult, ALU.mult).then_inc(s_xn, 1)
            for u in range(4):
                dve.wait_ge(s_flip, u + 1)
                kd, half = u // 2, u % 2
                out = hT[:, kd, half * 512:(half + 1) * 512]
                src = flip[u][:].rearrange("p a b -> p (a b)")
                dve.tensor_copy(out, src).then_inc(s_ht, 1)
            dve.wait_ge(s_ht, 4)
            if rms:
                dve.wait_ge(s_x, 1)

        @block.scalar
        def _(act):
            act.wait_ge(s_spread, 1)
            act.activation(root[:], spread[:], ACT.Sqrt).then_inc(s_root, 1)
            if rms:
                act.wait_ge(s_spread, 2)
                act.activation(root[:], spread[:], ACT.Sqrt).then_inc(s_root, 1)

        @block.tensor
        def _(pe):
            for u in range(4):
                kd, half = u // 2, u % 2
                for j in range(4):
                    t = half * 4 + j
                    pe.wait_ge(s_xn if rms else s_ln, t + 1)
                    ins = pe.transpose(flip[u][:, j], xn[:, t, kd * P:(kd + 1) * P], ident[:])
                ins.then_inc(s_flip, 1)


HK = 16
HD = 2
C = NT
IT = C * HD
LEVELS = 7
G_, NGAM, GAM, TAIL, GAMC, BETA = range(6)
NQ = 6


class Uses:

    def __init__(self, sem, first, mid, last, before=0):
        self.sem, self.lists, self.before = sem, {"first": first, "mid": mid, "last": last}, before

    def base(self, kind, h):
        if kind == "first":
            return self.before
        if kind == "last":
            return self.before + len(self.lists["first"]) + (HK - 1) * len(self.lists["mid"])
        return self.before + len(self.lists["first"]) + (h - 1) * len(self.lists["mid"])

    def done(self, kind, h, name):
        return self.base(kind, h) + self.lists[kind].index(name) + 1

    def ahead(self, kind, h, name):
        i = self.lists[kind].index(name)
        if kind == "first" and i + self.before == 0:
            return None
        return self.base(kind, h) + i


def step_plan():
    slots = ["decay", "level1"]
    for lv in range(2, LEVELS + 1):
        slots += [f"below{lv}", f"merge{lv}"]
    return slots + ["attn"]


SLOTS = step_plan()
SCAN_AT = {k + 1: k for k in range(12)}
PROJ_AT = [{0: 0, 4: 1, 8: 2, 12: 3}, {2: 4, 8: 5}]
PROJ_TAIL = [6, 7]


def gated_delta(nc, x, hT, consts, d):
    with ExitStack() as stack:
        a = Alloc(nc, stack, "gdn")
        with ExitStack() as inner:
            layernorm_transposed(nc, Alloc(nc, inner, "norm1", a), x, hT, consts["ident"], EPS_LN)
        coef = a.sb("coef", [P, NQ, HK, IT])
        conv_w = a.sb("conv_w", [P, HK, 4, 4])
        gamma = a.sb("gamma", [P, 1])
        powers = a.sb("powers", [P, 2 * C])
        minus_half = a.sb("minus_half", [P, IT])
        S = a.sb("S", [P, HD, P])
        raw = [a.sb(f"raw{i}", [P, 3 + T]) for i in range(2)]

        gate_coefficients(nc, a, hT, consts, d, coef, conv_w, gamma, powers, minus_half, raw)
        with ExitStack() as inner:
            heads(nc, Alloc(nc, inner, "heads", a), x, hT, consts, d, coef, conv_w, gamma, powers, minus_half, S, raw)
        a.clear_sems()


def gate_coefficients(nc, outer, hT, consts, d, coef, conv_w, gamma, powers, minus_half, raw):
    with ExitStack() as stack:
        a = Alloc(nc, stack, "gate", outer)
        w_ba = a.sb("w_ba", [P, KD, 64])
        dt_b = a.sb("dt_b", [P, 32])
        a_log = a.sb("a_log", [P, 32])
        ones = a.sb("ones", [P, P])
        neg_rate = a.sb("neg_rate", [P, 32])
        ba = a.sb("ba", [P, C, 64])
        e_b = a.sb("e_b", [P, C, 32])
        y = a.sb("y", [P, C, 32])
        ay = a.sb("ay", [P, C, 32])
        l1 = a.sb("l1", [P, C, 32])
        sp = a.sb("sp", [P, C, 32])
        g = a.sb("g", [P, C, 32])
        tot = a.sb("tot", [P, HK * IT])
        diff = a.sb("diff", [P, HK * IT])
        acc = a.psum([P, C, 64])
        cum = a.psum([P, 512])
        total = a.psum([P, 512])
        s_in = [a.sem(f"in{i}") for i in range(5)]
        s_mm, s_v, s_a, s_cum = a.sem("mm"), a.sem("vector_step"), a.sem("scalar_step"), a.sem("cum")

        def by_head(ap):
            return ap.rearrange("p c (h e) -> p h c e", e=HD)

        def q(k):
            return coef[:, k].rearrange("p h i -> p (h i)")

        def q4(k):
            return coef[:, k].rearrange("p h (c e) -> p h c e", e=HD)

        with nc.Block() as block:
            @block.sync
            def _(sp_):
                sp_.dma_start(w_ba[:], d["w_ba"]).then_inc(s_in[0], 16)
                sp_.dma_start(dt_b[:], d["dt_bias"].to_broadcast([P, 32])).then_inc(s_in[1], 16)
                sp_.dma_start(a_log[:], d["A_log"].to_broadcast([P, 32])).then_inc(s_in[2], 16)
                sp_.dma_start(conv_w[:], d["conv_w"]).then_inc(s_in[3], 16)
                sp_.dma_start(gamma[:], d["gamma"]).then_inc(s_in[4], 16)
                sp_.wait_ge(s_in[3], 16)
                sp_.wait_ge(s_in[4], 16)

            @block.gpsimd
            def _(pool):
                pool.memset(powers[:, 0:C], 0.5)
                pool.memset(powers[:, C:2 * C], -0.5)
                pool.memset(minus_half[:], -0.5)
                for r in raw:
                    pool.memset(r[:, 0:3], 0.0)

            @block.tensor
            def _(pe):
                pe.wait_ge(s_in[0], 16)
                for c in range(C):
                    for kd in range(KD):
                        ins = pe.matmul(acc[:, c], hT[:, kd, c * P:(c + 1) * P], w_ba[:, kd],
                                        start=kd == 0, stop=kd == KD - 1)
                ins.then_inc(s_mm, 1)
                pe.wait_ge(s_v, 10)
                pe.matmul(cum[:, 0:HK * IT], consts["upto"][:], q(G_), start=True, stop=True).then_inc(s_cum, 1)
                pe.matmul(total[:, 0:HK * IT], ones[:], q(G_), start=True, stop=True).then_inc(s_cum, 1)

            @block.scalar
            def _(act):
                act.wait_ge(s_in[2], 16)
                act.activation(neg_rate[:], a_log[:], ACT.Exp).then_inc(s_a, 1)
                act.wait_ge(s_v, 2)
                act.activation(e_b[:], ba[:, :, 0:32], ACT.Exp, scale=-1.0).then_inc(s_a, 1)
                act.wait_ge(s_v, 4)
                act.activation(l1[:], ay[:], ACT.Exp, scale=-1.0).then_inc(s_a, 1)
                act.wait_ge(s_v, 7)
                act.activation(ay[:], l1[:], ACT.Ln).then_inc(s_a, 1)
                act.wait_ge(s_v, 11)
                act.wait_ge(s_cum, 2)
                act.activation(q(GAM), diff[:], ACT.Exp).then_inc(s_a, 1)
                act.activation(q(GAMC), tot[:], ACT.Exp).then_inc(s_a, 1)
                act.wait_ge(s_v, 13)
                act.activation(q(TAIL), tot[:], ACT.Exp).then_inc(s_a, 1)

            @block.vector
            def _(dve):
                dve.memset(ones[:], 1.0).then_inc(s_v, 1)
                dve.wait_ge(s_mm, 1)
                dve.tensor_copy(ba[:], acc[:]).then_inc(s_v, 1)
                dve.wait_ge(s_in[1], 16)
                dve.wait_ge(s_v, 2)
                dve.tensor_tensor(y[:], ba[:, :, 32:64], bc_mid(dt_b[:], C), ALU.add).then_inc(s_v, 1)
                dve.wait_ge(s_v, 3)
                dve.scalar_tensor_tensor(ay[:], y[:], -1.0, y[:], ALU.mult, ALU.max).then_inc(s_v, 1)
                dve.wait_ge(s_a, 2)
                dve.tensor_scalar(e_b[:], e_b[:], 1.0, None, ALU.add).then_inc(s_v, 1)
                dve.wait_ge(s_v, 5)
                dve.reciprocal(q4(BETA), by_head(e_b[:])).then_inc(s_v, 1)
                dve.wait_ge(s_a, 3)
                dve.tensor_scalar(l1[:], l1[:], 1.0, None, ALU.add).then_inc(s_v, 1)
                dve.wait_ge(s_a, 4)
                dve.scalar_tensor_tensor(sp[:], y[:], 0.0, ay[:], ALU.max, ALU.add).then_inc(s_v, 1)
                dve.wait_ge(s_v, 8)
                dve.scalar_tensor_tensor(g[:], sp[:], -1.0, bc_mid(neg_rate[:], C), ALU.mult, ALU.mult).then_inc(s_v, 1)
                dve.wait_ge(s_v, 9)
                dve.tensor_copy(q4(G_), by_head(g[:])).then_inc(s_v, 1)
                dve.wait_ge(s_cum, 2)
                dve.tensor_copy(tot[:], total[:, 0:HK * IT])
                dve.tensor_copy(diff[:], cum[:, 0:HK * IT]).then_inc(s_v, 1)
                dve.wait_ge(s_a, 6)
                dve.tensor_scalar(q(NGAM), q(GAM), -1.0, None, ALU.mult).then_inc(s_v, 1)
                dve.wait_ge(s_v, 11)
                dve.tensor_tensor(tot[:], tot[:], diff[:], ALU.subtract).then_inc(s_v, 1)
                dve.wait_ge(s_a, 7)


def heads(nc, a, x, hT, consts, d, coef, conv_w, gamma, powers, minus_half, S, raw):
    ident, upto, after, levels = consts["ident"], consts["upto"], consts["after"], consts["levels"]
    dm_mask, before_ = upto, consts["before"]

    w_in = a.sb("w_in", [P, KD, 4 * P])
    w_z = a.sb("w_z", [P, KD, HD * P])
    w_o = a.sb("w_o", [P, HD, D])
    y = [a.sb(f"y{j}", [P, T]) for j in range(4)]
    kT = [a.sb(f"kT{i}", [P, T]) for i in range(2)]
    qT = [a.sb(f"qT{i}", [P, T]) for i in range(2)]
    k_tok = [a.sb(f"k_tok{i}", [P, C, P]) for i in range(2)]
    v_s = [a.sb(f"v_s{i}", [P, IT, P]) for i in range(2)]
    cf = [a.sb(f"cf{i}", [P, NQ, IT]) for i in range(2)]
    cc = [a.sb(f"cc{i}", [P, IT]) for i in range(2)]
    norms = a.sb("norms", [P, 2 * C])
    inv = a.sb("inv", [P, C])
    roots = [a.sb(f"roots{i}", [P, 2 * C]) for i in range(2)]
    ones_col = a.sb("ones_col", [P, 1])
    z = a.sb("z", [P, C, HD * P])
    gU = [a.sb(f"gU{g}", [P, 4, P]) for g in range(2)]
    Dx = [a.sb(f"Dx{g}", [P, 4, P]) for g in range(2)]
    Ds = [a.sb(f"Ds{g}", [P, 4, P]) for g in range(2)]
    Dm = [a.sb(f"Dm{g}", [P, 4, P]) for g in range(2)]
    G = [a.sb(f"G{g}", [P, 4, P]) for g in range(2)]
    Gl = [[a.sb(f"Gl{g}_{i}", [P, 4, P]) for i in range(2)] for g in range(2)]
    Tn = [a.sb(f"Tn{g}", [P, 4, P]) for g in range(2)]
    Ut = [a.sb(f"Ut{g}", [P, 4, P]) for g in range(2)]
    W = [a.sb(f"W{g}", [P, 4, P]) for g in range(2)]
    Uf = a.sb("Uf", [P, IT, P])
    At = a.sb("At", [P, IT, P])
    X = a.sb("X", [P, HD, P])
    O1 = a.sb("O1", [P, HD, P])
    Dl = a.sb("Dl", [P, HD, P])
    Dt = a.sb("Dt", [P, HD, P])
    O2 = a.sb("O2", [P, HD, P])
    og = a.sb("og", [P, IT, P])
    junk = a.sb("junk", [P, P])
    ms = a.sb("ms", [P, IT])
    rq2 = a.sb("rq2", [P, C])
    var = a.sb("var", [P, IT])
    rs = a.sb("rs", [P, IT])
    fac = a.sb("fac", [P, IT])
    ogT = a.sb("ogT", [P, IT, P])

    bank = [a.psum([P, 4, P]) for i in range(4)]
    bank_a = a.psum([P, 4, P])
    bank_b = a.psum([P, 4, P])
    bank_c = a.psum([P, 4, P])
    bank_p = a.psum([P, 512])

    head_z = [["z0"], ["z1"], ["z2"], ["z3"]]
    head_kv = [["k0", "v1"], ["k1", "v2"], ["norm", "v3"], ["v0"]]
    even, odd = [], []
    for sg in range(2):
        even += [f"decay_{sg}", f"level1_{sg}"]
        odd += [f"kk_{sg}"]
        for lv in range(2, LEVELS + 1):
            even += [f"below{lv}_{sg}"] + ([f"T{lv}_{sg}"] if lv < LEVELS else [])
            odd += [f"U{lv}_{sg}"]
        even += [f"attn_{sg}"]
    inverse = [even, odd, even, odd]
    tail = [["flip0", "out0"], ["flip1", "out1"], ["flip2", "out2"], ["flip3", "out3"]]
    first = [head_kv[b] + inverse[b] for b in range(4)]
    mid = [head_z[b] + head_kv[b] + inverse[b] + tail[b] for b in range(4)]
    last = [head_z[b] + tail[b] for b in range(4)]
    full = [Uses(a.sem(f"bank{b}_full"), first[b], mid[b], last[b]) for b in range(4)]
    free = [Uses(a.sem(f"bank{b}_free"), first[b], mid[b], last[b]) for b in range(4)]

    def per_scan(sem, *names):
        seq = [f"{n}{c}" for c in range(C) for n in names]
        return Uses(a.sem(sem), [], seq, seq)

    a_full, a_free = per_scan("scan_a_full", "ks", "su"), per_scan("scan_a_free", "ks", "su")
    b_full, b_free = per_scan("scan_b_full", "qs", "o"), per_scan("scan_b_free", "qs", "o")
    c_full, c_free = per_scan("scan_c_full", "tx"), per_scan("scan_c_free", "tx")
    dt_ready = per_scan("dt_ready", "dt")
    o_ready = per_scan("o_summed", "o")
    og_ready = per_scan("og_ready", "og")
    sq_ready = per_scan("squares_summed", "sq")
    s_zero = Uses(a.sem("state_zero"), ["zero"], ["zero"], [])
    proj = [f"p{u}" for u in range(8)]
    p_full = Uses(a.sem("proj_full"), proj, proj, [], before=8)
    p_free = Uses(a.sem("proj_free"), proj, proj, [], before=8)
    taps = [f"tap{j}_{t}" for j in range(4) for t in range(4)]
    conv_done = Uses(a.sem("conv_tap_done"), taps, taps, [], before=16)
    w_in_ready = Uses(a.sem("w_in_loaded"), ["w"], ["w"], [], before=1)
    w_z_ready = Uses(a.sem("w_z_loaded"), [], ["w"], ["w"])
    w_o_ready = Uses(a.sem("w_o_loaded"), [], ["w"], ["w"])
    acts = ["k", "q", "sk", "sq", "v0", "v1"]
    act_ready = Uses(a.sem("silu_ready"), acts, acts, [])
    one = ["it"]
    cf_ready = Uses(a.sem("coef_ready"), one, one, [])
    norms_ready = Uses(a.sem("norms_ready"), one, one, [])
    inv_ready = Uses(a.sem("inverse_norm_ready"), one, one, [])
    cc_ready = Uses(a.sem("cc_ready"), one, one, [])
    roots_ready = Uses(a.sem("roots_ready"), one, one, [])
    per_group = [f"{sg}_{g}" for sg in range(2) for g in range(2)]
    gu_ready = Uses(a.sem("g_columns_ready"), per_group, per_group, [])
    ds_ready = Uses(a.sem("strict_decay_ready"), per_group, per_group, [])
    dm_ready = Uses(a.sem("decay_ready"), per_group, per_group, [])
    u1_ready = Uses(a.sem("U1_ready"), per_group, per_group, [])
    lv_names = [f"{lv}_{sg}_{g}" for sg in range(2) for lv in range(1, LEVELS + 1) for g in range(2)]
    gl_ready = Uses(a.sem("level_masked"), lv_names, lv_names, [])
    small = ["rq2", "var0", "var", "fac", "ogn"]
    tail_dve = Uses(a.sem("tail_vector"), [], small, small)
    tail_pow = Uses(a.sem("tail_pow"), [], one, one)
    s_const = a.sem("ones_ready")

    def flat(ap):
        return ap.rearrange("p a b -> p (a b)")

    def run_steps(eng, step):
        step("first", 0, 0)
        step("mid", 1, 1)
        with eng.Fori(1, HK // 2 - 1) as t:
            step("mid", 2 * t, 0)
            step("mid", 2 * t + 1, 1)
        step("mid", HK - 2, 0)
        step("mid", HK - 1, 1)
        step("last", HK, 0)

    def wait(eng, use, value, times=1):
        if value is None or (isinstance(value, int) and value <= 0):
            return
        eng.wait_ge(use.sem, value * times)

    with nc.Block() as block:
        @block.sync
        def _(sp):
            sp.dma_start(w_in[:], d["w_in"][0]).then_inc(w_in_ready.sem, 16)
            sp.wait_ge(p_full.sem, 8)
            sp.dma_start(w_in[:], d["w_in"][1]).then_inc(w_in_ready.sem, 16)
            sp.dma_start(w_z[:], d["w_z"][0]).then_inc(w_z_ready.sem, 16)
            sp.dma_start(w_o[:], d["w_o"][0]).then_inc(w_o_ready.sem, 16)

            def step(kind, h, par):
                if kind == "mid":
                    sp.wait_ge(full[3].sem, full[3].done(kind, h, "z3"))
                    sp.dma_start(w_z[:], d["w_z"][bass.ds(h, 1)].rearrange("a p k n -> (a p) k n")).then_inc(w_z_ready.sem, 16)
                if kind in ("first", "mid") and not (isinstance(h, int) and h >= HK - 2):
                    sp.wait_ge(p_full.sem, p_full.done(kind, h, "p7"))
                    sp.dma_start(w_in[:], d["w_in"][bass.ds(h + 2, 1)].rearrange("a p k n -> (a p) k n")).then_inc(w_in_ready.sem, 16)
                if kind == "mid":
                    sp.wait_ge(full[3].sem, full[3].done(kind, h, "out3"))
                    sp.dma_start(w_o[:], d["w_o"][bass.ds(h, 1)].rearrange("a p k n -> (a p) k n")).then_inc(w_o_ready.sem, 16)

            step("first", 0, 0)
            with sp.Fori(0, (HK - 4) // 2) as t:
                step("mid", 2 * t + 1, 1)
                step("mid", 2 * t + 2, 0)
            step("mid", HK - 3, 1)
            step("mid", HK - 2, 0)
            step("mid", HK - 1, 1)

        @block.tensor
        def _(pe):
            def project(kind, h, u, src_ready, frees):
                j, half = u // 2, u % 2
                if u == 0:
                    pe.wait_ge(w_in_ready.sem, src_ready * 16)
                if frees is not None:
                    pe.wait_ge(p_free.sem, frees)
                for kd in range(KD):
                    ins = pe.matmul(bank_p[:], w_in[:, kd, j * P:(j + 1) * P],
                                    hT[:, kd, half * 512:(half + 1) * 512], start=kd == 0, stop=kd == KD - 1)
                ins.then_inc(p_full.sem, 1)

            def take(b, kind, h, name):
                wait(pe, free[b], free[b].ahead(kind, h, name))

            def step(kind, h, par):
                scan = kind != "first"
                inv_ = kind != "last"
                no_proj = kind == "last" or (isinstance(h, int) and h == HK - 1)
                sp_ = 1 - par

                def scan_quantum(i):
                    c, part = i // 3, i % 3
                    cs = slice(c * P, (c + 1) * P)
                    if part == 0:
                        wait(pe, a_free, a_free.ahead(kind, h, f"ks{c}"))
                        wait(pe, b_free, b_free.ahead(kind, h, f"qs{c}"))
                        if c == 0:
                            pe.wait_ge(s_zero.sem, h)
                        pe.matmul(flat(bank_a[:, 0:2]), kT[sp_][:, cs], flat(S[:]), start=True, stop=True).then_inc(a_full.sem, 1)
                        pe.matmul(flat(bank_b[:, 0:2]), qT[sp_][:, cs], flat(S[:]), start=True, stop=True).then_inc(b_full.sem, 1)
                    elif part == 1:
                        pe.wait_ge(a_free.sem, a_free.done(kind, h, f"ks{c}"))
                        wait(pe, c_free, c_free.ahead(kind, h, f"tx{c}"))
                        for e in range(HD):
                            ins = pe.matmul(bank_c[:, e], Uf[:, c * HD + e], X[:, e], start=True, stop=True)
                        ins.then_inc(c_full.sem, 1)
                    else:
                        pe.wait_ge(c_free.sem, c_free.done(kind, h, f"tx{c}"))
                        pe.wait_ge(b_free.sem, b_free.done(kind, h, f"qs{c}"))
                        for e in range(HD):
                            ins = pe.matmul(bank_b[:, e], At[:, c * HD + e], Dl[:, e], start=True, stop=True)
                        ins.then_inc(b_full.sem, 1)
                        pe.wait_ge(dt_ready.sem, dt_ready.done(kind, h, f"dt{c}"))
                        pe.matmul(flat(bank_a[:, 0:2]), k_tok[sp_][:, c], flat(Dt[:]), start=True, stop=True).then_inc(a_full.sem, 1)

                if scan:
                    pe.wait_ge(w_z_ready.sem, w_z_ready.done(kind, h, "w") * 16)
                    for u in range(4):
                        take(u, kind, h, f"z{u}")
                        for j in range(2):
                            c = 2 * u + j
                            for kd in range(KD):
                                ins = pe.matmul(flat(bank[u][:, 2 * j:2 * j + 2]), hT[:, kd, c * P:(c + 1) * P], w_z[:, kd],
                                                start=kd == 0, stop=kd == KD - 1)
                        ins.then_inc(full[u].sem, 1)
                if inv_:
                    pe.wait_ge(act_ready.sem, act_ready.done(kind, h, "k"))
                    for u in range(2):
                        take(u, kind, h, f"k{u}")
                        for j in range(4):
                            ins = pe.transpose(bank[u][:, j], kT[par][:, (4 * u + j) * P:(4 * u + j + 1) * P], ident[:])
                        ins.then_inc(full[u].sem, 1)
                    pe.wait_ge(act_ready.sem, act_ready.done(kind, h, "sq"))
                    take(2, kind, h, "norm")
                    for w in range(2):
                        for c in range(C):
                            ins = pe.matmul(bank[2][:, 0, w * C + c:w * C + c + 1], y[w][:, c * P:(c + 1) * P], ones_col[:],
                                            start=True, stop=True)
                    ins.then_inc(full[2].sem, 1)
                    pe.wait_ge(act_ready.sem, act_ready.done(kind, h, "v1"))
                    for u in range(4):
                        b = (3 + u) % 4
                        take(b, kind, h, f"v{u}")
                        for j in range(4):
                            c, e = 2 * u + j // 2, j % 2
                            ins = pe.transpose(bank[b][:, j], y[2 + e][:, c * P:(c + 1) * P], ident[:])
                        ins.then_inc(full[b].sem, 1)
                    for sg in range(2):
                        for k, slot in enumerate(SLOTS):
                            for g in range(2):
                                b0, b1, gi = 2 * g, 2 * g + 1, f"{sg}_{g}"
                                if slot == "decay":
                                    pe.wait_ge(gu_ready.sem, gu_ready.done(kind, h, gi))
                                    take(b0, kind, h, f"decay_{sg}")
                                    pe.matmul(flat(bank[b0][:]), after[:], flat(gU[g][:]), start=True, stop=True).then_inc(full[b0].sem, 1)
                                    take(b1, kind, h, f"kk_{sg}")
                                    for j in range(2):
                                        c = 4 * sg + 2 * g + j
                                        kc = kT[par][:, c * P:(c + 1) * P]
                                        ins = pe.matmul(bank[b1][:, j], kc, kc, start=True, stop=True)
                                    ins.then_inc(full[b1].sem, 1)
                                elif slot == "level1":
                                    pe.wait_ge(gl_ready.sem, gl_ready.done(kind, h, f"1_{gi}"))
                                    take(b0, kind, h, f"level1_{sg}")
                                    for i in range(4):
                                        ins = pe.matmul(bank[b0][:, i], Gl[g][1][:, i], ident[:], start=True, stop=True)
                                    ins.then_inc(full[b0].sem, 1)
                                elif slot.startswith("below"):
                                    lv = int(slot[5:])
                                    pe.wait_ge(gl_ready.sem, gl_ready.done(kind, h, f"{lv}_{gi}"))
                                    take(b0, kind, h, f"below{lv}_{sg}")
                                    for i in range(4):
                                        ins = pe.matmul(bank[b0][:, i], Gl[g][lv % 2][:, i], Tn[g][:, i], start=True, stop=True)
                                    ins.then_inc(full[b0].sem, 1)
                                elif slot.startswith("merge"):
                                    lv = int(slot[5:])
                                    pe.wait_ge(free[b0].sem, free[b0].done(kind, h, f"below{lv}_{sg}"))
                                    if lv == 2:
                                        pe.wait_ge(u1_ready.sem, u1_ready.done(kind, h, gi))
                                    take(b1, kind, h, f"U{lv}_{sg}")
                                    if lv < LEVELS:
                                        for i in range(4):
                                            ins = pe.matmul(bank[b0][:, i], Ut[g][:, i], W[g][:, i], start=True, stop=True)
                                        ins.then_inc(full[b0].sem, 1)
                                    for i in range(4):
                                        ins = pe.matmul(bank[b1][:, i], W[g][:, i], Ut[g][:, i], start=True, stop=True)
                                    ins.then_inc(full[b1].sem, 1)
                                elif slot == "attn":
                                    take(b0, kind, h, f"attn_{sg}")
                                    for j in range(2):
                                        c = 4 * sg + 2 * g + j
                                        ins = pe.matmul(bank[b0][:, j], kT[par][:, c * P:(c + 1) * P], qT[par][:, c * P:(c + 1) * P],
                                                        start=True, stop=True)
                                    ins.then_inc(full[b0].sem, 1)
                            if scan and k in SCAN_AT:
                                scan_quantum(12 * sg + SCAN_AT[k])
                            if not no_proj and k in PROJ_AT[sg]:
                                u = PROJ_AT[sg][k]
                                project(kind, h, u, w_in_ready.done(kind, h, "w"), p_free.ahead(kind, h, f"p{u}"))
                else:
                    for i in range(24):
                        scan_quantum(i)
                if not no_proj:
                    for u in PROJ_TAIL:
                        project(kind, h, u, w_in_ready.done(kind, h, "w"), p_free.ahead(kind, h, f"p{u}"))
                if scan:
                    pe.wait_ge(tail_dve.sem, tail_dve.done(kind, h, "ogn"))
                    for u in range(4):
                        take(u, kind, h, f"flip{u}")
                        for i in range(4):
                            ins = pe.transpose(bank[u][:, i], og[:, 4 * u + i], ident[:])
                        ins.then_inc(full[u].sem, 1)
                    pe.wait_ge(w_o_ready.sem, w_o_ready.done(kind, h, "w") * 16)
                    for u in range(4):
                        take(u, kind, h, f"out{u}")
                        for j in range(2):
                            c = 2 * u + j
                            for e in range(HD):
                                ins = pe.matmul(flat(bank[u][:, 2 * j:2 * j + 2]), ogT[:, c * HD + e], w_o[:, e],
                                                start=e == 0, stop=e == HD - 1)
                        ins.then_inc(full[u].sem, 1)

            pe.wait_ge(s_const, 1)
            for u in range(8):
                project("pre", 0, u, 1, u if u else None)
            run_steps(pe, step)

        @block.scalar
        def _(act):
            def copy_raw(u, fulls, conv_two_before):
                j, half = u // 2, u % 2
                act.wait_ge(p_full.sem, fulls)
                if half == 0 and conv_two_before is not None:
                    act.wait_ge(conv_done.sem, conv_two_before)
                act.activation(raw[j % 2][:, 3 + half * 512:3 + (half + 1) * 512], bank_p[:], ACT.Copy).then_inc(p_free.sem, 1)

            def step(kind, h, par):
                scan = kind != "first"
                inv_ = kind != "last"
                no_proj = kind == "last" or (isinstance(h, int) and h == HK - 1)

                def raw_unit(u):
                    j = u // 2
                    base = conv_done.base(kind, h)
                    copy_raw(u, p_full.done(kind, h, f"p{u}"), base + 4 * (j - 1))

                def scan_quantum(i):
                    c, part = i // 3, i % 3
                    if part == 0:
                        act.wait_ge(b_full.sem, b_full.done(kind, h, f"qs{c}"))
                        for e in range(HD):
                            ins = act.activation(O1[:, e], bank_b[:, e], ACT.Copy, scale=cf[1 - par][:, GAM, c * HD + e:c * HD + e + 1])
                        ins.then_inc(b_free.sem, 1)
                    elif part == 1:
                        act.wait_ge(c_free.sem, c_free.done(kind, h, f"tx{c}"))
                        for e in range(HD):
                            ins = act.activation(Dt[:, e], Dl[:, e], ACT.Copy, scale=cf[1 - par][:, TAIL, c * HD + e:c * HD + e + 1])
                        ins.then_inc(dt_ready.sem, 1)
                    elif c > 0:
                        squares(c - 1)

                def squares(c):
                    act.wait_ge(og_ready.sem, og_ready.done(kind, h, f"og{c}"))
                    for e in range(HD):
                        wait(act, sq_ready, 2 * (sq_ready.ahead(kind, h, f"sq{c}")) + e)
                        act.activation(junk[:], og[:, c * HD + e], ACT.Square,
                                       accum_out=ms[:, c * HD + e:c * HD + e + 1]).then_inc(sq_ready.sem, 1)

                def z_unit(u):
                    act.wait_ge(full[u].sem, full[u].done(kind, h, f"z{u}"))
                    if u == 0:
                        wait(act, og_ready, og_ready.base(kind, h))
                    act.activation(z[:, 2 * u:2 * u + 2].rearrange("p a b -> p (a b)"), flat(bank[u][:]), ACT.Silu).then_inc(free[u].sem, 1)

                if inv_:
                    conv = conv_done.base(kind, h)
                    act.wait_ge(conv_done.sem, conv - 12)
                    wait(act, a_full, a_full.base(kind, h))
                    wait(act, b_full, b_full.base(kind, h))
                    act.activation(kT[par][:], y[0][:], ACT.Silu).then_inc(act_ready.sem, 1)
                if scan:
                    z_unit(0)
                if inv_:
                    act.wait_ge(conv_done.sem, conv - 8)
                    act.activation(qT[par][:], y[1][:], ACT.Silu).then_inc(act_ready.sem, 1)
                if scan:
                    z_unit(1)
                if inv_:
                    act.wait_ge(act_ready.sem, act_ready.done(kind, h, "k"))
                    act.activation(y[0][:], kT[par][:], ACT.Square).then_inc(act_ready.sem, 1)
                if scan:
                    z_unit(2)
                if inv_:
                    act.wait_ge(act_ready.sem, act_ready.done(kind, h, "q"))
                    act.activation(y[1][:], qT[par][:], ACT.Square).then_inc(act_ready.sem, 1)
                if scan:
                    z_unit(3)
                if inv_:
                    act.wait_ge(conv_done.sem, conv)
                    act.activation(y[2][:], y[2][:], ACT.Silu).then_inc(act_ready.sem, 1)
                    act.activation(y[3][:], y[3][:], ACT.Silu).then_inc(act_ready.sem, 1)
                    for sg in range(2):
                        for k, slot in enumerate(SLOTS):
                            for g in range(2):
                                b0, b1, gi = 2 * g, 2 * g + 1, f"{sg}_{g}"
                                if slot == "decay":
                                    act.wait_ge(full[b0].sem, full[b0].done(kind, h, f"decay_{sg}"))
                                    wait(act, dm_ready, dm_ready.done(kind, h, gi) - 2)
                                    act.activation(flat(Dx[g][:]), flat(bank[b0][:]), ACT.Exp).then_inc(free[b0].sem, 1)
                                elif slot.startswith("merge"):
                                    lv = int(slot[5:])
                                    if lv < LEVELS:
                                        act.wait_ge(full[b0].sem, full[b0].done(kind, h, f"T{lv}_{sg}"))
                                        act.activation(flat(Tn[g][:]), flat(bank[b0][:]), ACT.Copy).then_inc(free[b0].sem, 1)
                                    act.wait_ge(full[b1].sem, full[b1].done(kind, h, f"U{lv}_{sg}"))
                                    dst = Ut[g][:] if lv < LEVELS else Uf[:, 8 * sg + 4 * g:8 * sg + 4 * g + 4]
                                    act.activation(flat(dst), flat(bank[b1][:]), ACT.Copy).then_inc(free[b1].sem, 1)
                            if scan and k in SCAN_AT:
                                scan_quantum(12 * sg + SCAN_AT[k])
                            if not no_proj and k in PROJ_AT[sg]:
                                raw_unit(PROJ_AT[sg][k])
                else:
                    for i in range(24):
                        scan_quantum(i)
                if scan:
                    squares(C - 1)
                if not no_proj:
                    for u in PROJ_TAIL:
                        raw_unit(u)
                if scan:
                    for u in range(4):
                        act.wait_ge(full[u].sem, full[u].done(kind, h, f"flip{u}"))
                        act.activation(flat(ogT[:, 4 * u:4 * u + 4]), flat(bank[u][:]), ACT.Copy, scale=gamma[:]).then_inc(free[u].sem, 1)

            for u in range(8):
                j = u // 2
                copy_raw(u, u + 1, 4 * (j - 1) if j >= 2 else None)
            run_steps(act, step)

        @block.vector
        def _(dve):
            def conv(j, head, raws, base):
                dve.wait_ge(p_free.sem, raws)
                for t in range(4):
                    tap = conv_w[:, bass.ds(head, 1), j, t:t + 1].rearrange("p a b -> p (a b)")
                    src = raw[j % 2][:, t:t + T]
                    if t == 0:
                        dve.tensor_scalar(y[j][:], src, tap, None, ALU.mult).then_inc(conv_done.sem, 1)
                    else:
                        dve.wait_ge(conv_done.sem, base + 4 * j + t)
                        dve.scalar_tensor_tensor(y[j][:], src, tap, y[j][:], ALU.mult, ALU.add).then_inc(conv_done.sem, 1)

            def step(kind, h, par):
                scan = kind != "first"
                inv_ = kind != "last"
                no_proj = kind == "last" or (isinstance(h, int) and h == HK - 1)
                cfs, ccs = cf[1 - par], cc[1 - par]

                def scan_quantum(i):
                    c, part = i // 3, i % 3
                    it = c * HD
                    if part == 0:
                        dve.wait_ge(a_full.sem, a_full.done(kind, h, f"ks{c}"))
                        for e in range(HD):
                            ins = dve.scalar_tensor_tensor(X[:, e], bank_a[:, e], cfs[:, NGAM, it + e:it + e + 1],
                                                           v_s[1 - par][:, it + e], ALU.mult, ALU.add)
                        ins.then_inc(a_free.sem, 1)
                    elif part == 1:
                        dve.wait_ge(c_full.sem, c_full.done(kind, h, f"tx{c}"))
                        wait(dve, dt_ready, dt_ready.ahead(kind, h, f"dt{c}"))
                        dve.tensor_tensor(Dl[:], bank_c[:, 0:2], bc_last(ccs[:, it:it + 2], P), ALU.mult).then_inc(c_free.sem, 1)
                    else:
                        dve.wait_ge(a_full.sem, a_full.done(kind, h, f"su{c}"))
                        for e in range(HD):
                            ins = dve.scalar_tensor_tensor(S[:, e], S[:, e], cfs[:, GAMC, it + e:it + e + 1],
                                                           bank_a[:, e], ALU.mult, ALU.add)
                        ins.then_inc(a_free.sem, 1)
                        dve.wait_ge(b_full.sem, b_full.done(kind, h, f"o{c}"))
                        wait(dve, og_ready, og_ready.ahead(kind, h, f"og{c}"))
                        dve.tensor_tensor(O2[:], bank_b[:, 0:2], O1[:], ALU.add).then_inc(b_free.sem, 1)

                if inv_:
                    dve.tensor_copy(cf[par][:], coef[:, :, bass.ds(h, 1)].rearrange("p q a i -> p q (a i)")).then_inc(cf_ready.sem, 1)
                    for u in range(2):
                        dve.wait_ge(full[u].sem, full[u].done(kind, h, f"k{u}"))
                        dve.tensor_copy(flat(k_tok[par][:, 4 * u:4 * u + 4]), flat(bank[u][:])).then_inc(free[u].sem, 1)
                    dve.wait_ge(full[2].sem, full[2].done(kind, h, "norm"))
                    wait(dve, roots_ready, roots_ready.base(kind, h))
                    dve.tensor_scalar(norms[:], bank[2][:, 0, 0:2 * C], EPS, None, ALU.add).then_inc(free[2].sem, 1)
                    dve.wait_ge(free[2].sem, free[2].done(kind, h, "norm"))
                    wait(dve, cc_ready, cc_ready.base(kind, h))
                    dve.reciprocal(inv[:], norms[:, 0:C]).then_inc(inv_ready.sem, 1)
                    dve.wait_ge(inv_ready.sem, inv_ready.done(kind, h, "it"))
                    dve.wait_ge(cf_ready.sem, cf_ready.done(kind, h, "it"))
                    dve.tensor_tensor(cc[par][:].rearrange("p (c e) -> p c e", e=HD), bc_last(inv[:], HD),
                                      cf[par][:, BETA].rearrange("p (c e) -> p c e", e=HD), ALU.mult).then_inc(cc_ready.sem, 1)
                    dve.wait_ge(roots_ready.sem, roots_ready.done(kind, h, "it"))
                    for u in range(4):
                        b = (3 + u) % 4
                        dve.wait_ge(full[b].sem, full[b].done(kind, h, f"v{u}"))
                        for j in range(2):
                            c = 2 * u + j
                            ins = dve.tensor_scalar(flat(v_s[par][:, 2 * c:2 * c + 2]), flat(bank[b][:, 2 * j:2 * j + 2]),
                                                    roots[par][:, c:c + 1], None, ALU.mult)
                        ins.then_inc(free[b].sem, 1)
                    for sg in range(2):
                        for k, slot in enumerate(SLOTS):
                            for g in range(2):
                                b0, b1, gi = 2 * g, 2 * g + 1, f"{sg}_{g}"
                                if slot == "decay":
                                    dve.wait_ge(full[b1].sem, full[b1].done(kind, h, f"kk_{sg}"))
                                    dve.wait_ge(ds_ready.sem, ds_ready.done(kind, h, gi))
                                    wait(dve, gl_ready, gl_ready.done(kind, h, f"{LEVELS}_{gi}") - 2 * LEVELS)
                                    dve.wait_ge(cc_ready.sem, cc_ready.done(kind, h, "it"))
                                    for i in range(4):
                                        it = 8 * sg + 4 * g + i
                                        ins = dve.scalar_tensor_tensor(G[g][:, i], bank[b1][:, i // 2], cc[par][:, it:it + 1],
                                                                       Ds[g][:, i], ALU.mult, ALU.mult)
                                    ins.then_inc(free[b1].sem, 1)
                                elif slot == "level1":
                                    dve.wait_ge(full[b0].sem, full[b0].done(kind, h, f"level1_{sg}"))
                                    dve.tensor_tensor(Tn[g][:], bc_mid(ident[:], 4), bank[b0][:], ALU.subtract).then_inc(free[b0].sem, 1)
                                elif slot.startswith("below"):
                                    lv = int(slot[5:])
                                    dve.wait_ge(full[b0].sem, full[b0].done(kind, h, f"below{lv}_{sg}"))
                                    dve.tensor_tensor(W[g][:], bc_mid(ident[:], 4), bank[b0][:], ALU.subtract).then_inc(free[b0].sem, 1)
                                elif slot == "attn":
                                    dve.wait_ge(full[b0].sem, full[b0].done(kind, h, f"attn_{sg}"))
                                    dve.wait_ge(dm_ready.sem, dm_ready.done(kind, h, gi))
                                    for j in range(2):
                                        it = 8 * sg + 4 * g + 2 * j
                                        ins = dve.tensor_tensor(At[:, it:it + 2], bc_mid(bank[b0][:, j], 2),
                                                                Dm[g][:, 2 * j:2 * j + 2], ALU.mult)
                                    ins.then_inc(free[b0].sem, 1)
                            if scan and k in SCAN_AT:
                                scan_quantum(12 * sg + SCAN_AT[k])
                            if not no_proj and k in PROJ_AT[sg] and PROJ_AT[sg][k] % 2:
                                u = PROJ_AT[sg][k]
                                conv(u // 2, h + 1, p_free.done(kind, h, f"p{u}"), conv_done.base(kind, h))
                else:
                    for i in range(24):
                        scan_quantum(i)
                if scan:
                    rq = roots[1 - par][:, C:2 * C]
                    dve.tensor_tensor(rq2[:], rq, rq, ALU.mult).then_inc(tail_dve.sem, 1)
                    dve.wait_ge(tail_dve.sem, tail_dve.done(kind, h, "rq2"))
                    dve.wait_ge(sq_ready.sem, 2 * sq_ready.done(kind, h, f"sq{C - 1}"))
                    dve.tensor_tensor(var[:].rearrange("p (c e) -> p c e", e=HD), ms[:].rearrange("p (c e) -> p c e", e=HD),
                                      bc_last(rq2[:], HD), ALU.mult).then_inc(tail_dve.sem, 1)
                    dve.wait_ge(tail_dve.sem, tail_dve.done(kind, h, "var0"))
                    dve.tensor_scalar(var[:], var[:], 1.0 / (P * P), EPS, ALU.mult, ALU.add).then_inc(tail_dve.sem, 1)
                if not no_proj:
                    conv(3, h + 1, p_free.done(kind, h, "p7"), conv_done.base(kind, h))
                if scan:
                    dve.wait_ge(tail_pow.sem, tail_pow.done(kind, h, "it"))
                    dve.scalar_tensor_tensor(fac[:].rearrange("p (c e) -> p c e", e=HD), rs[:].rearrange("p (c e) -> p c e", e=HD),
                                             float(P) ** -0.5, bc_last(rq, HD), ALU.mult, ALU.mult).then_inc(tail_dve.sem, 1)
                    dve.wait_ge(tail_dve.sem, tail_dve.done(kind, h, "fac"))
                    dve.tensor_tensor(og[:], og[:], bc_last(fac[:], P), ALU.mult).then_inc(tail_dve.sem, 1)
                    if not (isinstance(h, int) and h == HK):
                        dve.memset(S[:], 0.0).then_inc(s_zero.sem, 1)
                    for u in range(4):
                        dve.wait_ge(full[u].sem, full[u].done(kind, h, f"out{u}"))
                        xs = x[:, 2 * u:2 * u + 2]
                        wait(dve, free[u], free[u].base(kind, h))
                        dve.tensor_tensor(xs.rearrange("p a b -> p (a b)"), xs.rearrange("p a b -> p (a b)"),
                                          flat(bank[u][:]), ALU.add).then_inc(free[u].sem, 1)
                else:
                    dve.memset(S[:], 0.0).then_inc(s_zero.sem, 1)

            dve.memset(ones_col[:], 1.0).then_inc(s_const, 1)
            for j in range(4):
                conv(j, 0, 2 * j + 2, 0)
            run_steps(dve, step)
            for u in range(4):
                dve.wait_ge(free[u].sem, free[u].done("last", HK, f"out{u}"))

        @block.gpsimd
        def _(pool):
            def step(kind, h, par):
                scan = kind != "first"
                inv_ = kind != "last"

                def gate(c):
                    it = c * HD
                    pool.wait_ge(b_free.sem, b_free.done(kind, h, f"o{c}"))
                    if c == 0:
                        for u in range(4):
                            wait(pool, full[u], full[u].base(kind, h))
                    pool.tensor_tensor(og[:, it:it + 2], O2[:], z[:, c].rearrange("p (e d) -> p e d", e=HD),
                                       ALU.mult).then_inc(og_ready.sem, 1)

                if inv_:
                    pool.wait_ge(free[2].sem, free[2].done(kind, h, "norm"))
                    pool.tensor_tensor(roots[par][:], norms[:], powers[:], ALU.pow).then_inc(roots_ready.sem, 1)
                    pool.wait_ge(cf_ready.sem, cf_ready.done(kind, h, "it"))
                    for sg in range(2):
                        for k, slot in enumerate(SLOTS):
                            for g in range(2):
                                b0, b1, gi = 2 * g, 2 * g + 1, f"{sg}_{g}"
                                it = 8 * sg + 4 * g
                                if slot == "decay":
                                    if g == 0:
                                        for gg in range(2):
                                            i2 = 8 * sg + 4 * gg
                                            wait(pool, full[2 * gg], full[2 * gg].done(kind, h, "decay_0") if sg else full[2 * gg].base(kind, h))
                                            pool.tensor_tensor(gU[gg][:], bc_mid(upto[:], 4), bc_last(cf[par][:, G_, i2:i2 + 4], P),
                                                               ALU.mult).then_inc(gu_ready.sem, 1)
                                    pool.wait_ge(free[b0].sem, free[b0].done(kind, h, f"decay_{sg}"))
                                    pool.tensor_tensor(Ds[g][:], Dx[g][:], bc_mid(before_[:], 4), ALU.mult).then_inc(ds_ready.sem, 1)
                                elif slot == "level1":
                                    pool.wait_ge(free[b1].sem, free[b1].done(kind, h, f"kk_{sg}"))
                                    read_before(kind, h, sg, b0, f"below{LEVELS}_0")
                                    mask_level(kind, h, sg, g, 1)
                                    pool.wait_ge(gl_ready.sem, gl_ready.done(kind, h, f"1_{gi}"))
                                    read_before(kind, h, sg, b1, f"U{LEVELS}_0")
                                    pool.tensor_tensor(Ut[g][:], bc_mid(ident[:], 4), Gl[g][1][:], ALU.subtract).then_inc(u1_ready.sem, 1)
                                elif slot.startswith("below") and int(slot[5:]) < LEVELS:
                                    lv = int(slot[5:])
                                    if lv == 2 and g == 0:
                                        for gg in range(2):
                                            read_before(kind, h, sg, 2 * gg, f"below{LEVELS - 1}_0")
                                            mask_level(kind, h, sg, gg, 2)
                                    what = f"below{lv - 1}_{sg}" if lv > 2 else f"level1_{sg}"
                                    pool.wait_ge(full[b0].sem, full[b0].done(kind, h, what))
                                    if lv == 2:
                                        pool.wait_ge(u1_ready.sem, u1_ready.done(kind, h, gi))
                                    mask_level(kind, h, sg, g, lv + 1)
                                elif slot == "merge3":
                                    pool.tensor_tensor(Dm[g][:], Dx[g][:], bc_mid(dm_mask[:], 4), ALU.mult).then_inc(dm_ready.sem, 1)
                            if scan and k in SCAN_AT and SCAN_AT[k] % 3 == 2:
                                gate(4 * sg + SCAN_AT[k] // 3)
                else:
                    for c in range(C):
                        gate(c)
                if scan:
                    pool.wait_ge(tail_dve.sem, tail_dve.done(kind, h, "var"))
                    pool.tensor_tensor(rs[:], var[:], minus_half[:], ALU.pow).then_inc(tail_pow.sem, 1)

            def read_before(kind, h, sg, b, name):
                wait(pool, full[b], full[b].done(kind, h, name) if sg else full[b].base(kind, h))

            def mask_level(kind, h, sg, g, lv):
                pool.tensor_tensor(Gl[g][lv % 2][:], G[g][:], bc_mid(levels[:, lv - 1], 4), ALU.mult).then_inc(gl_ready.sem, 1)

            run_steps(pool, step)


F1 = 512
NF = F1 // P


def perceptron(nc, x, hT, consts, d):
    with ExitStack() as stack:
        a = Alloc(nc, stack, "mlp")
        w1 = a.sb("w1", [P, KD, F1])
        w2 = a.sb("w2", [P, NF, F1])
        w3 = a.sb("w3", [P, NF, D])
        b12 = a.sb("b12", [P, 2, NF])
        b3 = a.sb("b3", [P, D])
        names = ["w1", "w2", "w3", "b12", "b3"]
        tiles = dict(zip(names, [w1, w2, w3, b12, b3]))
        loaded = {n: a.sem(f"{n}_loaded") for n in names}

        def prefetch(sp):
            for n in names:
                src = d[f"mlp_{n}"]
                sp.dma_start(tiles[n][:], src.to_broadcast([P, D]) if n == "b3" else src).then_inc(loaded[n], 16)

        with ExitStack() as inner:
            layernorm_transposed(nc, Alloc(nc, inner, "norm2", a), x, hT, consts["ident"], EPS_LN, prefetch=prefetch)
        h = [a.sb("h1", [P, NF, T]), a.sb("h2", [P, NF, T])]
        bank = [a.psum([P, 512]) for i in range(4)]
        s_full, s_relu = a.sem("product_ready"), a.sem("relu_written")
        s_bias, s_out, s_sum = a.sem("bias_added"), a.sem("out_ready"), a.sem("out_added")
        units = [(l, half, f) for l in range(2) for half in range(2) for f in range(NF)]
        with nc.Block() as block:
            @block.tensor
            def _(pe):
                pe.wait_ge(loaded["w1"], 16)
                for n, (l, half, f) in enumerate(units):
                    if l == 1 and half == 0 and f == 0:
                        pe.wait_ge(loaded["w2"], 16)
                    if n >= 4:
                        pe.wait_ge(s_relu, n - 3)
                    if l == 1 and f == 0:
                        pe.wait_ge(s_relu, NF * (half + 1))
                    src, w, nk = (hT, w1, KD) if l == 0 else (h[0], w2, NF)
                    for k in range(nk):
                        ins = pe.matmul(bank[n % 4][:], w[:, k, f * P:(f + 1) * P], src[:, k, half * 512:(half + 1) * 512],
                                        start=k == 0, stop=k == nk - 1)
                    ins.then_inc(s_full, 1)
                pe.wait_ge(loaded["w3"], 16)
                for u in range(NT // 2):
                    n = len(units)
                    pe.wait_ge(s_relu, n)
                    for j in range(2):
                        t = 2 * u + j
                        for k in range(NF):
                            ins = pe.matmul(bank[u][:, j * D:(j + 1) * D], h[1][:, k, t * P:(t + 1) * P], w3[:, k],
                                            start=k == 0, stop=k == NF - 1)
                    ins.then_inc(s_out, 1)

            @block.scalar
            def _(act):
                act.wait_ge(loaded["b12"], 16)
                for n, (l, half, f) in enumerate(units):
                    act.wait_ge(s_full, n + 1)
                    act.activation(h[l][:, f, half * 512:(half + 1) * 512], bank[n % 4][:], ACT.Relu,
                                   bias=b12[:, l, f:f + 1]).then_inc(s_relu, 1)

            @block.vector
            def _(dve):
                dve.wait_ge(loaded["b3"], 16)
                dve.tensor_tensor(x[:], x[:], bc_mid(b3[:], NT), ALU.add).then_inc(s_bias, 1)
                dve.wait_ge(s_bias, 1)
                for u in range(NT // 2):
                    dve.wait_ge(s_out, u + 1)
                    xs = x[:, 2 * u:2 * u + 2].rearrange("p a b -> p (a b)")
                    dve.tensor_tensor(xs, xs, bank[u][:], ALU.add).then_inc(s_sum, 1)
                dve.wait_ge(s_sum, NT // 2)
        a.clear_sems()


NH = 4
DH = D // NH


def attention(nc, x, hT, consts, d):
    ident = consts["ident"]
    with ExitStack() as stack:
        a = Alloc(nc, stack, "attn")
        names = ["wq", "wk", "wv", "wo", "bqk", "bv", "bo"]
        tiles = {n: a.sb(n, [P, KD, D]) for n in names[:4]}
        tiles["bqk"] = a.sb("bqk", [P, 2, KD])
        tiles["bv"], tiles["bo"] = a.sb("bv", [P, D]), a.sb("bo", [P, D])
        loaded = {n: a.sem(f"{n}_loaded") for n in names}

        def prefetch(sp):
            for n in names:
                src = d[f"attn_{n}"]
                sp.dma_start(tiles[n][:], src.to_broadcast([P, D]) if n in ("bv", "bo") else src).then_inc(loaded[n], 16)

        with ExitStack() as inner:
            layernorm_transposed(nc, Alloc(nc, inner, "norm3", a), x, hT, ident, EPS_LN, prefetch=prefetch)
        qkT = [a.sb("qT", [P, KD, T]), a.sb("kT", [P, KD, T])]
        v = a.sb("v", [P, NT, D])
        feats = a.sb("feats", [P, NT, D])
        featsT = a.sb("featsT", [P, KD, T])
        prob = [a.sb(f"prob{i}", [P, T]) for i in range(2)]
        probT = [a.sb(f"probT{i}", [P, NT, P]) for i in range(2)]
        neg = a.sb("neg_max", [P, NH * NT])
        total = a.sb("total", [P, NH * NT])
        rtotal = a.sb("rtotal", [P, NH * NT])
        score = [a.psum([P, T]) for i in range(2)]
        flip = [a.psum([P, 4, P]) for i in range(2)]
        mix = a.psum([P, 512])
        spare = a.psum([P, 512])

        bank = [score[0][:, 0:512], score[1][:, 0:512], flip[0][:].rearrange("p a b -> p (a b)"), mix[:]]
        s_full, s_qk, s_v = a.sem("proj_ready"), a.sem("qk_written"), a.sem("v_written")
        qk_units = [(w, f, half) for w in range(2) for f in range(KD) for half in range(2)]
        with nc.Block() as block:
            @block.tensor
            def _(pe):
                for n, (w, f, half) in enumerate(qk_units):
                    pe.wait_ge(loaded[names[w]], 16)
                    if n >= 4:
                        pe.wait_ge(s_qk, n - 3)
                    for kd in range(KD):
                        ins = pe.matmul(bank[n % 4], tiles[names[w]][:, kd, f * P:(f + 1) * P],
                                        hT[:, kd, half * 512:(half + 1) * 512], start=kd == 0, stop=kd == KD - 1)
                    ins.then_inc(s_full, 1)
                pe.wait_ge(loaded["wv"], 16)
                for u in range(NT // 2):
                    pe.wait_ge(s_qk, u + 5)
                    for j in range(2):
                        t = 2 * u + j
                        for kd in range(KD):
                            ins = pe.matmul(bank[u][:, j * D:(j + 1) * D], hT[:, kd, t * P:(t + 1) * P], tiles["wv"][:, kd],
                                            start=kd == 0, stop=kd == KD - 1)
                    ins.then_inc(s_full, 1)

            @block.scalar
            def _(act):
                act.wait_ge(loaded["bqk"], 16)
                for n, (w, f, half) in enumerate(qk_units):
                    act.wait_ge(s_full, n + 1)
                    act.activation(qkT[w][:, f, half * 512:(half + 1) * 512], bank[n % 4], ACT.Identity,
                                   bias=tiles["bqk"][:, w, f:f + 1]).then_inc(s_qk, 1)

            @block.vector
            def _(dve):
                dve.wait_ge(loaded["bv"], 16)
                for u in range(NT // 2):
                    dve.wait_ge(s_full, 8 + u + 1)
                    dve.tensor_tensor(v[:, 2 * u:2 * u + 2], bank[u].rearrange("p (a b) -> p a b", a=2),
                                      bc_mid(tiles["bv"][:], 2), ALU.add).then_inc(s_v, 1)
                dve.wait_ge(s_v, NT // 2)

        rows = [(hh, t) for hh in range(NH) for t in range(NT)]
        R = len(rows)
        s_score, s_max, s_exp = a.sem("scores_ready"), a.sem("max_ready"), a.sem("probs_ready")
        s_flip, s_pt, s_mix = a.sem("probs_flipped"), a.sem("probT_written"), a.sem("mixed")
        s_rt, s_feat, s_rowmax = a.sem("total_inverted"), a.sem("feats_written"), a.sem("row_max")
        with nc.Block() as block:
            @block.tensor
            def _(pe):
                def scores(r):
                    hh, t = rows[r]
                    f, p0 = hh // 2, (hh % 2) * DH
                    if r >= 2:
                        pe.wait_ge(s_exp, r - 1)
                    for half in range(2):
                        ins = pe.matmul(score[r % 2][:, half * 512:(half + 1) * 512], qkT[0][p0:p0 + DH, f, t * P:(t + 1) * P],
                                        qkT[1][p0:p0 + DH, f, half * 512:(half + 1) * 512], start=True, stop=True)
                    ins.then_inc(s_score, 1)

                def transposes(r):
                    pe.wait_ge(s_exp, r + 1)
                    for half in range(2):
                        if r >= 1:
                            pe.wait_ge(s_pt, 2 * (r - 1) + half + 1)
                        for j in range(4):
                            k = half * 4 + j
                            ins = pe.transpose(flip[half][:, j], prob[r % 2][:, k * P:(k + 1) * P], ident[:])
                        ins.then_inc(s_flip, 1)

                def mixes(r):
                    hh, t = rows[r]
                    pe.wait_ge(s_pt, 2 * r + 2)
                    out = (mix, spare)[r % 2]
                    if r >= 2:
                        pe.wait_ge(s_feat, r - 1)
                    for k in range(NT):
                        ins = pe.matmul(out[:, 0:DH], probT[r % 2][:, k], v[:, k, hh * DH:(hh + 1) * DH],
                                        start=k == 0, stop=k == NT - 1)
                    ins.then_inc(s_mix, 1)

                scores(0)
                for r in range(R + 1):
                    if r + 1 < R:
                        scores(r + 1)
                    if r >= 1:
                        mixes(r - 1)
                    if r < R:
                        transposes(r)

            @block.scalar
            def _(act):
                for r in range(R + 1):
                    if r < R:
                        act.wait_ge(s_max, r + 1)
                        if r >= 2:
                            act.wait_ge(s_flip, 2 * (r - 1))
                        act.activation(prob[r % 2][:], score[r % 2][:], ACT.Exp, bias=neg[:, r:r + 1], scale=0.5,
                                       accum_out=total[:, r:r + 1]).then_inc(s_exp, 1)
                    if r >= 1:
                        act.wait_ge(s_flip, 2 * r)
                        if r >= 3:
                            act.wait_ge(s_mix, r - 2)
                        act.wait_ge(s_pt, 2 * r - 1)
                        act.activation(probT[(r - 1) % 2][:, 4:8].rearrange("p a b -> p (a b)"),
                                       flip[1][:].rearrange("p a b -> p (a b)"), ACT.Copy).then_inc(s_pt, 1)

            @block.vector
            def _(dve):
                for r in range(R + 2):
                    if r < R:
                        dve.wait_ge(s_score, r + 1)
                        dve.tensor_reduce(neg[:, r:r + 1], score[r % 2][:], AX_X, ALU.max).then_inc(s_rowmax, 1)
                        dve.wait_ge(s_rowmax, r + 1)
                        dve.tensor_scalar(neg[:, r:r + 1], neg[:, r:r + 1], -0.5, None, ALU.mult).then_inc(s_max, 1)
                    if 1 <= r <= R:
                        dve.wait_ge(s_flip, 2 * r - 1)
                        if r >= 3:
                            dve.wait_ge(s_mix, r - 2)
                        if r >= 2:
                            dve.wait_ge(s_pt, 2 * r - 2)
                        dve.tensor_copy(probT[(r - 1) % 2][:, 0:4].rearrange("p a b -> p (a b)"),
                                        flip[0][:].rearrange("p a b -> p (a b)")).then_inc(s_pt, 1)
                    if r >= 2:
                        hh, t = rows[r - 2]
                        dve.wait_ge(s_mix, r - 1)
                        dve.reciprocal(rtotal[:, r - 2:r - 1], total[:, r - 2:r - 1]).then_inc(s_rt, 1)
                        dve.wait_ge(s_rt, r - 1)
                        dve.tensor_scalar(feats[:, t, hh * DH:(hh + 1) * DH], (mix, spare)[r % 2][:, 0:DH], rtotal[:, r - 2:r - 1],
                                          None, ALU.mult).then_inc(s_feat, 1)
                dve.wait_ge(s_feat, R)

        s_ft, s_ftw, s_o, s_bo, s_add = (a.sem(n) for n in ("feats_flipped", "featsT_written", "out_ready", "bias_added", "out_added"))
        flat_bank = [score[0][:, 0:512], score[1][:, 0:512], flip[0][:].rearrange("p a b -> p (a b)"), mix[:]]
        with nc.Block() as block:
            @block.tensor
            def _(pe):
                for u in range(4):
                    f, half = u // 2, u % 2
                    for j in range(4):
                        t = half * 4 + j
                        ins = pe.transpose(flat_bank[u][:, j * P:(j + 1) * P], feats[:, t, f * P:(f + 1) * P], ident[:])
                    ins.then_inc(s_ft, 1)
                pe.wait_ge(s_ftw, 4)
                pe.wait_ge(loaded["wo"], 16)
                for u in range(NT // 2):
                    for j in range(2):
                        t = 2 * u + j
                        for f in range(KD):
                            ins = pe.matmul(flat_bank[u][:, j * D:(j + 1) * D], featsT[:, f, t * P:(t + 1) * P], tiles["wo"][:, f],
                                            start=f == 0, stop=f == KD - 1)
                    ins.then_inc(s_o, 1)

            @block.scalar
            def _(act):
                for u in range(4):
                    f, half = u // 2, u % 2
                    act.wait_ge(s_ft, u + 1)
                    act.activation(featsT[:, f, half * 512:(half + 1) * 512], flat_bank[u], ACT.Copy).then_inc(s_ftw, 1)

            @block.vector
            def _(dve):
                dve.wait_ge(loaded["bo"], 16)
                dve.tensor_tensor(x[:], x[:], bc_mid(tiles["bo"][:], NT), ALU.add).then_inc(s_bo, 1)
                dve.wait_ge(s_bo, 1)
                for u in range(NT // 2):
                    dve.wait_ge(s_o, u + 1)
                    xs = x[:, 2 * u:2 * u + 2].rearrange("p a b -> p (a b)")
                    dve.tensor_tensor(xs, xs, flat_bank[u], ALU.add).then_inc(s_add, 1)
                dve.wait_ge(s_add, NT // 2)
        a.clear_sems()


E = 32
TOPK = 4
FE = 176
FH = FE // 2
FS = 704
CAP = 128
SKIP = 8192.0
SH = [(i * P, min(P, FS - i * P)) for i in range((FS + P - 1) // P)]


def mixture(nc, x, hT, consts, d, w_gu, gu_loaded, buf, ybuf, s_zeroed, out):
    ident = consts["ident"]
    with ExitStack() as stack:
        a = Alloc(nc, stack, "moe")
        w_norm = a.sb("w_norm", [P, D])
        w_r = a.sb("w_r", [P, KD, E + 1])
        iota = a.sb("iota", [P, E])
        xn = a.sb("xn", [P, NT, D])
        rows = a.sb("rows", [P, NT * TOPK], U32)
        wv = a.sb("wv", [P, NT * TOPK])
        names = ["w_norm", "w_r", "iota"]
        tiles = dict(zip(names, [w_norm, w_r, iota]))
        loaded = {n: a.sem(f"{n}_loaded") for n in names + ["sw_gu", "sw_down"]}
        route_stack = ExitStack()
        b = Alloc(nc, route_stack, "route", a)
        sw_gu = b.sb("sw_gu", [P, 2, KD, FS])
        sw_down = b.sb("sw_down", [P, len(SH), D])

        def prefetch(sp):
            for n in names:
                src = d[f"moe_{n}"]
                sp.dma_start(tiles[n][:], src if n == "w_r" else src.to_broadcast(list(tiles[n].shape))).then_inc(loaded[n], 16)
            sp.dma_start(sw_gu[:], d["sw_gu"]).then_inc(loaded["sw_gu"], 16)
            sp.dma_start(sw_down[:, 0:5], d["sw_down"][:, 0:5]).then_inc(loaded["sw_down"], 16)
            sp.dma_start(sw_down[0:64, 5], d["sw_down"][0:64, 5]).then_inc(loaded["sw_down"], 16)

        with ExitStack() as inner:
            layernorm_transposed(nc, Alloc(nc, inner, "norm4", a), x, hT, ident, EPS_LN, prefetch=prefetch,
                                 rms_weight=w_norm, weight_ready=loaded["w_norm"], xn=xn)
        with route_stack:
            route_and_share(nc, b, x, hT, consts, xn, w_r, iota, loaded, sw_gu, sw_down, rows, wv, buf, s_zeroed)
        experts(nc, a, consts, d, w_gu, gu_loaded, buf, ybuf)
        combine(nc, a, x, rows, wv, ybuf, out)


def route_and_share(nc, a, x, hT, consts, xn, w_r, iota, loaded, sw_gu, sw_down, rows, wv, buf, s_zeroed):
    N = NT * TOPK
    before_, ones = consts["before"], a.sb("ones", [P, P])
    lg = a.sb("lg", [P, NT, E + 1])
    top = a.sb("top", [P, NT, 8])
    idx = a.sb("idx", [P, NT, 8], U32)
    idxf = a.sb("idxf", [P, NT, TOPK])
    hot = a.sb("hot", [P, NT, TOPK, E])
    prod = a.sb("prod", [P, NT, TOPK, E])
    chosen = a.sb("chosen", [P, NT, E])
    shift = a.sb("shift", [P, NT, E])
    shift4 = a.sb("shift4", [P, NT, TOPK])
    esum = a.sb("esum", [P, NT])
    rsum = a.sb("rsum", [P, NT])
    gate = a.sb("gate", [P, NT])
    pos = a.sb("pos", [P, N])
    valid = a.sb("valid", [P, N])
    row = a.sb("row", [P, N])
    dest_f = a.sb("dest_f", [P, N])
    dest = a.sb("dest", [P, N], U32)
    hsh = a.sb("hsh", [P, len(SH), T])
    up = a.sb("up", [P, 2, 512])
    lg_ps = a.psum([P, NT, 64])
    pos_ps = a.psum([P, NT, 64])
    gp = [a.psum([P, 512]) for i in range(2)]
    upp = [a.psum([P, 512]) for i in range(2)]
    down = [a.psum([P, 2, D]) for i in range(2)]
    s_lg, s_ones, s_r, s_e = a.sem("logits_ready"), a.sem("ones_ready"), a.sem("routing_step"), a.sem("exp_step")
    s_tops, s_pos, s_scat = a.sem("tops_step"), a.sem("places_ready"), a.sem("scattered")
    s_gp, s_upp, s_silu, s_hsh, s_down, s_add = (a.sem(n) for n in ("gate_ready", "up_ready", "silu_written", "hidden_written",
                                                                 "down_ready", "shared_added"))
    units = [(half, f) for half in range(2) for f in range(len(SH))]
    with nc.Block() as block:
        @block.tensor
        def _(pe):
            pe.wait_ge(loaded["w_r"], 16)
            for t in range(NT):
                for kd in range(KD):
                    ins = pe.matmul(lg_ps[:, t, 0:E + 1], hT[:, kd, t * P:(t + 1) * P], w_r[:, kd], start=kd == 0, stop=kd == KD - 1)
            ins.then_inc(s_lg, 1)
            pe.wait_ge(loaded["sw_gu"], 16)

            def places():
                pe.wait_ge(s_ones, 1)
                pe.wait_ge(s_r, 3)
                for t in range(NT):
                    for u in range(t + 1):
                        ins = pe.matmul(pos_ps[:, t, 0:E], before_[:] if u == t else ones[:], chosen[:, u], start=u == 0, stop=u == t)
                ins.then_inc(s_pos, 1)

            for n, (half, f) in enumerate(units):
                f0, fn = SH[f]
                if n >= 2:
                    pe.wait_ge(s_silu, n - 1)
                for w, ps, done in ((0, gp, s_gp), (1, upp, s_upp)):
                    if w == 1 and n >= 2:
                        pe.wait_ge(s_hsh, n - 1)
                    for kd in range(KD):
                        ins = pe.matmul(ps[n % 2][0:fn, :], sw_gu[:, w, kd, f0:f0 + fn], hT[:, kd, half * 512:(half + 1) * 512],
                                        start=kd == 0, stop=kd == KD - 1)
                    ins.then_inc(done, 1)
                if n == 4:
                    places()
            pe.wait_ge(loaded["sw_down"], 32)
            for u in range(NT // 2):
                pe.wait_ge(s_hsh, len(SH) * (u // 2 + 1))
                if u >= 2:
                    pe.wait_ge(s_add, 2 * (u - 1))
                for j in range(2):
                    t = 2 * u + j
                    for f, (f0, fn) in enumerate(SH):
                        ins = pe.matmul(down[u % 2][:, j], hsh[0:fn, f, t * P:(t + 1) * P], sw_down[0:fn, f],
                                        start=f == 0, stop=f == len(SH) - 1)
                ins.then_inc(s_down, 1)

        @block.scalar
        def _(act):
            act.wait_ge(s_tops, 2 * NT + 1)
            act.activation(gate[:], lg[:, :, E], ACT.Exp, scale=-1.0).then_inc(s_e, 1)
            act.wait_ge(s_r, 5)
            act.activation(shift[:], shift[:], ACT.Exp).then_inc(s_e, 1)
            act.activation(shift4[:], shift4[:], ACT.Exp).then_inc(s_e, 1)
            for n, (half, f) in enumerate(units):
                f0, fn = SH[f]
                act.wait_ge(s_gp, n + 1)
                if n >= 2:
                    act.wait_ge(s_hsh, n - 1)
                act.activation(up[0:fn, n % 2], gp[n % 2][0:fn, :], ACT.Silu).then_inc(s_silu, 1)

        @block.vector
        def _(dve):
            def hidden(n):
                half, f = units[n]
                f0, fn = SH[f]
                dve.wait_ge(s_silu, n + 1)
                dve.wait_ge(s_upp, n + 1)
                dve.tensor_tensor(hsh[0:fn, f, half * 512:(half + 1) * 512], up[0:fn, n % 2], upp[n % 2][0:fn, :],
                                  ALU.mult).then_inc(s_hsh, 1)

            dve.memset(ones[:], 1.0).then_inc(s_ones, 1)
            dve.wait_ge(s_lg, 1)
            dve.tensor_copy(lg[:], lg_ps[:, :, 0:E + 1]).then_inc(s_tops, 1)
            dve.wait_ge(s_tops, 1)
            for t in range(NT):
                dve.max(top[:, t], lg[:, t, 0:E]).then_inc(s_tops, 1)
            for t in range(NT):
                dve.wait_ge(s_tops, t + 2)
                dve.max_index(idx[:, t], top[:, t], lg[:, t, 0:E]).then_inc(s_tops, 1)
            dve.wait_ge(s_tops, 2 * NT + 1)
            dve.tensor_copy(idxf[:], idx[:, :, 0:TOPK]).then_inc(s_r, 1)
            dve.wait_ge(s_r, 1)
            dve.wait_ge(loaded["iota"], 16)
            dve.tensor_tensor(hot[:].rearrange("p t s e -> p (t s) e"), bc_last(idxf[:].rearrange("p t s -> p (t s)"), E),
                              bc_mid(iota[:], N), ALU.is_equal).then_inc(s_r, 1)
            dve.wait_ge(s_r, 2)
            dve.tensor_reduce(chosen[:], hot[:].rearrange("p t s e -> p t e s"), AX_X, ALU.add).then_inc(s_r, 1)
            dve.tensor_tensor(shift[:], lg[:, :, 0:E], bc_last(top[:, :, 0], E), ALU.subtract).then_inc(s_r, 1)
            dve.tensor_tensor(shift4[:], top[:, :, 0:TOPK], bc_last(top[:, :, 0], TOPK), ALU.subtract).then_inc(s_r, 1)
            dve.wait_ge(s_e, 3)
            dve.tensor_reduce(esum[:], shift[:], AX_X, ALU.add).then_inc(s_r, 1)
            dve.tensor_scalar(gate[:], gate[:], 1.0, None, ALU.add).then_inc(s_r, 1)
            dve.wait_ge(s_r, 7)
            dve.reciprocal(rsum[:], esum[:]).then_inc(s_r, 1)
            dve.reciprocal(gate[:], gate[:]).then_inc(s_r, 1)
            dve.wait_ge(s_r, 9)
            for n in range(4):
                hidden(n)
            dve.wait_ge(s_pos, 1)
            for t in range(NT):
                ins = dve.tensor_tensor(prod[:, t], hot[:, t], bc_mid(pos_ps[:, t, 0:E], TOPK), ALU.mult)
            ins.then_inc(s_r, 1)
            dve.wait_ge(s_r, 10)
            dve.tensor_reduce(pos[:], prod[:].rearrange("p t s e -> p (t s) e"), AX_X, ALU.add).then_inc(s_r, 1)
            dve.wait_ge(s_r, 11)
            dve.tensor_scalar(valid[:], pos[:], float(CAP), None, ALU.is_lt).then_inc(s_r, 1)
            dve.tensor_scalar(row[:], pos[:], float(CAP - 1), None, ALU.min).then_inc(s_r, 1)
            dve.wait_ge(s_r, 13)
            dve.scalar_tensor_tensor(row[:], idxf[:].rearrange("p t s -> p (t s)"), float(CAP), row[:], ALU.mult, ALU.add).then_inc(s_r, 1)
            dve.tensor_tensor(wv[:].rearrange("p (t s) -> p t s", s=TOPK), shift4[:], bc_last(rsum[:], TOPK), ALU.mult).then_inc(s_r, 1)
            dve.wait_ge(s_r, 15)
            dve.scalar_tensor_tensor(dest_f[:], valid[:], -SKIP, row[:], ALU.mult, ALU.add).then_inc(s_r, 1)
            dve.tensor_tensor(wv[:], wv[:], valid[:], ALU.mult).then_inc(s_r, 1)
            dve.wait_ge(s_r, 17)
            dve.tensor_copy(rows[:], row[:]).then_inc(s_r, 1)
            dve.tensor_scalar(dest[:], dest_f[:], SKIP, None, ALU.add).then_inc(s_r, 1)
            for n in range(4, len(units)):
                hidden(n)
            for u in range(NT // 2):
                dve.wait_ge(s_down, u + 1)
                for j in range(2):
                    t = 2 * u + j
                    dve.scalar_tensor_tensor(x[:, t], down[u % 2][:, j], gate[:, t:t + 1], x[:, t], ALU.mult, ALU.add).then_inc(s_add, 1)
            dve.wait_ge(s_add, NT)
            dve.wait_ge(s_r, 19)

        @block.gpsimd
        def _(pool):
            pool.wait_ge(s_zeroed, 16)
            pool.wait_ge(s_r, 19)
            for t in range(NT):
                for s in range(TOPK):
                    n = t * TOPK + s
                    pool.indirect_dma_start(out=buf, out_offset=bass.IndirectOffsetOnAxis(ap=dest[:, n:n + 1], axis=0),
                                            in_=xn[:, t], in_offset=None, bounds_check=E * CAP - 1,
                                            oob_is_err=False).then_inc(s_scat, 16)
            pool.wait_ge(s_scat, 16 * N)


UN = 4


def experts(nc, a, consts, d, w_gu, gu_loaded, buf, ybuf):
    ident = consts["ident"]
    be = [a.sb(f"be{i}", [P, D]) for i in range(UN)]
    wd = [a.sb(f"wd{i}", [FH, 2, D]) for i in range(UN)]
    bT = [a.sb(f"bT{i}", [P, KD, P]) for i in range(UN)]
    sg = [a.sb(f"sg{i}", [P, FE]) for i in range(UN)]
    hh = [a.sb(f"hh{i}", [P, FE]) for i in range(UN)]
    hhT = [a.sb(f"hhT{i}", [FH, 2, P]) for i in range(UN)]
    ys = [a.sb(f"ys{i}", [P, D]) for i in range(UN)]
    tb = [a.psum([P, 4, P]) for i in range(2)]
    gb = [a.psum([P, 512]) for i in range(2)]
    ht = [a.psum([P, 4, P]) for i in range(2)]
    yb = [a.psum([P, 512]) for i in range(2)]
    s_be = [a.sem(f"rows{i}_loaded") for i in range(UN)]
    s_wd = [a.sem(f"wd{i}_loaded") for i in range(UN)]
    s_y = [a.sem(f"y{i}_stored") for i in range(UN)]
    s_tb, s_bt, s_gb, s_sg, s_hh = (a.sem(n) for n in ("rows_flipped", "rowsT_written", "hidden_ready", "silu_written", "hidden_written"))
    s_ht, s_hht, s_yb, s_ys = (a.sem(n) for n in ("hidden_flipped", "hiddenT_written", "y_ready", "y_copied"))
    TURNS = E // UN

    def per_expert(eng, step):
        for i in range(UN):
            step(True, 0, i)
        with eng.Fori(1, TURNS) as t:
            for i in range(UN):
                step(False, t, i)

    with nc.Block() as block:
        @block.sync
        def _(sp):
            def load(first, t, i):
                e = t * UN + i
                if not first:
                    sp.wait_ge(s_tb, e - UN + 1)
                sp.dma_start(be[i][:], buf.rearrange("(e c) n -> e c n", c=CAP)[bass.ds(e, 1)].rearrange("a c n -> (a c) n")).then_inc(s_be[i], 16)

            per_expert(sp, load)

        @block.gpsimd
        def _(pool):
            def load_down(e, i):
                pool.dma_start(wd[i][:], d["w_down"][bass.ds(e, 1)].rearrange("a p k n -> (a p) k n")).then_inc(s_wd[i], 16)

            def store(t, i):
                e = t * UN + i
                pool.wait_ge(s_ys, e + 1)
                pool.dma_start(ybuf.rearrange("(e c) n -> e c n", c=CAP)[bass.ds(e, 1)].rearrange("a c n -> (a c) n"), ys[i][:]).then_inc(s_y[i], 16)

            for i in range(UN):
                load_down(i, i)
            with pool.Fori(0, TURNS - 1) as t:
                for i in range(UN):
                    store(t, i)
                    load_down(t * UN + UN + i, i)
            for i in range(UN):
                store(TURNS - 1, i)
            for s in s_y:
                pool.wait_ge(s, 16 * TURNS)

        @block.tensor
        def _(pe):
            def flip(first, t, i):
                e = t * UN + i
                pe.wait_ge(s_be[i], 16 * t + 16)
                if not (first and i < 2):
                    pe.wait_ge(s_bt, e - 1)
                for kd in range(KD):
                    ins = pe.transpose(tb[i % 2][:, kd], be[i][:, kd * P:(kd + 1) * P], ident[:])
                ins.then_inc(s_tb, 1)

            def hidden(first, t, i):
                e = t * UN + i
                pe.wait_ge(s_bt, e + 1)
                if not (first and i < 2):
                    pe.wait_ge(s_hh, e - 1)
                for kd in range(KD):
                    w = w_gu[:, bass.ds(e, 1), kd].rearrange("p a n -> p (a n)")
                    ins = pe.matmul(gb[i % 2][:, 0:2 * FE], bT[i][:, kd], w, start=kd == 0, stop=kd == KD - 1)
                ins.then_inc(s_gb, 1)

            def output(first, t, i):
                e = t * UN + i
                pe.wait_ge(s_hh, e + 1)
                if not (first and i < 2):
                    pe.wait_ge(s_hht, e - 1)
                    pe.wait_ge(s_ys, e - 1)
                for k in range(2):
                    ins = pe.transpose(ht[i % 2][0:FH, k], hh[i][:, k * FH:(k + 1) * FH], ident[:])
                ins.then_inc(s_ht, 1)
                pe.wait_ge(s_hht, e + 1)
                pe.wait_ge(s_wd[i], 16 * t + 16)
                for k in range(2):
                    ins = pe.matmul(yb[i % 2][:, 0:D], hhT[i][:, k], wd[i][:, k], start=k == 0, stop=k == 1)
                ins.then_inc(s_yb, 1)

            def turn(first, t, last):
                hidden(first, t, 0)
                for i in range(1, UN):
                    hidden(first, t, i)
                    if i == UN - 1 and not last:
                        for k in range(2):
                            flip(False, t + 1, k)
                    output(first, t, i - 1)
                if not last:
                    for k in range(2, UN):
                        flip(False, t + 1, k)
                output(first, t, UN - 1)

            for s in gu_loaded:
                pe.wait_ge(s, 16)
            for i in range(UN):
                flip(True, 0, i)
            turn(True, 0, False)
            with pe.Fori(1, TURNS - 1) as t:
                turn(False, t, False)
            turn(False, TURNS - 1, True)

        @block.vector
        def _(dve):
            def rows_out(first, t, i):
                e = t * UN + i
                dve.wait_ge(s_tb, e + 1)
                if not first:
                    dve.wait_ge(s_gb, e - UN + 1)
                dve.tensor_copy(bT[i][:], tb[i % 2][:, 0:KD]).then_inc(s_bt, 1)

            def hidden(first, t, i):
                e = t * UN + i
                dve.wait_ge(s_sg, e + 1)
                if not first:
                    dve.wait_ge(s_ht, e - UN + 1)
                dve.tensor_tensor(hh[i][:], sg[i][:], gb[i % 2][:, FE:2 * FE], ALU.mult).then_inc(s_hh, 1)

            def y_out(first, t, i):
                e = t * UN + i
                dve.wait_ge(s_yb, e + 1)
                if not first:
                    dve.wait_ge(s_y[i], 16 * t)
                dve.tensor_copy(ys[i][:], yb[i % 2][:, 0:D]).then_inc(s_ys, 1)

            def turn(first, t, last):
                hidden(first, t, 0)
                for i in range(1, UN):
                    hidden(first, t, i)
                    if i == UN - 1 and not last:
                        for k in range(2):
                            rows_out(False, t + 1, k)
                    y_out(first, t, i - 1)
                if not last:
                    for k in range(2, UN):
                        rows_out(False, t + 1, k)
                y_out(first, t, UN - 1)

            for i in range(UN):
                rows_out(True, 0, i)
            turn(True, 0, False)
            with dve.Fori(1, TURNS - 1) as t:
                turn(False, t, False)
            turn(False, TURNS - 1, True)

        @block.scalar
        def _(act):
            def silu(first, t, i):
                e = t * UN + i
                act.wait_ge(s_gb, e + 1)
                if not first:
                    act.wait_ge(s_hh, e - UN + 1)
                act.activation(sg[i][:], gb[i % 2][:, 0:FE], ACT.Silu).then_inc(s_sg, 1)

            def hT_out(first, t, i):
                e = t * UN + i
                act.wait_ge(s_ht, e + 1)
                if not first:
                    act.wait_ge(s_yb, e - UN + 1)
                act.activation(hhT[i][:], ht[i % 2][0:FH, 0:2], ACT.Copy).then_inc(s_hht, 1)

            def turn(first, t):
                silu(first, t, 0)
                for i in range(1, UN):
                    silu(first, t, i)
                    hT_out(first, t, i - 1)
                hT_out(first, t, UN - 1)

            turn(True, 0)
            with act.Fori(1, TURNS) as t:
                turn(False, t)


def combine(nc, a, x, rows, wv, ybuf, out):
    NB = 8
    yg = [a.sb(f"yg{i}", [P, D]) for i in range(NB)]
    s_g = [a.sem(f"gathered{i}") for i in range(NB)]
    s_sum, s_out = a.sem("expert_added"), a.sem("out_written")
    with nc.Block() as block:
        @block.gpsimd
        def _(pool):
            for n in range(NT * TOPK):
                if n >= NB:
                    pool.wait_ge(s_sum, n - NB + 1)
                pool.indirect_dma_start(out=yg[n % NB][:], out_offset=None, in_=ybuf,
                                        in_offset=bass.IndirectOffsetOnAxis(ap=rows[:, n:n + 1], axis=0)).then_inc(s_g[n % NB], 16)

        @block.vector
        def _(dve):
            for n in range(NT * TOPK):
                t = n // TOPK
                dve.wait_ge(s_g[n % NB], 16 * (n // NB + 1))
                if n % TOPK:
                    dve.wait_ge(s_sum, n)
                dve.scalar_tensor_tensor(x[:, t], yg[n % NB][:], wv[:, n:n + 1], x[:, t], ALU.mult, ALU.add).then_inc(s_sum, 1)

        @block.sync
        def _(sp):
            o = out.rearrange("a (t p) n -> p (a t) n", p=P)
            for t in range(NT):
                sp.wait_ge(s_sum, TOPK * (t + 1))
                sp.dma_start(o[:, t], x[:, t]).then_inc(s_out, 16)
            sp.wait_ge(s_out, 16 * NT)


CONSTS = ["ident", "upto", "after", "before", "levels"]


def load_constants(nc, a, d, x, buf, s_zeroed):
    consts = {
        "ident": a.sb("ident", [P, P]),
        "upto": a.sb("upto", [P, P]),
        "after": a.sb("after", [P, P]),
        "before": a.sb("before", [P, P]),
        "levels": a.sb("levels", [P, LEVELS, P]),
    }
    s_x, s_zero = a.sem("x_loaded"), a.sem("zero_row_ready")
    zeros = a.sb("zeros", [P, D])
    s_const = [a.sem(f"const_{n}_loaded") for n in CONSTS]
    with nc.Block() as block:
        @block.sync
        def _(sp):
            sp.dma_start(x[:], d["x"].rearrange("(t p) n -> p t n", p=P)).then_inc(s_x, 16)
            for n, s in zip(CONSTS, s_const):
                sp.dma_start(consts[n][:], d[n]).then_inc(s, 16)
            sp.wait_ge(s_zero, 1)
            sp.dma_start(buf.rearrange("(p r) n -> p r n", p=P),
                         zeros[:].unsqueeze(1).to_broadcast([P, E * CAP // P, D])).then_inc(s_zeroed, 16)
            for s in s_const:
                sp.wait_ge(s, 16)
            sp.wait_ge(s_x, 16)

        @block.gpsimd
        def _(pool):
            pool.memset(zeros[:], 0.0).then_inc(s_zero, 1)

    return consts


def program(nc, d, out, stages=4):
    with ExitStack() as stack:
        a = Alloc(nc, stack, "main")
        Alloc.psum_banks = stack.enter_context(nc.psum_tensor("psum_banks", [P, 8, 512], F32))
        x = a.sb("x", [P, NT, D])
        hT = a.sb("hT", [P, KD, T])
        buf = nc.dram_tensor("expert_rows", (E * CAP, D), F32, kind="Internal").ap()
        ybuf = nc.dram_tensor("expert_out", (E * CAP, D), F32, kind="Internal").ap()
        s_zeroed = a.sem("expert_rows_zeroed")
        consts = load_constants(nc, a, d, x, buf, s_zeroed)
        gated_delta(nc, x, hT, consts, d)
        w_gu = a.sb("w_gu", [P, E, KD, 2 * FE])
        gu_loaded = [a.sem(f"w_gu{i}_loaded") for i in range(4)]
        with nc.Block() as block:
            @block.sync
            def _(sp):
                for i, s in enumerate(gu_loaded):
                    n = E // len(gu_loaded)
                    sp.dma_start(w_gu[:, i * n:(i + 1) * n], d["w_gu"][:, i * n:(i + 1) * n]).then_inc(s, 16)
        if stages >= 2:
            perceptron(nc, x, hT, consts, d)
        if stages >= 3:
            attention(nc, x, hT, consts, d)
        if stages >= 4:
            mixture(nc, x, hT, consts, d, w_gu, gu_loaded, buf, ybuf, s_zeroed, out)
            return
        s_out = a.sem("out_written")
        with nc.Block() as block:
            @block.sync
            def _(sp):
                sp.dma_start(out.rearrange("a (t p) n -> p (a t) n", p=P), x[:]).then_inc(s_out, 16)
                sp.wait_ge(s_out, 16)


def shape_constants():
    import numpy as np
    j, i = np.indices((P, P))
    masks = []
    for lv in range(1, LEVELS + 1):
        s = 1 << (lv - 1)
        masks.append((j // (2 * s) == i // (2 * s)) & (j % (2 * s) < s) & (i % (2 * s) >= s))
    f = np.float32
    return {"ident": np.eye(P, dtype=f), "upto": (j <= i).astype(f), "after": (j > i).astype(f), "before": (j < i).astype(f),
            "levels": np.stack(masks, 1).astype(f)}


def layouts(inp):
    import numpy as np

    def rows(w):
        w = np.asarray(w)
        return w.reshape(w.shape[0] // P, P, -1).transpose(1, 0, 2)

    out = {"x": np.asarray(inp["L0_attn_hidden_states"]).reshape(T, D)}
    w = rows(inp["L0_attn_w_qkv"])
    q, k, v = w[..., :2048], w[..., 2048:4096], w[..., 4096:]
    q, k = (m.reshape(P, KD, HK, P) for m in (q, k))
    v = v.reshape(P, KD, HK, 2 * P)
    out["w_in"] = np.concatenate([k, q, v], -1).transpose(2, 0, 1, 3)
    out["w_z"] = rows(inp["L0_attn_w_z"]).reshape(P, KD, HK, 2 * P).transpose(2, 0, 1, 3)
    out["w_o"] = np.asarray(inp["L0_attn_w_out"]).reshape(HK, HD, P, D).transpose(0, 2, 1, 3)
    out["w_ba"] = np.concatenate([rows(inp["L0_attn_w_b"]), rows(inp["L0_attn_w_a"])], -1)
    cw = np.asarray(inp["L0_attn_conv_w"]).reshape(64, P, 4)
    blocks = [[HK + hk, hk, 2 * HK + 2 * hk, 2 * HK + 2 * hk + 1] for hk in range(HK)]
    out["conv_w"] = cw[np.array(blocks)].transpose(2, 0, 1, 3)
    out["dt_bias"] = np.asarray(inp["L0_attn_dt_bias"]).reshape(1, 32)
    out["A_log"] = np.asarray(inp["L0_attn_A_log"]).reshape(1, 32)
    out["gamma"] = np.asarray(inp["L0_attn_norm_gamma"]).reshape(P, 1)

    get = lambda n: np.asarray(inp[n])
    out["mlp_w1"], out["mlp_w2"], out["mlp_w3"] = (rows(get(f"L0_ffn_W{i}").T) for i in (1, 2, 3))
    out["mlp_b12"] = np.stack([get(f"L0_ffn_b{i}").reshape(NF, P).T for i in (1, 2)], 1)
    out["mlp_b3"] = get("L0_ffn_b3").reshape(1, D)
    for n in "qkvo":
        out[f"attn_w{n}"] = rows(get(f"L1_attn_W{n}"))
    out["attn_bqk"] = np.stack([get(f"L1_attn_b{n}").reshape(KD, P).T for n in "qk"], 1)
    out["attn_bv"], out["attn_bo"] = get("L1_attn_bv").reshape(1, D), get("L1_attn_bo").reshape(1, D)
    out["moe_w_norm"] = get("L1_ffn_w_norm").reshape(1, D)
    out["moe_w_r"] = np.concatenate([rows(get("L1_ffn_w_router")), rows(get("L1_ffn_w_shared_gate"))], -1)
    out["moe_iota"] = np.arange(E, dtype=np.float32).reshape(1, E)
    gu = np.concatenate([get("L1_ffn_w_gate"), get("L1_ffn_w_up")], -1)
    out["w_gu"] = gu.reshape(E, KD, P, 2 * FE).transpose(2, 0, 1, 3)
    out["w_down"] = get("L1_ffn_w_down").reshape(E, 2, FH, D).transpose(0, 2, 1, 3)
    out["sw_gu"] = np.stack([rows(get("L1_ffn_sw_gate")), rows(get("L1_ffn_sw_up"))], 1)
    down = get("L1_ffn_sw_down")
    tail = np.zeros((len(SH) * P, D), down.dtype)
    tail[:FS] = down
    out["sw_down"] = rows(tail)
    out.update(shape_constants())
    return {n: np.ascontiguousarray(v) for n, v in out.items()}


def kernel(**inputs):
    import concourse.bacc as _bacc
    from concourse import mybir as _mybir
    from concourse.bass_utils import run_bass_kernel_spmd as _run

    nc = _bacc.Bacc("TRN2", target_bir_lowering=False, num_devices=1)
    arrays = {f"in_{n}": v for n, v in layouts(inputs).items()}
    d = {n[3:]: nc.dram_tensor(n, v.shape, _mybir.dt.from_np(v.dtype), kind="ExternalInput").ap() for n, v in arrays.items()}
    out = nc.dram_tensor("out", (1, T, D), F32, kind="ExternalOutput").ap()
    program(nc, d, out)
    return _run(nc, [arrays], core_ids=[0]).results[0]["out"]
```

```python
from contextlib import ExitStack

import concourse.bass as bass
from concourse import mybir

ALU = mybir.AluOpType
ACT = mybir.ActivationFunctionType
AX_X = mybir.AxisListType.X
F32 = mybir.dt.float32
U32 = mybir.dt.uint32

P = 128
T = 1024
D = 256
KD = D // P
NT = T // P
EPS_LN = 1e-5
EPS = 1e-6


class Alloc:

    psum_banks = None

    def __init__(self, nc, stack, stage, outer=None):
        self.nc, self.stack, self.stage, self.outer = nc, stack, stage, outer
        self.next_bank = 0
        self.sems = []

    def sb(self, name, shape, dtype=F32):
        return self.stack.enter_context(self.nc.sbuf_tensor(f"{self.stage}_{name}", shape, dtype))

    def psum(self, shape):
        first = self.next_bank
        self.next_bank += -(-int(shape[1] * (shape[2] if len(shape) > 2 else 1)) // 512)
        ap = self.psum_banks[:, first:self.next_bank].rearrange("p a b -> p (a b)")
        return ap.rearrange("p (a b) -> p a b", b=shape[2]) if len(shape) > 2 else ap

    def sem(self, name, stage=None):
        stage = stage or self.stage
        if self.outer:
            return self.outer.sem(name, stage)
        self.sems.append(self.stack.enter_context(self.nc.semaphore(f"{stage}_{name}")))
        return self.sems[-1]

    def clear_sems(self):
        with self.nc.Block() as block:
            @block.gpsimd
            def _(pool):
                for s in self.sems:
                    pool.sem_clear(s)


def bc_mid(ap, n):
    p, m = ap.shape
    return ap.unsqueeze(1).to_broadcast([p, n, m])


def bc_last(ap, n):
    p, m = ap.shape
    return ap.unsqueeze(2).to_broadcast([p, m, n])


def layernorm_transposed(nc, a, x, hT, ident, eps, prefetch=None, rms_weight=None, weight_ready=None, xn=None):
    rms = rms_weight is not None
    stats = a.sb("ln_stats", [P, NT, 6])
    mv = a.sb("ln_mv", [P, NT, 2])
    spread = a.sb("ln_spread", [P, NT])
    root = a.sb("ln_root", [P, NT])
    rstd = a.sb("ln_rstd", [P, NT])
    ln = a.sb("ln_out", [P, NT, D])
    rstd2 = a.sb("ln_rstd2", [P, NT]) if rms else None
    xn = xn if rms else ln
    flip = [a.psum([P, 4, P]) for i in range(4)]
    s_stats, s_mv, s_spread = a.sem("ln_stats_ready"), a.sem("ln_mv_ready"), a.sem("ln_spread_ready")
    s_root, s_rstd = a.sem("ln_root_ready"), a.sem("ln_rstd_ready")
    s_ln, s_x = a.sem("ln_ready"), a.sem("x_plus_ln")
    s_xn, s_flip, s_ht = a.sem("ln_xn_ready"), a.sem("ln_flipped"), a.sem("ln_ht_written")
    with nc.Block() as block:
        @block.sync
        def _(sp):
            if prefetch:
                prefetch(sp)

        @block.vector
        def _(dve):
            for t in range(NT):
                dve.bn_stats(stats[:, t], x[:, t]).then_inc(s_stats, 1)
            for t in range(NT):
                dve.wait_ge(s_stats, t + 1)
                dve.bn_aggr(mv[:, t], stats[:, t]).then_inc(s_mv, 1)
            dve.wait_ge(s_mv, NT)
            dve.tensor_scalar(spread[:], mv[:, :, 1], eps, None, ALU.add).then_inc(s_spread, 1)
            dve.wait_ge(s_root, 1)
            dve.reciprocal(rstd[:], root[:]).then_inc(s_rstd, 1)
            dve.wait_ge(s_rstd, 1)
            for t in range(NT):
                dve.tensor_scalar(ln[:, t], x[:, t], mv[:, t, 0:1], rstd[:, t:t + 1], ALU.subtract, ALU.mult).then_inc(s_ln, 1)
            if rms:
                dve.tensor_tensor(rstd2[:], rstd[:], rstd[:], ALU.mult).then_inc(s_rstd, 1)
                dve.wait_ge(s_rstd, 2)
                dve.tensor_tensor(rstd2[:], rstd2[:], mv[:, :, 1], ALU.mult).then_inc(s_rstd, 1)
                dve.wait_ge(s_rstd, 3)
                dve.tensor_scalar(spread[:], rstd2[:], EPS, None, ALU.add).then_inc(s_spread, 1)
                dve.wait_ge(s_ln, NT)
                dve.tensor_tensor(x[:], x[:], ln[:], ALU.add).then_inc(s_x, 1)
                dve.wait_ge(s_root, 2)
                dve.reciprocal(rstd2[:], root[:]).then_inc(s_rstd, 1)
                dve.wait_ge(s_rstd, 4)
                dve.wait_ge(weight_ready, 16)
                for t in range(NT):
                    dve.scalar_tensor_tensor(xn[:, t], ln[:, t], rstd2[:, t:t + 1], rms_weight[:], ALU.mult, ALU.mult).then_inc(s_xn, 1)
            for u in range(4):
                dve.wait_ge(s_flip, u + 1)
                kd, half = u // 2, u % 2
                out = hT[:, kd, half * 512:(half + 1) * 512]
                src = flip[u][:].rearrange("p a b -> p (a b)")
                dve.tensor_copy(out, src).then_inc(s_ht, 1)
            dve.wait_ge(s_ht, 4)
            if rms:
                dve.wait_ge(s_x, 1)

        @block.scalar
        def _(act):
            act.wait_ge(s_spread, 1)
            act.activation(root[:], spread[:], ACT.Sqrt).then_inc(s_root, 1)
            if rms:
                act.wait_ge(s_spread, 2)
                act.activation(root[:], spread[:], ACT.Sqrt).then_inc(s_root, 1)

        @block.tensor
        def _(pe):
            for u in range(4):
                kd, half = u // 2, u % 2
                for j in range(4):
                    t = half * 4 + j
                    pe.wait_ge(s_xn if rms else s_ln, t + 1)
                    ins = pe.transpose(flip[u][:, j], xn[:, t, kd * P:(kd + 1) * P], ident[:])
                ins.then_inc(s_flip, 1)


HK = 16
HD = 2
C = NT
IT = C * HD
LEVELS = 7
HALF = P // 2
G_, NGAM, GAM, TAIL, GAMC, BETA = range(6)
NQ = 6


class Uses:

    def __init__(self, sem, first, mid, last, before=0, second=None, final=()):
        self.lists = {"first": first, "second": mid if second is None else second, "mid": mid, "last": last, "final": list(final)}
        self.sem, self.before = sem, before

    def base(self, kind, h):
        value = self.before
        if kind != "first":
            value += len(self.lists["first"])
        if kind in ("mid", "last", "final"):
            value += len(self.lists["second"])
        if kind == "mid":
            return value + (h - 2) * len(self.lists["mid"])
        if kind in ("last", "final"):
            value += (HK - 2) * len(self.lists["mid"])
        if kind == "final":
            value += len(self.lists["last"])
        return value

    def done(self, kind, h, name):
        return self.base(kind, h) + self.lists[kind].index(name) + 1

    def ahead(self, kind, h, name):
        i = self.lists[kind].index(name)
        if kind == "first" and i + self.before == 0:
            return None
        return self.base(kind, h) + i


def works(kind):
    return kind in ("first", "second", "mid"), kind in ("second", "mid", "last"), kind in ("mid", "last", "final")


def head_plan(kind):
    invert, scan, finish = works(kind)
    plan = [("decay_0", 1), ("decay_1", 3)] if invert else []
    plan += [("z0", 0), ("z1", 2)] if scan else []
    plan += [("kk_0", 1), ("kk_1", 3), ("norm_k", 0), ("k0", 2), ("k1", 0)] if invert else []
    plan += [("z2", 2), ("z3", 0)] if scan else []
    plan += [("norm_q", 2), ("v0", 0), ("v1", 2)] if invert else []
    plan += [("flip0", 1), ("flip1", 3)] if finish else []
    plan += [("v2", 0), ("v3", 2)] if invert else []
    plan += [("flip2", 1), ("flip3", 3), ("out0", 0), ("out1", 2), ("out2", 1), ("out3", 3)] if finish else []
    return plan


def slots_of(sg):
    slots = ["level1"]
    for lv in range(2, LEVELS + 1):
        slots += [f"below{lv}", f"merge{lv}"]
        if sg == 0 and lv == 4:
            slots += ["decay"]
        if sg == 0 and lv == 5:
            slots += ["kk"]
    return slots + ["attn"]


def bank_plan(kind):
    banks = [[], [], [], []]
    for name, b in head_plan(kind):
        banks[b].append(name)
    if works(kind)[0]:
        for sg in range(2):
            for slot in slots_of(sg):
                for g in range(2):
                    even, odd = banks[2 * g], banks[2 * g + 1]
                    if slot == "level1" or slot == "attn" or slot.startswith("below"):
                        even.append(f"{slot}_{sg}")
                        if slot.startswith("below") and slot != "below2":
                            odd.append(f"U{int(slot[5:]) - 1}_{sg}")
                    elif slot == "decay":
                        even.append("sg1_decay")
                    elif slot == "kk":
                        odd.append("sg1_kk")
                    else:
                        lv = int(slot[5:])
                        if lv < LEVELS:
                            even.append(f"T{lv}_{sg}")
                        else:
                            odd.append(f"U{lv}_{sg}")
    return banks


SLOTS = [slots_of(0), slots_of(1)]
SCAN_AT = [{k + 1: k for k in range(12)}, {k: k for k in range(12)}]
PROJ_AT = [{0: 0, 3: 1, 6: 2, 9: 3, 12: 4}, {1: 5, 4: 6, 7: 7}]


def gated_delta(nc, x, hT, consts, d):
    with ExitStack() as stack:
        a = Alloc(nc, stack, "gdn")
        with ExitStack() as inner:
            layernorm_transposed(nc, Alloc(nc, inner, "norm1", a), x, hT, consts["ident"], EPS_LN)
        coef = a.sb("coef", [P, NQ, HK, IT])
        conv_w = a.sb("conv_w", [P, HK, 4, 4])
        gamma = a.sb("gamma", [P, 1])
        powers = a.sb("powers", [P, 2 * C])
        minus_half = a.sb("minus_half", [P, IT])
        S = a.sb("S", [P, HD, P])
        raw = [a.sb(f"raw{i}", [P, 3 + T]) for i in range(2)]

        gate_coefficients(nc, a, hT, consts, d, coef, conv_w, gamma, powers, minus_half, raw)
        with ExitStack() as inner:
            heads(nc, Alloc(nc, inner, "heads", a), x, hT, consts, d, coef, conv_w, gamma, powers, minus_half, S, raw)
        a.clear_sems()


def gate_coefficients(nc, outer, hT, consts, d, coef, conv_w, gamma, powers, minus_half, raw):
    with ExitStack() as stack:
        a = Alloc(nc, stack, "gate", outer)
        w_ba = a.sb("w_ba", [P, KD, 64])
        dt_b = a.sb("dt_b", [P, 32])
        a_log = a.sb("a_log", [P, 32])
        ones = a.sb("ones", [P, P])
        neg_rate = a.sb("neg_rate", [P, 32])
        ba = a.sb("ba", [P, C, 64])
        e_b = a.sb("e_b", [P, C, 32])
        y = a.sb("y", [P, C, 32])
        ay = a.sb("ay", [P, C, 32])
        l1 = a.sb("l1", [P, C, 32])
        sp = a.sb("sp", [P, C, 32])
        g = a.sb("g", [P, C, 32])
        tot = a.sb("tot", [P, HK * IT])
        diff = a.sb("diff", [P, HK * IT])
        acc = a.psum([P, C, 64])
        cum = a.psum([P, 512])
        total = a.psum([P, 512])
        s_in = [a.sem(f"in{i}") for i in range(5)]
        s_mm, s_v, s_a, s_cum = a.sem("mm"), a.sem("vector_step"), a.sem("scalar_step"), a.sem("cum")

        def by_head(ap):
            return ap.rearrange("p c (h e) -> p h c e", e=HD)

        def q(k):
            return coef[:, k].rearrange("p h i -> p (h i)")

        def q4(k):
            return coef[:, k].rearrange("p h (c e) -> p h c e", e=HD)

        with nc.Block() as block:
            @block.sync
            def _(sp_):
                sp_.dma_start(w_ba[:], d["w_ba"]).then_inc(s_in[0], 16)
                sp_.dma_start(dt_b[:], d["dt_bias"].to_broadcast([P, 32])).then_inc(s_in[1], 16)
                sp_.dma_start(a_log[:], d["A_log"].to_broadcast([P, 32])).then_inc(s_in[2], 16)
                sp_.dma_start(conv_w[:], d["conv_w"]).then_inc(s_in[3], 16)
                sp_.dma_start(gamma[:], d["gamma"]).then_inc(s_in[4], 16)
                sp_.wait_ge(s_in[3], 16)
                sp_.wait_ge(s_in[4], 16)

            @block.gpsimd
            def _(pool):
                pool.memset(powers[:, 0:C], 0.5)
                pool.memset(powers[:, C:2 * C], -0.5)
                pool.memset(minus_half[:], -0.5)
                for r in raw:
                    pool.memset(r[:, 0:3], 0.0)

            @block.tensor
            def _(pe):
                pe.wait_ge(s_in[0], 16)
                for c in range(C):
                    for kd in range(KD):
                        ins = pe.matmul(acc[:, c], hT[:, kd, c * P:(c + 1) * P], w_ba[:, kd],
                                        start=kd == 0, stop=kd == KD - 1)
                ins.then_inc(s_mm, 1)
                pe.wait_ge(s_v, 10)
                pe.matmul(cum[:, 0:HK * IT], consts["upto"][:], q(G_), start=True, stop=True).then_inc(s_cum, 1)
                pe.matmul(total[:, 0:HK * IT], ones[:], q(G_), start=True, stop=True).then_inc(s_cum, 1)

            @block.scalar
            def _(act):
                act.wait_ge(s_in[2], 16)
                act.activation(neg_rate[:], a_log[:], ACT.Exp).then_inc(s_a, 1)
                act.wait_ge(s_v, 2)
                act.activation(e_b[:], ba[:, :, 0:32], ACT.Exp, scale=-1.0).then_inc(s_a, 1)
                act.wait_ge(s_v, 4)
                act.activation(l1[:], ay[:], ACT.Exp, scale=-1.0).then_inc(s_a, 1)
                act.wait_ge(s_v, 7)
                act.activation(ay[:], l1[:], ACT.Ln).then_inc(s_a, 1)
                act.wait_ge(s_v, 11)
                act.wait_ge(s_cum, 2)
                act.activation(q(GAM), diff[:], ACT.Exp).then_inc(s_a, 1)
                act.activation(q(GAMC), tot[:], ACT.Exp).then_inc(s_a, 1)
                act.wait_ge(s_v, 13)
                act.activation(q(TAIL), tot[:], ACT.Exp).then_inc(s_a, 1)

            @block.vector
            def _(dve):
                dve.memset(ones[:], 1.0).then_inc(s_v, 1)
                dve.wait_ge(s_mm, 1)
                dve.tensor_copy(ba[:], acc[:]).then_inc(s_v, 1)
                dve.wait_ge(s_in[1], 16)
                dve.wait_ge(s_v, 2)
                dve.tensor_tensor(y[:], ba[:, :, 32:64], bc_mid(dt_b[:], C), ALU.add).then_inc(s_v, 1)
                dve.wait_ge(s_v, 3)
                dve.scalar_tensor_tensor(ay[:], y[:], -1.0, y[:], ALU.mult, ALU.max).then_inc(s_v, 1)
                dve.wait_ge(s_a, 2)
                dve.tensor_scalar(e_b[:], e_b[:], 1.0, None, ALU.add).then_inc(s_v, 1)
                dve.wait_ge(s_v, 5)
                dve.reciprocal(q4(BETA), by_head(e_b[:])).then_inc(s_v, 1)
                dve.wait_ge(s_a, 3)
                dve.tensor_scalar(l1[:], l1[:], 1.0, None, ALU.add).then_inc(s_v, 1)
                dve.wait_ge(s_a, 4)
                dve.scalar_tensor_tensor(sp[:], y[:], 0.0, ay[:], ALU.max, ALU.add).then_inc(s_v, 1)
                dve.wait_ge(s_v, 8)
                dve.scalar_tensor_tensor(g[:], sp[:], -1.0, bc_mid(neg_rate[:], C), ALU.mult, ALU.mult).then_inc(s_v, 1)
                dve.wait_ge(s_v, 9)
                dve.tensor_copy(q4(G_), by_head(g[:])).then_inc(s_v, 1)
                dve.wait_ge(s_cum, 2)
                dve.tensor_copy(tot[:], total[:, 0:HK * IT])
                dve.tensor_copy(diff[:], cum[:, 0:HK * IT]).then_inc(s_v, 1)
                dve.wait_ge(s_a, 6)
                dve.tensor_scalar(q(NGAM), q(GAM), -1.0, None, ALU.mult).then_inc(s_v, 1)
                dve.wait_ge(s_v, 11)
                dve.tensor_tensor(tot[:], tot[:], diff[:], ALU.subtract).then_inc(s_v, 1)
                dve.wait_ge(s_a, 7)


def heads(nc, a, x, hT, consts, d, coef, conv_w, gamma, powers, minus_half, S, raw):
    ident, upto, after, levels = consts["ident"], consts["upto"], consts["after"], consts["levels"]
    dm_mask, before_ = upto, consts["before"]

    w_in = a.sb("w_in", [P, KD, 4 * P])
    w_z = a.sb("w_z", [P, KD, HD * P])
    w_o = a.sb("w_o", [P, HD, D])
    y = [a.sb(f"y{j}", [P, T]) for j in range(4)]
    kT = [a.sb(f"kT{i}", [P, T]) for i in range(2)]
    qT = [a.sb(f"qT{i}", [P, T]) for i in range(2)]
    k_tok = [a.sb(f"k_tok{i}", [P, C, P]) for i in range(2)]
    v_s = [a.sb(f"v_s{i}", [P, IT, P]) for i in range(2)]
    cf = [a.sb(f"cf{i}", [P, NQ, IT]) for i in range(2)]
    cc = [a.sb(f"cc{i}", [P, IT]) for i in range(2)]
    norms = a.sb("norms", [P, 2 * C])
    inv = a.sb("inv", [P, C])
    roots = [a.sb(f"roots{i}", [P, 2 * C]) for i in range(2)]
    ones_col = a.sb("ones_col", [P, 1])
    z = a.sb("z", [P, C, HD * P])
    gU = [a.sb(f"gU{g}", [P, 4, P]) for g in range(2)]
    Dx = [a.sb(f"Dx{g}", [P, 4, P]) for g in range(2)]
    Ds = [a.sb(f"Ds{g}", [P, 4, P]) for g in range(2)]
    Dm = [a.sb(f"Dm{g}", [P, 4, P]) for g in range(2)]
    G = [[a.sb(f"G{sg}_{g}", [P, 4, P]) for g in range(2)] for sg in range(2)]
    Gl = [[a.sb(f"Gl{g}_{i}", [P, 4, P]) for i in range(3)] for g in range(2)]
    Tn = [a.sb(f"Tn{g}", [P, 4, P]) for g in range(2)]
    Ut = [a.sb(f"Ut{g}", [P, 4, P]) for g in range(2)]
    W = [a.sb(f"W{g}", [P, 4, P]) for g in range(2)]
    Uf = a.sb("Uf", [P, IT, P])
    At = a.sb("At", [P, IT, P])
    X = a.sb("X", [P, HD, P])
    O1 = a.sb("O1", [P, HD, P])
    Dl = a.sb("Dl", [P, HD, P])
    Dt = a.sb("Dt", [P, HD, P])
    O2 = a.sb("O2", [P, HD, P])
    og = a.sb("og", [P, IT, P])
    junk = a.sb("junk", [P, P])
    ms = a.sb("ms", [P, IT])
    rqs = a.sb("rqs", [P, C])
    rq2 = a.sb("rq2", [P, C])
    var = a.sb("var", [P, IT])
    rs = a.sb("rs", [P, IT])
    fac = a.sb("fac", [P, IT])
    ogT = a.sb("ogT", [P, IT, P])

    bank = [a.psum([P, 4, P]) for i in range(4)]
    bank_a = a.psum([P, 4, P])
    bank_b = a.psum([P, 4, P])
    bank_c = a.psum([P, 4, P])
    bank_p = a.psum([P, 512])

    plans = {kind: bank_plan(kind) for kind in ("first", "second", "mid", "last", "final")}

    def per_bank(sem, b):
        return Uses(a.sem(sem), *[plans[k][b] for k in ("first", "mid", "last")], second=plans["second"][b], final=plans["final"][b])

    full = [per_bank(f"bank{b}_full", b) for b in range(4)]
    free = [per_bank(f"bank{b}_free", b) for b in range(4)]

    def per_scan(sem, *names):
        seq = [f"{n}{c}" for c in range(C) for n in names]
        return Uses(a.sem(sem), [], seq, seq)

    a_full, a_free = per_scan("scan_a_full", "ks", "su"), per_scan("scan_a_free", "ks", "su")
    b_full, b_free = per_scan("scan_b_full", "qs", "o"), per_scan("scan_b_free", "qs", "o")
    c_full, c_free = per_scan("scan_c_full", "tx"), per_scan("scan_c_free", "tx")
    dt_ready = per_scan("dt_ready", "dt")
    o_ready = per_scan("o_summed", "o")
    og_ready = per_scan("og_ready", "og")
    sq_ready = per_scan("squares_summed", "sq")
    s_zero = Uses(a.sem("state_zero"), ["zero"], ["zero"], [])
    proj = [f"p{u}" for u in range(8)]
    p_full = Uses(a.sem("proj_full"), proj, proj, [], before=8)
    p_free = Uses(a.sem("proj_free"), proj, proj, [], before=8)
    taps = [f"tap{j}_{t}" for j in range(4) for t in range(4)]
    conv_done = Uses(a.sem("conv_tap_done"), taps, taps, [], before=16)
    w_in_ready = Uses(a.sem("w_in_loaded"), ["w"], ["w"], [], before=1)
    w_z_ready = Uses(a.sem("w_z_loaded"), [], ["w"], ["w"])
    w_o_ready = Uses(a.sem("w_o_loaded"), [], ["w"], ["w"], second=[], final=["w"])
    acts = ["k", "q", "sk", "sq", "v0", "v1"]
    act_ready = Uses(a.sem("silu_ready"), acts, acts, [])
    one = ["it"]
    cf_ready = Uses(a.sem("coef_ready"), one, one, [])
    norm_q_ready = Uses(a.sem("norm_q_ready"), one, one, [])
    inv_ready = Uses(a.sem("inverse_norm_ready"), one, one, [])
    cc_ready = Uses(a.sem("cc_ready"), one, one, [])
    roots_ready = Uses(a.sem("roots_ready"), ["k", "q"], ["k", "q"], [])
    per_group = [f"{sg}_{g}" for sg in range(2) for g in range(2)]
    columns = ["this_0", "this_1", "next_0", "next_1"]
    gu_ready = Uses(a.sem("g_columns_ready"), columns, columns, [], before=2)
    ds_ready = Uses(a.sem("strict_decay_ready"), per_group, per_group, [])
    dm_ready = Uses(a.sem("decay_ready"), per_group, per_group, [])
    u1_ready = Uses(a.sem("U1_ready"), per_group, per_group, [])
    lv_names = [f"{lv}_{sg}_{g}" for sg in range(2) for lv in range(1, LEVELS + 1) for g in range(2)]
    gl_ready = Uses(a.sem("level_masked"), lv_names, lv_names, [])
    small = ["rqs", "rq2", "var0", "var"]
    tail_dve = Uses(a.sem("tail_vector"), [], ["fac", "ogn"] + small, ["fac", "ogn"] + small, second=small, final=["fac", "ogn"])
    tail_pow = Uses(a.sem("tail_pow"), [], one, one)
    s_const = a.sem("ones_ready")

    def flat(ap):
        return ap.rearrange("p a b -> p (a b)")

    def changed(ap, lv):
        return ap.rearrange("p (n k) -> p n k", k=1 << lv)[:, :, 0:1 << (lv - 1)]

    def per_item(ap, lv):
        return ap.rearrange("p a (n k) -> p a n k", k=1 << lv)[:, :, :, 0:1 << (lv - 1)]

    def level_buffer(g, lv):
        return Gl[g][2 if lv == 1 else lv % 2]

    def run_steps(eng, step):
        step("first", 0, 0)
        step("second", 1, 1)
        with eng.Fori(1, HK // 2 - 1) as t:
            step("mid", 2 * t, 0)
            step("mid", 2 * t + 1, 1)
        step("mid", HK - 2, 0)
        step("mid", HK - 1, 1)
        step("last", HK, 0)
        step("final", HK + 1, 1)

    def wait(eng, use, value, times=1):
        if value is None or (isinstance(value, int) and value <= 0):
            return
        eng.wait_ge(use.sem, value * times)

    with nc.Block() as block:
        @block.sync
        def _(sp):
            sp.dma_start(w_in[:], d["w_in"][0]).then_inc(w_in_ready.sem, 16)
            sp.wait_ge(p_full.sem, 8)
            sp.dma_start(w_in[:], d["w_in"][1]).then_inc(w_in_ready.sem, 16)
            sp.dma_start(w_z[:], d["w_z"][0]).then_inc(w_z_ready.sem, 16)
            sp.dma_start(w_o[:], d["w_o"][0]).then_inc(w_o_ready.sem, 16)

            def step(kind, h):
                if kind in ("second", "mid"):
                    sp.wait_ge(full[0].sem, full[0].done(kind, h, "z3"))
                    sp.dma_start(w_z[:], d["w_z"][bass.ds(h, 1)].rearrange("a p k n -> (a p) k n")).then_inc(w_z_ready.sem, 16)
                if kind in ("mid", "last"):
                    sp.wait_ge(full[3].sem, full[3].done(kind, h, "out3"))
                    sp.dma_start(w_o[:], d["w_o"][bass.ds(h - 1, 1)].rearrange("a p k n -> (a p) k n")).then_inc(w_o_ready.sem, 16)
                if kind in ("first", "second", "mid") and not (isinstance(h, int) and h >= HK - 2):
                    sp.wait_ge(p_full.sem, p_full.done(kind, h, "p7"))
                    sp.dma_start(w_in[:], d["w_in"][bass.ds(h + 2, 1)].rearrange("a p k n -> (a p) k n")).then_inc(w_in_ready.sem, 16)

            step("first", 0)
            step("second", 1)
            with sp.Fori(2, HK - 2) as h:
                step("mid", h)
            step("mid", HK - 2)
            step("mid", HK - 1)
            step("last", HK)

        @block.tensor
        def _(pe):
            def project(kind, h, u, src_ready, frees):
                j, half = u // 2, u % 2
                if u == 0:
                    pe.wait_ge(w_in_ready.sem, src_ready * 16)
                if frees is not None:
                    pe.wait_ge(p_free.sem, frees)
                for kd in range(KD):
                    ins = pe.matmul(bank_p[:], w_in[:, kd, j * P:(j + 1) * P],
                                    hT[:, kd, half * 512:(half + 1) * 512], start=kd == 0, stop=kd == KD - 1)
                ins.then_inc(p_full.sem, 1)

            def take(b, kind, h, name):
                wait(pe, free[b], free[b].ahead(kind, h, name))

            def step(kind, h, par):
                inv_, scan, finish = works(kind)
                no_proj = not inv_ or (isinstance(h, int) and h == HK - 1)
                sp_ = 1 - par

                def scan_quantum(i):
                    c, part = i // 3, i % 3
                    cs = slice(c * P, (c + 1) * P)
                    if part == 0:
                        wait(pe, a_free, a_free.ahead(kind, h, f"ks{c}"))
                        wait(pe, b_free, b_free.ahead(kind, h, f"qs{c}"))
                        if c == 0:
                            pe.wait_ge(s_zero.sem, h)
                        pe.matmul(flat(bank_a[:, 0:2]), kT[sp_][:, cs], flat(S[:]), start=True, stop=True).then_inc(a_full.sem, 1)
                        pe.matmul(flat(bank_b[:, 0:2]), qT[sp_][:, cs], flat(S[:]), start=True, stop=True).then_inc(b_full.sem, 1)
                    elif part == 1:
                        pe.wait_ge(a_free.sem, a_free.done(kind, h, f"ks{c}"))
                        wait(pe, c_free, c_free.ahead(kind, h, f"tx{c}"))
                        for e in range(HD):
                            ins = pe.matmul(bank_c[:, e], Uf[:, c * HD + e], X[:, e], start=True, stop=True)
                        ins.then_inc(c_full.sem, 1)
                    else:
                        pe.wait_ge(c_free.sem, c_free.done(kind, h, f"tx{c}"))
                        pe.wait_ge(b_free.sem, b_free.done(kind, h, f"qs{c}"))
                        for e in range(HD):
                            ins = pe.matmul(bank_b[:, e], At[:, c * HD + e], Dl[:, e], start=True, stop=True)
                        ins.then_inc(b_full.sem, 1)
                        pe.wait_ge(dt_ready.sem, dt_ready.done(kind, h, f"dt{c}"))
                        pe.matmul(flat(bank_a[:, 0:2]), k_tok[sp_][:, c], flat(Dt[:]), start=True, stop=True).then_inc(a_full.sem, 1)

                def open_step(name, b):
                    u = int(name[-1]) if name[-1].isdigit() else 0
                    if name == "z0":
                        pe.wait_ge(w_z_ready.sem, w_z_ready.done(kind, h, "w") * 16)
                    elif name.startswith("decay"):
                        pe.wait_ge(gu_ready.sem, gu_ready.base(kind, h) - 1 + u)
                    elif name in ("kk_0", "k0"):
                        pe.wait_ge(act_ready.sem, act_ready.done(kind, h, "k"))
                    elif name == "norm_k":
                        pe.wait_ge(act_ready.sem, act_ready.done(kind, h, "sk"))
                    elif name == "norm_q":
                        pe.wait_ge(act_ready.sem, act_ready.done(kind, h, "sq"))
                    elif name == "v0":
                        pe.wait_ge(act_ready.sem, act_ready.done(kind, h, "v1"))
                    elif name == "flip0":
                        pe.wait_ge(tail_dve.sem, tail_dve.done(kind, h, "ogn"))
                    elif name == "out0":
                        pe.wait_ge(w_o_ready.sem, w_o_ready.done(kind, h, "w") * 16)
                    elif name == "out2":
                        pe.wait_ge(free[3].sem, free[3].done(kind, h, "flip3"))
                    if name == "out0":
                        pe.wait_ge(free[3].sem, free[3].done(kind, h, "flip1"))
                    take(b, kind, h, name)
                    if name.startswith("z"):
                        for j in range(2):
                            c = 2 * u + j
                            for kd in range(KD):
                                ins = pe.matmul(flat(bank[b][:, 2 * j:2 * j + 2]), hT[:, kd, c * P:(c + 1) * P], w_z[:, kd],
                                                start=kd == 0, stop=kd == KD - 1)
                    elif name.startswith("decay"):
                        ins = pe.matmul(flat(bank[b][:]), after[:], flat(gU[u][:]), start=True, stop=True)
                    elif name.startswith("kk"):
                        for j in range(2):
                            kc = kT[par][:, (2 * u + j) * P:(2 * u + j + 1) * P]
                            ins = pe.matmul(bank[b][:, j], kc, kc, start=True, stop=True)
                    elif name.startswith("norm"):
                        w = int(name == "norm_q")
                        for c in range(C):
                            ins = pe.matmul(bank[b][:, 0, c:c + 1], y[w][:, c * P:(c + 1) * P], ones_col[:], start=True, stop=True)
                    elif name.startswith("k"):
                        for j in range(4):
                            ins = pe.transpose(bank[b][:, j], kT[par][:, (4 * u + j) * P:(4 * u + j + 1) * P], ident[:])
                    elif name.startswith("v"):
                        for j in range(4):
                            c, e = 2 * u + j // 2, j % 2
                            ins = pe.transpose(bank[b][:, j], y[2 + e][:, c * P:(c + 1) * P], ident[:])
                    elif name.startswith("flip"):
                        for i in range(4):
                            ins = pe.transpose(bank[b][:, i], og[:, 4 * u + i], ident[:])
                    else:
                        for j in range(2):
                            c = 2 * u + j
                            for e in range(HD):
                                ins = pe.matmul(flat(bank[b][:, 2 * j:2 * j + 2]), ogT[:, c * HD + e], w_o[:, e],
                                                start=e == 0, stop=e == HD - 1)
                    ins.then_inc(full[b].sem, 1)

                for name, b in head_plan(kind):
                    open_step(name, b)
                if inv_:
                    for sg in range(2):
                        for k, slot in enumerate(SLOTS[sg]):
                            for g in range(2):
                                b0, b1, gi = 2 * g, 2 * g + 1, f"{sg}_{g}"
                                if slot == "decay":
                                    pe.wait_ge(gu_ready.sem, gu_ready.done(kind, h, f"this_{g}"))
                                    take(b0, kind, h, "sg1_decay")
                                    pe.matmul(flat(bank[b0][:]), after[:], flat(gU[g][:]), start=True, stop=True).then_inc(full[b0].sem, 1)
                                elif slot == "kk":
                                    take(b1, kind, h, "sg1_kk")
                                    for j in range(2):
                                        c = 4 + 2 * g + j
                                        kc = kT[par][:, c * P:(c + 1) * P]
                                        ins = pe.matmul(bank[b1][:, j], kc, kc, start=True, stop=True)
                                    ins.then_inc(full[b1].sem, 1)
                                elif slot == "level1":
                                    pe.wait_ge(gl_ready.sem, gl_ready.done(kind, h, f"1_{gi}"))
                                    take(b0, kind, h, f"level1_{sg}")
                                    for i in range(4):
                                        ins = pe.transpose(bank[b0][:, i], level_buffer(g, 1)[:, i], ident[:])
                                    ins.then_inc(full[b0].sem, 1)
                                elif slot.startswith("below"):
                                    lv = int(slot[5:])
                                    pe.wait_ge(gl_ready.sem, gl_ready.done(kind, h, f"{lv}_{gi}"))
                                    take(b0, kind, h, f"below{lv}_{sg}")
                                    for i in range(4):
                                        ins = pe.matmul(changed(bank[b0][:, i], lv), level_buffer(g, lv)[:, i], changed(Tn[g][:, i], lv), start=True, stop=True)
                                    ins.then_inc(full[b0].sem, 1)
                                elif slot.startswith("merge"):
                                    lv = int(slot[5:])
                                    pe.wait_ge(free[b0].sem, free[b0].done(kind, h, f"below{lv}_{sg}"))
                                    if lv == 2:
                                        pe.wait_ge(u1_ready.sem, u1_ready.done(kind, h, gi))
                                    else:
                                        pe.wait_ge(free[b1].sem, free[b1].done(kind, h, f"U{lv - 1}_{sg}"))
                                    if lv < LEVELS:
                                        for i in range(4):
                                            ins = pe.matmul(changed(bank[b0][:, i], lv), Ut[g][:, i], changed(W[g][:, i], lv), start=True, stop=True)
                                        ins.then_inc(full[b0].sem, 1)
                                    else:
                                        for i in range(4):
                                            ins = pe.matmul(bank[b1][0:HALF, i, HALF:P], W[g][:, i, 0:HALF], Uf[:, 8 * sg + 4 * g + i, HALF:P],
                                                            start=True, stop=True)
                                        ins.then_inc(full[b1].sem, 1)
                                elif slot == "attn":
                                    take(b0, kind, h, f"attn_{sg}")
                                    for j in range(2):
                                        c = 4 * sg + 2 * g + j
                                        ins = pe.matmul(bank[b0][:, j], kT[par][:, c * P:(c + 1) * P], qT[par][:, c * P:(c + 1) * P],
                                                        start=True, stop=True)
                                    ins.then_inc(full[b0].sem, 1)
                            if slot.startswith("below") and slot != "below2":
                                for g in range(2):
                                    b1 = 2 * g + 1
                                    take(b1, kind, h, f"U{int(slot[5:]) - 1}_{sg}")
                                    for i in range(4):
                                        ins = pe.transpose(bank[b1][:, i], Tn[g][:, i], ident[:])
                                    ins.then_inc(full[b1].sem, 1)
                            if scan and k in SCAN_AT[sg]:
                                scan_quantum(12 * sg + SCAN_AT[sg][k])
                            if not no_proj and k in PROJ_AT[sg]:
                                u = PROJ_AT[sg][k]
                                project(kind, h, u, w_in_ready.done(kind, h, "w"), p_free.ahead(kind, h, f"p{u}"))
                elif scan:
                    for i in range(24):
                        scan_quantum(i)

            pe.wait_ge(s_const, 1)
            for u in range(8):
                project("pre", 0, u, 1, u if u else None)
            run_steps(pe, step)

        @block.scalar
        def _(act):
            def copy_raw(u, fulls, conv_two_before):
                j, half = u // 2, u % 2
                act.wait_ge(p_full.sem, fulls)
                if half == 0 and conv_two_before is not None:
                    act.wait_ge(conv_done.sem, conv_two_before)
                act.activation(raw[j % 2][:, 3 + half * 512:3 + (half + 1) * 512], bank_p[:], ACT.Copy).then_inc(p_free.sem, 1)

            def step(kind, h, par):
                inv_, scan, finish = works(kind)
                no_proj = not inv_ or (isinstance(h, int) and h == HK - 1)

                def raw_unit(u):
                    j = u // 2
                    base = conv_done.base(kind, h)
                    copy_raw(u, p_full.done(kind, h, f"p{u}"), base + 4 * (j - 1))

                def scan_quantum(i):
                    c, part = i // 3, i % 3
                    if part == 0:
                        act.wait_ge(b_full.sem, b_full.done(kind, h, f"qs{c}"))
                        for e in range(HD):
                            ins = act.activation(O1[:, e], bank_b[:, e], ACT.Copy, scale=cf[1 - par][:, GAM, c * HD + e:c * HD + e + 1])
                        ins.then_inc(b_free.sem, 1)
                    elif part == 1:
                        act.wait_ge(c_free.sem, c_free.done(kind, h, f"tx{c}"))
                        for e in range(HD):
                            ins = act.activation(Dt[:, e], Dl[:, e], ACT.Copy, scale=cf[1 - par][:, TAIL, c * HD + e:c * HD + e + 1])
                        ins.then_inc(dt_ready.sem, 1)
                    elif c > 0:
                        squares(c - 1)

                def squares(c):
                    act.wait_ge(og_ready.sem, og_ready.done(kind, h, f"og{c}"))
                    for e in range(HD):
                        wait(act, sq_ready, 2 * (sq_ready.ahead(kind, h, f"sq{c}")) + e)
                        act.activation(junk[:], og[:, c * HD + e], ACT.Square,
                                       accum_out=ms[:, c * HD + e:c * HD + e + 1]).then_inc(sq_ready.sem, 1)

                def z_unit(u):
                    b = 2 * (u in (1, 2))
                    act.wait_ge(full[b].sem, full[b].done(kind, h, f"z{u}"))
                    if u == 0:
                        wait(act, og_ready, og_ready.base(kind, h))
                    act.activation(z[:, 2 * u:2 * u + 2].rearrange("p a b -> p (a b)"), flat(bank[b][:]), ACT.Silu).then_inc(free[b].sem, 1)

                def exp_decay(sg, g, b, name):
                    act.wait_ge(full[b].sem, full[b].done(kind, h, name))
                    wait(act, dm_ready, dm_ready.done(kind, h, f"{sg}_{g}") - 2)
                    act.activation(flat(Dx[g][:]), flat(bank[b][:]), ACT.Exp).then_inc(free[b].sem, 1)

                if inv_:
                    for g in range(2):
                        exp_decay(0, g, 2 * g + 1, f"decay_{g}")
                    conv = conv_done.base(kind, h)
                    act.wait_ge(conv_done.sem, conv - 12)
                    wait(act, a_full, a_full.base(kind, h))
                    wait(act, b_full, b_full.base(kind, h))
                    act.activation(kT[par][:], y[0][:], ACT.Silu).then_inc(act_ready.sem, 1)
                    act.wait_ge(conv_done.sem, conv - 8)
                    act.activation(qT[par][:], y[1][:], ACT.Silu).then_inc(act_ready.sem, 1)
                    act.wait_ge(act_ready.sem, act_ready.done(kind, h, "k"))
                    act.activation(y[0][:], kT[par][:], ACT.Square).then_inc(act_ready.sem, 1)
                if scan:
                    z_unit(0)
                    z_unit(1)
                if inv_:
                    act.wait_ge(act_ready.sem, act_ready.done(kind, h, "q"))
                    act.activation(y[1][:], qT[par][:], ACT.Square).then_inc(act_ready.sem, 1)
                if scan:
                    z_unit(2)
                    z_unit(3)
                if inv_:
                    act.wait_ge(conv_done.sem, conv)
                    act.activation(y[2][:], y[2][:], ACT.Silu).then_inc(act_ready.sem, 1)
                    act.activation(y[3][:], y[3][:], ACT.Silu).then_inc(act_ready.sem, 1)
                if finish:
                    for u in range(4):
                        b = 2 * (u % 2) + 1
                        act.wait_ge(full[b].sem, full[b].done(kind, h, f"flip{u}"))
                        act.activation(flat(ogT[:, 4 * u:4 * u + 4]), flat(bank[b][:]), ACT.Copy, scale=gamma[:]).then_inc(free[b].sem, 1)
                if inv_:
                    for sg in range(2):
                        for k, slot in enumerate(SLOTS[sg]):
                            for g in range(2):
                                b0, b1, gi = 2 * g, 2 * g + 1, f"{sg}_{g}"
                                if slot == "decay":
                                    exp_decay(1, g, b0, "sg1_decay")
                                elif slot.startswith("merge"):
                                    lv = int(slot[5:])
                                    if lv < LEVELS:
                                        act.wait_ge(full[b0].sem, full[b0].done(kind, h, f"T{lv}_{sg}"))
                                        act.activation(changed(flat(Tn[g][:]), lv), changed(flat(bank[b0][:]), lv), ACT.Copy).then_inc(free[b0].sem, 1)
                                    else:
                                        act.wait_ge(full[b1].sem, full[b1].done(kind, h, f"U{lv}_{sg}"))
                                        act.activation(Uf[0:HALF, 8 * sg + 4 * g:8 * sg + 4 * g + 4, HALF:P], bank[b1][0:HALF, :, HALF:P], ACT.Copy).then_inc(free[b1].sem, 1)
                                elif slot.startswith("below") and slot != "below2":
                                    act.wait_ge(full[b1].sem, full[b1].done(kind, h, f"U{int(slot[5:]) - 1}_{sg}"))
                                    dst = Ut[g][:] if int(slot[5:]) < LEVELS else Uf[:, 8 * sg + 4 * g:8 * sg + 4 * g + 4]
                                    act.activation(flat(dst), flat(bank[b1][:]), ACT.Copy).then_inc(free[b1].sem, 1)
                            if scan and k in SCAN_AT[sg]:
                                scan_quantum(12 * sg + SCAN_AT[sg][k])
                            if not no_proj and k in PROJ_AT[sg]:
                                raw_unit(PROJ_AT[sg][k])
                elif scan:
                    for i in range(24):
                        scan_quantum(i)
                if scan:
                    squares(C - 1)

            for u in range(8):
                j = u // 2
                copy_raw(u, u + 1, 4 * (j - 1) if j >= 2 else None)
            run_steps(act, step)

        @block.vector
        def _(dve):
            def conv_tap(j, t, head, raws, base):
                tap = conv_w[:, bass.ds(head, 1), j, t:t + 1].rearrange("p a b -> p (a b)")
                src = raw[j % 2][:, t:t + T]
                if t == 0:
                    dve.wait_ge(p_free.sem, raws)
                    dve.tensor_scalar(y[j][:], src, tap, None, ALU.mult).then_inc(conv_done.sem, 1)
                else:
                    dve.wait_ge(conv_done.sem, base + 4 * j + t)
                    dve.scalar_tensor_tensor(y[j][:], src, tap, y[j][:], ALU.mult, ALU.add).then_inc(conv_done.sem, 1)

            def step(kind, h, par):
                inv_, scan, finish = works(kind)
                no_proj = not inv_ or (isinstance(h, int) and h == HK - 1)
                cfs, ccs = cf[1 - par], cc[1 - par]

                def scan_quantum(i):
                    c, part = i // 3, i % 3
                    it = c * HD
                    if part == 0:
                        dve.wait_ge(a_full.sem, a_full.done(kind, h, f"ks{c}"))
                        for e in range(HD):
                            ins = dve.scalar_tensor_tensor(X[:, e], bank_a[:, e], cfs[:, NGAM, it + e:it + e + 1],
                                                           v_s[1 - par][:, it + e], ALU.mult, ALU.add)
                        ins.then_inc(a_free.sem, 1)
                    elif part == 1:
                        dve.wait_ge(c_full.sem, c_full.done(kind, h, f"tx{c}"))
                        wait(dve, dt_ready, dt_ready.ahead(kind, h, f"dt{c}"))
                        dve.tensor_tensor(Dl[:], bank_c[:, 0:2], bc_last(ccs[:, it:it + 2], P), ALU.mult).then_inc(c_free.sem, 1)
                    else:
                        dve.wait_ge(a_full.sem, a_full.done(kind, h, f"su{c}"))
                        for e in range(HD):
                            ins = dve.scalar_tensor_tensor(S[:, e], S[:, e], cfs[:, GAMC, it + e:it + e + 1],
                                                           bank_a[:, e], ALU.mult, ALU.add)
                        ins.then_inc(a_free.sem, 1)
                        dve.wait_ge(b_full.sem, b_full.done(kind, h, f"o{c}"))
                        wait(dve, og_ready, og_ready.ahead(kind, h, f"og{c}"))
                        dve.tensor_tensor(O2[:], bank_b[:, 0:2], O1[:], ALU.add).then_inc(b_free.sem, 1)

                def decayed_kk(sg, g, b, name):
                    dve.wait_ge(full[b].sem, full[b].done(kind, h, name))
                    dve.wait_ge(ds_ready.sem, ds_ready.done(kind, h, f"{sg}_{g}"))
                    wait(dve, gl_ready, gl_ready.done(kind, h, f"{LEVELS}_{sg}_{g}") - 4 * LEVELS)
                    for i in range(4):
                        it = 8 * sg + 4 * g + i
                        ins = dve.scalar_tensor_tensor(G[sg][g][:, i], bank[b][:, i // 2], cc[par][:, it:it + 1],
                                                       Ds[g][:, i], ALU.mult, ALU.mult)
                    ins.then_inc(free[b].sem, 1)

                if finish:
                    dve.wait_ge(tail_pow.sem, tail_pow.base(kind, h))
                    dve.tensor_tensor(fac[:].rearrange("p (c e) -> p c e", e=HD), rs[:].rearrange("p (c e) -> p c e", e=HD),
                                      bc_last(rqs[:], HD), ALU.mult).then_inc(tail_dve.sem, 1)
                    dve.wait_ge(tail_dve.sem, tail_dve.done(kind, h, "fac"))
                    dve.tensor_tensor(og[:], og[:], bc_last(fac[:], P), ALU.mult).then_inc(tail_dve.sem, 1)
                if inv_:
                    dve.tensor_copy(cf[par][:], coef[:, :, bass.ds(h, 1)].rearrange("p q a i -> p q (a i)")).then_inc(cf_ready.sem, 1)
                    dve.wait_ge(full[0].sem, full[0].done(kind, h, "norm_k"))
                    wait(dve, roots_ready, roots_ready.base(kind, h))
                    dve.tensor_scalar(norms[:, 0:C], bank[0][:, 0, 0:C], EPS, None, ALU.add).then_inc(free[0].sem, 1)
                    dve.wait_ge(free[0].sem, free[0].done(kind, h, "norm_k"))
                    wait(dve, cc_ready, cc_ready.base(kind, h))
                    dve.reciprocal(inv[:], norms[:, 0:C]).then_inc(inv_ready.sem, 1)
                    dve.wait_ge(inv_ready.sem, inv_ready.done(kind, h, "it"))
                    dve.wait_ge(cf_ready.sem, cf_ready.done(kind, h, "it"))
                    dve.tensor_tensor(cc[par][:].rearrange("p (c e) -> p c e", e=HD), bc_last(inv[:], HD),
                                      cf[par][:, BETA].rearrange("p (c e) -> p c e", e=HD), ALU.mult).then_inc(cc_ready.sem, 1)
                    for u in range(2):
                        b = (2, 0)[u]
                        dve.wait_ge(full[b].sem, full[b].done(kind, h, f"k{u}"))
                        dve.tensor_copy(flat(k_tok[par][:, 4 * u:4 * u + 4]), flat(bank[b][:])).then_inc(free[b].sem, 1)
                    dve.wait_ge(cc_ready.sem, cc_ready.done(kind, h, "it"))
                    for g in range(2):
                        decayed_kk(0, g, 2 * g + 1, f"kk_{g}")
                    dve.wait_ge(full[2].sem, full[2].done(kind, h, "norm_q"))
                    dve.tensor_scalar(norms[:, C:2 * C], bank[2][:, 0, 0:C], EPS, None, ALU.add).then_inc(free[2].sem, 1)
                    dve.wait_ge(roots_ready.sem, roots_ready.done(kind, h, "k"))
                    for u in range(4):
                        b = 2 * (u % 2)
                        dve.wait_ge(full[b].sem, full[b].done(kind, h, f"v{u}"))
                        for j in range(2):
                            c = 2 * u + j
                            ins = dve.tensor_scalar(flat(v_s[par][:, 2 * c:2 * c + 2]), flat(bank[b][:, 2 * j:2 * j + 2]),
                                                    roots[par][:, c:c + 1], None, ALU.mult)
                        ins.then_inc(free[b].sem, 1)
                if finish:
                    for u in range(4):
                        b = (0, 2, 1, 3)[u]
                        dve.wait_ge(full[b].sem, full[b].done(kind, h, f"out{u}"))
                        xs = flat(x[:, 2 * u:2 * u + 2])
                        dve.wait_ge(free[b].sem, free[b].ahead(kind, h, f"out{u}"))
                        dve.tensor_tensor(xs, xs, flat(bank[b][:]), ALU.add).then_inc(free[b].sem, 1)
                if inv_:
                    for sg in range(2):
                        for k, slot in enumerate(SLOTS[sg]):
                            for g in range(2):
                                b0, b1, gi = 2 * g, 2 * g + 1, f"{sg}_{g}"
                                if slot == "kk":
                                    decayed_kk(1, g, b1, "sg1_kk")
                                elif slot == "level1":
                                    dve.wait_ge(full[b0].sem, full[b0].done(kind, h, f"level1_{sg}"))
                                    dve.tensor_tensor(Tn[g][:], bc_mid(ident[:], 4), bank[b0][:], ALU.subtract).then_inc(free[b0].sem, 1)
                                elif slot.startswith("below"):
                                    lv = int(slot[5:])
                                    dve.wait_ge(full[b0].sem, full[b0].done(kind, h, f"below{lv}_{sg}"))
                                    dve.tensor_tensor(per_item(W[g][:], lv), per_item(bc_mid(ident[:], 4), lv),
                                                      per_item(bank[b0][:], lv), ALU.subtract).then_inc(free[b0].sem, 1)
                                elif slot == "attn":
                                    dve.wait_ge(full[b0].sem, full[b0].done(kind, h, f"attn_{sg}"))
                                    dve.wait_ge(dm_ready.sem, dm_ready.done(kind, h, gi))
                                    for j in range(2):
                                        it = 8 * sg + 4 * g + 2 * j
                                        ins = dve.tensor_tensor(At[:, it:it + 2], bc_mid(bank[b0][:, j], 2),
                                                                Dm[g][:, 2 * j:2 * j + 2], ALU.mult)
                                    ins.then_inc(free[b0].sem, 1)
                            if scan and k in SCAN_AT[sg]:
                                scan_quantum(12 * sg + SCAN_AT[sg][k])
                            for t in range(4):
                                u = PROJ_AT[sg].get(k - t, 0)
                                if not no_proj and u % 2:
                                    conv_tap(u // 2, t, h + 1, p_free.done(kind, h, f"p{u}"), conv_done.base(kind, h))
                elif scan:
                    for i in range(24):
                        scan_quantum(i)
                if scan:
                    dve.wait_ge(roots_ready.sem, roots_ready.base(kind, h) if not inv_ else roots_ready.done(kind, h, "q"))
                    dve.tensor_scalar(rqs[:], roots[1 - par][:, C:2 * C], float(P) ** -0.5, None, ALU.mult).then_inc(tail_dve.sem, 1)
                    dve.wait_ge(tail_dve.sem, tail_dve.done(kind, h, "rqs"))
                    dve.tensor_tensor(rq2[:], rqs[:], rqs[:], ALU.mult).then_inc(tail_dve.sem, 1)
                    dve.wait_ge(tail_dve.sem, tail_dve.done(kind, h, "rq2"))
                    dve.wait_ge(sq_ready.sem, 2 * sq_ready.done(kind, h, f"sq{C - 1}"))
                    dve.tensor_tensor(var[:].rearrange("p (c e) -> p c e", e=HD), ms[:].rearrange("p (c e) -> p c e", e=HD),
                                      bc_last(rq2[:], HD), ALU.mult).then_inc(tail_dve.sem, 1)
                    dve.wait_ge(tail_dve.sem, tail_dve.done(kind, h, "var0"))
                    dve.tensor_scalar(var[:], var[:], 1.0 / P, EPS, ALU.mult, ALU.add).then_inc(tail_dve.sem, 1)
                if inv_:
                    dve.memset(S[:], 0.0).then_inc(s_zero.sem, 1)

            dve.memset(ones_col[:], 1.0).then_inc(s_const, 1)
            for j in range(4):
                for t in range(4):
                    conv_tap(j, t, 0, 2 * j + 2, 0)
            run_steps(dve, step)
            for u in range(4):
                b = (0, 2, 1, 3)[u]
                dve.wait_ge(free[b].sem, free[b].done("final", HK + 1, f"out{u}"))

        @block.gpsimd
        def _(pool):
            def step(kind, h, par):
                inv_, scan, finish = works(kind)
                no_next = not inv_ or (isinstance(h, int) and h == HK - 1)

                def gate(c):
                    it = c * HD
                    pool.wait_ge(b_free.sem, b_free.done(kind, h, f"o{c}"))
                    if c == 0 and finish:
                        for b in (1, 3):
                            pool.wait_ge(full[b].sem, full[b].done(kind, h, f"flip{2 + b // 2}"))
                    pool.tensor_tensor(og[:, it:it + 2], O2[:], z[:, c].rearrange("p (e d) -> p e d", e=HD),
                                       ALU.mult).then_inc(og_ready.sem, 1)

                def strict_decay(g, b, name):
                    pool.wait_ge(free[b].sem, free[b].done(kind, h, name))
                    pool.tensor_tensor(Ds[g][:], Dx[g][:], bc_mid(before_[:], 4), ALU.mult).then_inc(ds_ready.sem, 1)

                if inv_:
                    for g in range(2):
                        strict_decay(g, 2 * g + 1, f"decay_{g}")
                    pool.wait_ge(free[0].sem, free[0].done(kind, h, "norm_k"))
                    pool.tensor_tensor(roots[par][:, 0:C], norms[:, 0:C], powers[:, 0:C], ALU.pow).then_inc(roots_ready.sem, 1)
                    for sg in range(2):
                        for k, slot in enumerate(SLOTS[sg]):
                            for g in range(2):
                                b0, b1, gi = 2 * g, 2 * g + 1, f"{sg}_{g}"
                                if slot == "decay":
                                    strict_decay(g, b0, "sg1_decay")
                                elif slot == "level1":
                                    if sg == 0:
                                        pool.wait_ge(free[b1].sem, free[b1].done(kind, h, f"kk_{g}"))
                                        mask_level(kind, h, 0, g, 1)
                                    pool.wait_ge(gl_ready.sem, gl_ready.done(kind, h, f"1_{gi}"))
                                    read_before(kind, h, sg, b1, f"U{LEVELS}_0")
                                    pool.tensor_tensor(Ut[g][:], bc_mid(ident[:], 4), level_buffer(g, 1)[:], ALU.subtract).then_inc(u1_ready.sem, 1)
                                elif slot.startswith("below") and int(slot[5:]) < LEVELS:
                                    lv = int(slot[5:])
                                    if sg == 0 and lv == 2 and g == 0:
                                        for gg in range(2):
                                            mask_level(kind, h, 0, gg, 2)
                                    if lv > 2:
                                        pool.wait_ge(full[b0].sem, full[b0].done(kind, h, f"below{lv - 1}_{sg}"))
                                    else:
                                        read_before(kind, h, sg, b0, f"below{LEVELS}_0")
                                    mask_level(kind, h, sg, g, lv + 1)
                                elif slot == "merge3":
                                    pool.tensor_tensor(Dm[g][:], Dx[g][:], bc_mid(dm_mask[:], 4), ALU.mult).then_inc(dm_ready.sem, 1)
                                elif slot == "merge6" and sg == 0:
                                    pool.wait_ge(free[b1].sem, free[b1].done(kind, h, "sg1_kk"))
                                    pool.wait_ge(full[b0].sem, full[b0].done(kind, h, "level1_0"))
                                    mask_level(kind, h, 1, g, 1)
                                elif slot == "merge7" and sg == 0:
                                    pool.wait_ge(full[b0].sem, full[b0].done(kind, h, f"below{LEVELS - 1}_0"))
                                    mask_level(kind, h, 1, g, 2)
                            if sg == 0 and slot == "below3":
                                pool.wait_ge(free[2].sem, free[2].done(kind, h, "norm_q"))
                                pool.tensor_tensor(roots[par][:, C:2 * C], norms[:, C:2 * C], powers[:, C:2 * C], ALU.pow).then_inc(roots_ready.sem, 1)
                            if slot == "below2":
                                for g in range(2):
                                    if sg == 0:
                                        columns_of_g(h, g, 8 + 4 * g, full[2 * g + 1], full[2 * g + 1].done(kind, h, f"decay_{g}"))
                                    elif not no_next:
                                        columns_of_g(h + 1, g, 4 * g, full[2 * g], full[2 * g].done(kind, h, "sg1_decay"))
                            if scan and SCAN_AT[sg].get(k, 0) % 3 == 2:
                                gate(4 * sg + SCAN_AT[sg][k] // 3)
                elif scan:
                    for c in range(C):
                        gate(c)
                if scan:
                    pool.wait_ge(tail_dve.sem, tail_dve.done(kind, h, "var"))
                    pool.tensor_tensor(rs[:], var[:], minus_half[:], ALU.pow).then_inc(tail_pow.sem, 1)

            def columns_of_g(head, g, item, use, used):
                wait(pool, use, used)
                src = coef[:, G_, bass.ds(head, 1), item:item + 4].rearrange("p a i -> p (a i)")
                pool.tensor_tensor(gU[g][:], bc_mid(upto[:], 4), bc_last(src, P), ALU.mult).then_inc(gu_ready.sem, 1)

            def read_before(kind, h, sg, b, name):
                wait(pool, full[b], full[b].done(kind, h, name) if sg else full[b].base(kind, h))

            def mask_level(kind, h, sg, g, lv):
                pool.tensor_tensor(level_buffer(g, lv)[:], G[sg][g][:], bc_mid(levels[:, lv - 1], 4), ALU.mult).then_inc(gl_ready.sem, 1)

            for g in range(2):
                columns_of_g(0, g, 4 * g, full[0], None)
            run_steps(pool, step)


F1 = 512
NF = F1 // P


def perceptron(nc, x, hT, consts, d, load_experts):
    with ExitStack() as stack:
        a = Alloc(nc, stack, "mlp")
        w1 = a.sb("w1", [P, KD, F1])
        w2 = a.sb("w2", [P, NF, F1])
        w3 = a.sb("w3", [P, NF, D])
        b12 = a.sb("b12", [P, 2, NF])
        b3 = a.sb("b3", [P, D])
        names = ["w1", "b12", "w2", "w3", "b3"]
        tiles = dict(zip(names, [w1, b12, w2, w3, b3]))
        loaded = {n: a.sem(f"{n}_loaded") for n in names}

        def prefetch(sp):
            for n in names:
                src = d[f"mlp_{n}"]
                sp.dma_start(tiles[n][:], src.to_broadcast([P, D]) if n == "b3" else src).then_inc(loaded[n], 16)
            load_experts(sp)

        with ExitStack() as inner:
            layernorm_transposed(nc, Alloc(nc, inner, "norm2", a), x, hT, consts["ident"], EPS_LN, prefetch=prefetch)
        h = [a.sb("h1", [P, NF, T]), a.sb("h2", [P, NF, T])]
        bank = [a.psum([P, 512]) for i in range(4)]
        s_full, s_relu = a.sem("product_ready"), a.sem("relu_written")
        s_bias, s_out, s_sum = a.sem("bias_added"), a.sem("out_ready"), a.sem("out_added")
        units = [(l, half, f) for l in range(2) for half in range(2) for f in range(NF)]
        with nc.Block() as block:
            @block.tensor
            def _(pe):
                pe.wait_ge(loaded["w1"], 16)
                for n, (l, half, f) in enumerate(units):
                    if l == 1 and half == 0 and f == 0:
                        pe.wait_ge(loaded["w2"], 16)
                    if n >= 4:
                        pe.wait_ge(s_relu, n - 3)
                    if l == 1 and f == 0:
                        pe.wait_ge(s_relu, NF * (half + 1))
                    src, w, nk = (hT, w1, KD) if l == 0 else (h[0], w2, NF)
                    for k in range(nk):
                        ins = pe.matmul(bank[n % 4][:], w[:, k, f * P:(f + 1) * P], src[:, k, half * 512:(half + 1) * 512],
                                        start=k == 0, stop=k == nk - 1)
                    ins.then_inc(s_full, 1)
                pe.wait_ge(loaded["w3"], 16)
                for u in range(NT // 2):
                    n = len(units)
                    pe.wait_ge(s_relu, n)
                    for j in range(2):
                        t = 2 * u + j
                        for k in range(NF):
                            ins = pe.matmul(bank[u][:, j * D:(j + 1) * D], h[1][:, k, t * P:(t + 1) * P], w3[:, k],
                                            start=k == 0, stop=k == NF - 1)
                    ins.then_inc(s_out, 1)

            @block.scalar
            def _(act):
                act.wait_ge(loaded["b12"], 16)
                for n, (l, half, f) in enumerate(units):
                    act.wait_ge(s_full, n + 1)
                    act.activation(h[l][:, f, half * 512:(half + 1) * 512], bank[n % 4][:], ACT.Relu,
                                   bias=b12[:, l, f:f + 1]).then_inc(s_relu, 1)

            @block.vector
            def _(dve):
                dve.wait_ge(loaded["b3"], 16)
                dve.tensor_tensor(x[:], x[:], bc_mid(b3[:], NT), ALU.add).then_inc(s_bias, 1)
                dve.wait_ge(s_bias, 1)
                for u in range(NT // 2):
                    dve.wait_ge(s_out, u + 1)
                    xs = x[:, 2 * u:2 * u + 2].rearrange("p a b -> p (a b)")
                    dve.tensor_tensor(xs, xs, bank[u][:], ALU.add).then_inc(s_sum, 1)
                dve.wait_ge(s_sum, NT // 2)
        a.clear_sems()


NH = 4
DH = D // NH


def attention(nc, x, hT, consts, d):
    ident = consts["ident"]
    with ExitStack() as stack:
        a = Alloc(nc, stack, "attn")
        names = ["wq", "wk", "wv", "wo", "bqk", "bv", "bo"]
        tiles = {n: a.sb(n, [P, KD, D]) for n in names[:4]}
        tiles["bqk"] = a.sb("bqk", [P, 2, KD])
        tiles["bv"], tiles["bo"] = a.sb("bv", [P, D]), a.sb("bo", [P, D])
        loaded = {n: a.sem(f"{n}_loaded") for n in names}

        def prefetch(sp):
            for n in names:
                src = d[f"attn_{n}"]
                sp.dma_start(tiles[n][:], src.to_broadcast([P, D]) if n in ("bv", "bo") else src).then_inc(loaded[n], 16)

        with ExitStack() as inner:
            layernorm_transposed(nc, Alloc(nc, inner, "norm3", a), x, hT, ident, EPS_LN, prefetch=prefetch)
        qkT = [a.sb("qT", [P, KD, T]), a.sb("kT", [P, KD, T])]
        v = a.sb("v", [P, NT, D])
        feats = a.sb("feats", [P, NT, D])
        featsT = a.sb("featsT", [P, KD, T])
        prob = [a.sb(f"prob{i}", [P, T]) for i in range(2)]
        probT = [a.sb(f"probT{i}", [P, NT, P]) for i in range(2)]
        neg = a.sb("neg_max", [P, NH * NT])
        total = a.sb("total", [P, NH * NT])
        rtotal = a.sb("rtotal", [P, NH * NT])
        score = [a.psum([P, T]) for i in range(2)]
        flip = [a.psum([P, 4, P]) for i in range(2)]
        mix = a.psum([P, 512])
        spare = a.psum([P, 512])

        bank = [score[0][:, 0:512], score[1][:, 0:512], flip[0][:].rearrange("p a b -> p (a b)"), mix[:]]
        s_full, s_qk, s_v = a.sem("proj_ready"), a.sem("qk_written"), a.sem("v_written")
        qk_units = [(w, f, half) for w in range(2) for f in range(KD) for half in range(2)]
        with nc.Block() as block:
            @block.tensor
            def _(pe):
                for n, (w, f, half) in enumerate(qk_units):
                    pe.wait_ge(loaded[names[w]], 16)
                    if n >= 4:
                        pe.wait_ge(s_qk, n - 3)
                    for kd in range(KD):
                        ins = pe.matmul(bank[n % 4], tiles[names[w]][:, kd, f * P:(f + 1) * P],
                                        hT[:, kd, half * 512:(half + 1) * 512], start=kd == 0, stop=kd == KD - 1)
                    ins.then_inc(s_full, 1)
                pe.wait_ge(loaded["wv"], 16)
                for u in range(NT // 2):
                    pe.wait_ge(s_qk, u + 5)
                    for j in range(2):
                        t = 2 * u + j
                        for kd in range(KD):
                            ins = pe.matmul(bank[u][:, j * D:(j + 1) * D], hT[:, kd, t * P:(t + 1) * P], tiles["wv"][:, kd],
                                            start=kd == 0, stop=kd == KD - 1)
                    ins.then_inc(s_full, 1)

            @block.scalar
            def _(act):
                act.wait_ge(loaded["bqk"], 16)
                for n, (w, f, half) in enumerate(qk_units):
                    act.wait_ge(s_full, n + 1)
                    act.activation(qkT[w][:, f, half * 512:(half + 1) * 512], bank[n % 4], ACT.Identity,
                                   bias=tiles["bqk"][:, w, f:f + 1]).then_inc(s_qk, 1)

            @block.vector
            def _(dve):
                dve.wait_ge(loaded["bv"], 16)
                for u in range(NT // 2):
                    dve.wait_ge(s_full, 8 + u + 1)
                    dve.tensor_tensor(v[:, 2 * u:2 * u + 2], bank[u].rearrange("p (a b) -> p a b", a=2),
                                      bc_mid(tiles["bv"][:], 2), ALU.add).then_inc(s_v, 1)
                dve.wait_ge(s_v, NT // 2)

        rows = [(hh, t) for hh in range(NH) for t in range(NT)]
        R = len(rows)
        s_score, s_max, s_exp = a.sem("scores_ready"), a.sem("max_ready"), a.sem("probs_ready")
        s_flip, s_pt, s_mix = a.sem("probs_flipped"), a.sem("probT_written"), a.sem("mixed")
        s_rt, s_feat, s_rowmax = a.sem("total_inverted"), a.sem("feats_written"), a.sem("row_max")
        with nc.Block() as block:
            @block.tensor
            def _(pe):
                def scores(r):
                    hh, t = rows[r]
                    f, p0 = hh // 2, (hh % 2) * DH
                    if r >= 2:
                        pe.wait_ge(s_exp, r - 1)
                    for half in range(2):
                        ins = pe.matmul(score[r % 2][:, half * 512:(half + 1) * 512], qkT[0][p0:p0 + DH, f, t * P:(t + 1) * P],
                                        qkT[1][p0:p0 + DH, f, half * 512:(half + 1) * 512], start=True, stop=True)
                    ins.then_inc(s_score, 1)

                def transposes(r):
                    pe.wait_ge(s_exp, r + 1)
                    for half in range(2):
                        if r >= 1:
                            pe.wait_ge(s_pt, 2 * (r - 1) + half + 1)
                        for j in range(4):
                            k = half * 4 + j
                            ins = pe.transpose(flip[half][:, j], prob[r % 2][:, k * P:(k + 1) * P], ident[:])
                        ins.then_inc(s_flip, 1)

                def mixes(r):
                    hh, t = rows[r]
                    pe.wait_ge(s_pt, 2 * r + 2)
                    out = (mix, spare)[r % 2]
                    if r >= 2:
                        pe.wait_ge(s_feat, r - 1)
                    for k in range(NT):
                        ins = pe.matmul(out[:, 0:DH], probT[r % 2][:, k], v[:, k, hh * DH:(hh + 1) * DH],
                                        start=k == 0, stop=k == NT - 1)
                    ins.then_inc(s_mix, 1)

                scores(0)
                for r in range(R + 1):
                    if r + 1 < R:
                        scores(r + 1)
                    if r >= 1:
                        mixes(r - 1)
                    if r < R:
                        transposes(r)

            @block.scalar
            def _(act):
                for r in range(R + 1):
                    if r < R:
                        act.wait_ge(s_max, r + 1)
                        if r >= 2:
                            act.wait_ge(s_flip, 2 * (r - 1))
                        act.activation(prob[r % 2][:], score[r % 2][:], ACT.Exp, bias=neg[:, r:r + 1], scale=0.5,
                                       accum_out=total[:, r:r + 1]).then_inc(s_exp, 1)
                    if r >= 1:
                        act.wait_ge(s_flip, 2 * r)
                        if r >= 3:
                            act.wait_ge(s_mix, r - 2)
                        act.wait_ge(s_pt, 2 * r - 1)
                        act.activation(probT[(r - 1) % 2][:, 4:8].rearrange("p a b -> p (a b)"),
                                       flip[1][:].rearrange("p a b -> p (a b)"), ACT.Copy).then_inc(s_pt, 1)

            @block.vector
            def _(dve):
                for r in range(R + 2):
                    if r < R:
                        dve.wait_ge(s_score, r + 1)
                        dve.tensor_reduce(neg[:, r:r + 1], score[r % 2][:], AX_X, ALU.max).then_inc(s_rowmax, 1)
                        dve.wait_ge(s_rowmax, r + 1)
                        dve.tensor_scalar(neg[:, r:r + 1], neg[:, r:r + 1], -0.5, None, ALU.mult).then_inc(s_max, 1)
                    if 1 <= r <= R:
                        dve.wait_ge(s_flip, 2 * r - 1)
                        if r >= 3:
                            dve.wait_ge(s_mix, r - 2)
                        if r >= 2:
                            dve.wait_ge(s_pt, 2 * r - 2)
                        dve.tensor_copy(probT[(r - 1) % 2][:, 0:4].rearrange("p a b -> p (a b)"),
                                        flip[0][:].rearrange("p a b -> p (a b)")).then_inc(s_pt, 1)
                    if r >= 2:
                        hh, t = rows[r - 2]
                        dve.wait_ge(s_mix, r - 1)
                        dve.reciprocal(rtotal[:, r - 2:r - 1], total[:, r - 2:r - 1]).then_inc(s_rt, 1)
                        dve.wait_ge(s_rt, r - 1)
                        dve.tensor_scalar(feats[:, t, hh * DH:(hh + 1) * DH], (mix, spare)[r % 2][:, 0:DH], rtotal[:, r - 2:r - 1],
                                          None, ALU.mult).then_inc(s_feat, 1)
                dve.wait_ge(s_feat, R)

        s_ft, s_ftw, s_o, s_bo, s_add = (a.sem(n) for n in ("feats_flipped", "featsT_written", "out_ready", "bias_added", "out_added"))
        flat_bank = [score[0][:, 0:512], score[1][:, 0:512], flip[0][:].rearrange("p a b -> p (a b)"), mix[:]]
        with nc.Block() as block:
            @block.tensor
            def _(pe):
                for u in range(4):
                    f, half = u // 2, u % 2
                    for j in range(4):
                        t = half * 4 + j
                        ins = pe.transpose(flat_bank[u][:, j * P:(j + 1) * P], feats[:, t, f * P:(f + 1) * P], ident[:])
                    ins.then_inc(s_ft, 1)
                pe.wait_ge(s_ftw, 4)
                pe.wait_ge(loaded["wo"], 16)
                for u in range(NT // 2):
                    for j in range(2):
                        t = 2 * u + j
                        for f in range(KD):
                            ins = pe.matmul(flat_bank[u][:, j * D:(j + 1) * D], featsT[:, f, t * P:(t + 1) * P], tiles["wo"][:, f],
                                            start=f == 0, stop=f == KD - 1)
                    ins.then_inc(s_o, 1)

            @block.scalar
            def _(act):
                for u in range(4):
                    f, half = u // 2, u % 2
                    act.wait_ge(s_ft, u + 1)
                    act.activation(featsT[:, f, half * 512:(half + 1) * 512], flat_bank[u], ACT.Copy).then_inc(s_ftw, 1)

            @block.vector
            def _(dve):
                dve.wait_ge(loaded["bo"], 16)
                dve.tensor_tensor(x[:], x[:], bc_mid(tiles["bo"][:], NT), ALU.add).then_inc(s_bo, 1)
                dve.wait_ge(s_bo, 1)
                for u in range(NT // 2):
                    dve.wait_ge(s_o, u + 1)
                    xs = x[:, 2 * u:2 * u + 2].rearrange("p a b -> p (a b)")
                    dve.tensor_tensor(xs, xs, flat_bank[u], ALU.add).then_inc(s_add, 1)
                dve.wait_ge(s_add, NT // 2)
        a.clear_sems()


E = 32
TOPK = 4
FE = 176
FH = FE // 2
FS = 704
CAP = 128
SKIP = 8192.0
SH = [(i * P, min(P, FS - i * P)) for i in range((FS + P - 1) // P)]


def mixture(nc, x, hT, consts, d, w_gu, gu_loaded, buf, ybuf, s_zeroed, out):
    ident = consts["ident"]
    with ExitStack() as stack:
        a = Alloc(nc, stack, "moe")
        w_norm = a.sb("w_norm", [P, D])
        w_r = a.sb("w_r", [P, KD, E + 1])
        iota = a.sb("iota", [P, E])
        xn = a.sb("xn", [P, NT, D])
        rows = a.sb("rows", [P, NT * TOPK], U32)
        wv = a.sb("wv", [P, NT * TOPK])
        names = ["w_norm", "w_r", "iota"]
        tiles = dict(zip(names, [w_norm, w_r, iota]))
        loaded = {n: a.sem(f"{n}_loaded") for n in names + ["sw_gu", "sw_down"]}
        route_stack = ExitStack()
        b = Alloc(nc, route_stack, "route", a)
        sw_gu = b.sb("sw_gu", [P, 2, KD, FS])
        sw_down = b.sb("sw_down", [P, len(SH), D])

        def prefetch(sp):
            for n in names:
                src = d[f"moe_{n}"]
                sp.dma_start(tiles[n][:], src if n == "w_r" else src.to_broadcast(list(tiles[n].shape))).then_inc(loaded[n], 16)
            sp.dma_start(sw_gu[:], d["sw_gu"]).then_inc(loaded["sw_gu"], 16)
            sp.dma_start(sw_down[:, 0:5], d["sw_down"][:, 0:5]).then_inc(loaded["sw_down"], 16)
            sp.dma_start(sw_down[0:64, 5], d["sw_down"][0:64, 5]).then_inc(loaded["sw_down"], 16)

        with ExitStack() as inner:
            layernorm_transposed(nc, Alloc(nc, inner, "norm4", a), x, hT, ident, EPS_LN, prefetch=prefetch,
                                 rms_weight=w_norm, weight_ready=loaded["w_norm"], xn=xn)
        with route_stack:
            route_and_share(nc, b, x, hT, consts, xn, w_r, iota, loaded, sw_gu, sw_down, rows, wv, buf, s_zeroed)
        experts(nc, a, consts, d, w_gu, gu_loaded, buf, ybuf)
        combine(nc, a, x, rows, wv, ybuf, out)


def route_and_share(nc, a, x, hT, consts, xn, w_r, iota, loaded, sw_gu, sw_down, rows, wv, buf, s_zeroed):
    N = NT * TOPK
    before_, ones = consts["before"], a.sb("ones", [P, P])
    lg = a.sb("lg", [P, NT, E + 1])
    top = a.sb("top", [P, NT, 8])
    idx = a.sb("idx", [P, NT, 8], U32)
    idxf = a.sb("idxf", [P, NT, TOPK])
    hot = a.sb("hot", [P, NT, TOPK, E])
    prod = a.sb("prod", [P, NT, TOPK, E])
    chosen = a.sb("chosen", [P, NT, E])
    shift = a.sb("shift", [P, NT, E])
    shift4 = a.sb("shift4", [P, NT, TOPK])
    esum = a.sb("esum", [P, NT])
    rsum = a.sb("rsum", [P, NT])
    gate = a.sb("gate", [P, NT])
    pos = a.sb("pos", [P, N])
    valid = a.sb("valid", [P, N])
    row = a.sb("row", [P, N])
    dest_f = a.sb("dest_f", [P, N])
    dest = a.sb("dest", [P, N], U32)
    hsh = a.sb("hsh", [P, len(SH), T])
    up = a.sb("up", [P, 2, 512])
    lg_ps = a.psum([P, NT, 64])
    pos_ps = a.psum([P, NT, 64])
    gp = [a.psum([P, 512]) for i in range(2)]
    upp = [a.psum([P, 512]) for i in range(2)]
    down = [a.psum([P, 2, D]) for i in range(2)]
    s_lg, s_ones, s_r, s_e = a.sem("logits_ready"), a.sem("ones_ready"), a.sem("routing_step"), a.sem("exp_step")
    s_tops, s_pos, s_scat = a.sem("tops_step"), a.sem("places_ready"), a.sem("scattered")
    s_gp, s_upp, s_silu, s_hsh, s_down, s_add = (a.sem(n) for n in ("gate_ready", "up_ready", "silu_written", "hidden_written",
                                                                 "down_ready", "shared_added"))
    units = [(half, f) for half in range(2) for f in range(len(SH))]
    with nc.Block() as block:
        @block.tensor
        def _(pe):
            pe.wait_ge(loaded["w_r"], 16)
            for t in range(NT):
                for kd in range(KD):
                    ins = pe.matmul(lg_ps[:, t, 0:E + 1], hT[:, kd, t * P:(t + 1) * P], w_r[:, kd], start=kd == 0, stop=kd == KD - 1)
            ins.then_inc(s_lg, 1)
            pe.wait_ge(loaded["sw_gu"], 16)

            def places():
                pe.wait_ge(s_ones, 1)
                pe.wait_ge(s_r, 3)
                for t in range(NT):
                    for u in range(t + 1):
                        ins = pe.matmul(pos_ps[:, t, 0:E], before_[:] if u == t else ones[:], chosen[:, u], start=u == 0, stop=u == t)
                ins.then_inc(s_pos, 1)

            for n, (half, f) in enumerate(units):
                f0, fn = SH[f]
                if n >= 2:
                    pe.wait_ge(s_silu, n - 1)
                for w, ps, done in ((0, gp, s_gp), (1, upp, s_upp)):
                    if w == 1 and n >= 2:
                        pe.wait_ge(s_hsh, n - 1)
                    for kd in range(KD):
                        ins = pe.matmul(ps[n % 2][0:fn, :], sw_gu[:, w, kd, f0:f0 + fn], hT[:, kd, half * 512:(half + 1) * 512],
                                        start=kd == 0, stop=kd == KD - 1)
                    ins.then_inc(done, 1)
                if n == 4:
                    places()
            pe.wait_ge(loaded["sw_down"], 32)
            for u in range(NT // 2):
                pe.wait_ge(s_hsh, len(SH) * (u // 2 + 1))
                if u >= 2:
                    pe.wait_ge(s_add, 2 * (u - 1))
                for j in range(2):
                    t = 2 * u + j
                    for f, (f0, fn) in enumerate(SH):
                        ins = pe.matmul(down[u % 2][:, j], hsh[0:fn, f, t * P:(t + 1) * P], sw_down[0:fn, f],
                                        start=f == 0, stop=f == len(SH) - 1)
                ins.then_inc(s_down, 1)

        @block.scalar
        def _(act):
            act.wait_ge(s_tops, 2 * NT + 1)
            act.activation(gate[:], lg[:, :, E], ACT.Exp, scale=-1.0).then_inc(s_e, 1)
            act.wait_ge(s_r, 5)
            act.activation(shift[:], shift[:], ACT.Exp).then_inc(s_e, 1)
            act.activation(shift4[:], shift4[:], ACT.Exp).then_inc(s_e, 1)
            for n, (half, f) in enumerate(units):
                f0, fn = SH[f]
                act.wait_ge(s_gp, n + 1)
                if n >= 2:
                    act.wait_ge(s_hsh, n - 1)
                act.activation(up[0:fn, n % 2], gp[n % 2][0:fn, :], ACT.Silu).then_inc(s_silu, 1)

        @block.vector
        def _(dve):
            def hidden(n):
                half, f = units[n]
                f0, fn = SH[f]
                dve.wait_ge(s_silu, n + 1)
                dve.wait_ge(s_upp, n + 1)
                dve.tensor_tensor(hsh[0:fn, f, half * 512:(half + 1) * 512], up[0:fn, n % 2], upp[n % 2][0:fn, :],
                                  ALU.mult).then_inc(s_hsh, 1)

            dve.memset(ones[:], 1.0).then_inc(s_ones, 1)
            dve.wait_ge(s_lg, 1)
            dve.tensor_copy(lg[:], lg_ps[:, :, 0:E + 1]).then_inc(s_tops, 1)
            dve.wait_ge(s_tops, 1)
            for t in range(NT):
                dve.max(top[:, t], lg[:, t, 0:E]).then_inc(s_tops, 1)
            for t in range(NT):
                dve.wait_ge(s_tops, t + 2)
                dve.max_index(idx[:, t], top[:, t], lg[:, t, 0:E]).then_inc(s_tops, 1)
            dve.wait_ge(s_tops, 2 * NT + 1)
            dve.tensor_copy(idxf[:], idx[:, :, 0:TOPK]).then_inc(s_r, 1)
            dve.wait_ge(s_r, 1)
            dve.wait_ge(loaded["iota"], 16)
            dve.tensor_tensor(hot[:].rearrange("p t s e -> p (t s) e"), bc_last(idxf[:].rearrange("p t s -> p (t s)"), E),
                              bc_mid(iota[:], N), ALU.is_equal).then_inc(s_r, 1)
            dve.wait_ge(s_r, 2)
            dve.tensor_reduce(chosen[:], hot[:].rearrange("p t s e -> p t e s"), AX_X, ALU.add).then_inc(s_r, 1)
            dve.tensor_tensor(shift[:], lg[:, :, 0:E], bc_last(top[:, :, 0], E), ALU.subtract).then_inc(s_r, 1)
            dve.tensor_tensor(shift4[:], top[:, :, 0:TOPK], bc_last(top[:, :, 0], TOPK), ALU.subtract).then_inc(s_r, 1)
            dve.wait_ge(s_e, 3)
            dve.tensor_reduce(esum[:], shift[:], AX_X, ALU.add).then_inc(s_r, 1)
            dve.tensor_scalar(gate[:], gate[:], 1.0, None, ALU.add).then_inc(s_r, 1)
            dve.wait_ge(s_r, 7)
            dve.reciprocal(rsum[:], esum[:]).then_inc(s_r, 1)
            dve.reciprocal(gate[:], gate[:]).then_inc(s_r, 1)
            dve.wait_ge(s_r, 9)
            for n in range(4):
                hidden(n)
            dve.wait_ge(s_pos, 1)
            for t in range(NT):
                ins = dve.tensor_tensor(prod[:, t], hot[:, t], bc_mid(pos_ps[:, t, 0:E], TOPK), ALU.mult)
            ins.then_inc(s_r, 1)
            dve.wait_ge(s_r, 10)
            dve.tensor_reduce(pos[:], prod[:].rearrange("p t s e -> p (t s) e"), AX_X, ALU.add).then_inc(s_r, 1)
            dve.wait_ge(s_r, 11)
            dve.tensor_scalar(valid[:], pos[:], float(CAP), None, ALU.is_lt).then_inc(s_r, 1)
            dve.tensor_scalar(row[:], pos[:], float(CAP - 1), None, ALU.min).then_inc(s_r, 1)
            dve.wait_ge(s_r, 13)
            dve.scalar_tensor_tensor(row[:], idxf[:].rearrange("p t s -> p (t s)"), float(CAP), row[:], ALU.mult, ALU.add).then_inc(s_r, 1)
            dve.tensor_tensor(wv[:].rearrange("p (t s) -> p t s", s=TOPK), shift4[:], bc_last(rsum[:], TOPK), ALU.mult).then_inc(s_r, 1)
            dve.wait_ge(s_r, 15)
            dve.scalar_tensor_tensor(dest_f[:], valid[:], -SKIP, row[:], ALU.mult, ALU.add).then_inc(s_r, 1)
            dve.tensor_tensor(wv[:], wv[:], valid[:], ALU.mult).then_inc(s_r, 1)
            dve.wait_ge(s_r, 17)
            dve.tensor_copy(rows[:], row[:]).then_inc(s_r, 1)
            dve.tensor_scalar(dest[:], dest_f[:], SKIP, None, ALU.add).then_inc(s_r, 1)
            for n in range(4, len(units)):
                hidden(n)
            for u in range(NT // 2):
                dve.wait_ge(s_down, u + 1)
                for j in range(2):
                    t = 2 * u + j
                    dve.scalar_tensor_tensor(x[:, t], down[u % 2][:, j], gate[:, t:t + 1], x[:, t], ALU.mult, ALU.add).then_inc(s_add, 1)
            dve.wait_ge(s_add, NT)
            dve.wait_ge(s_r, 19)

        @block.gpsimd
        def _(pool):
            pool.wait_ge(s_zeroed, 16)
            pool.wait_ge(s_r, 19)
            for t in range(NT):
                for s in range(TOPK):
                    n = t * TOPK + s
                    pool.indirect_dma_start(out=buf, out_offset=bass.IndirectOffsetOnAxis(ap=dest[:, n:n + 1], axis=0),
                                            in_=xn[:, t], in_offset=None, bounds_check=E * CAP - 1,
                                            oob_is_err=False).then_inc(s_scat, 16)
            pool.wait_ge(s_scat, 16 * N)


UN = 4


def experts(nc, a, consts, d, w_gu, gu_loaded, buf, ybuf):
    ident = consts["ident"]
    be = [a.sb(f"be{i}", [P, D]) for i in range(UN)]
    wd = [a.sb(f"wd{i}", [FH, 2, D]) for i in range(UN)]
    bT = [a.sb(f"bT{i}", [P, KD, P]) for i in range(UN)]
    sg = [a.sb(f"sg{i}", [P, FE]) for i in range(UN)]
    hh = [a.sb(f"hh{i}", [P, FE]) for i in range(UN)]
    hhT = [a.sb(f"hhT{i}", [FH, 2, P]) for i in range(UN)]
    ys = [a.sb(f"ys{i}", [P, D]) for i in range(UN)]
    tb = [a.psum([P, 4, P]) for i in range(2)]
    gb = [a.psum([P, 512]) for i in range(2)]
    ht = [a.psum([P, 4, P]) for i in range(2)]
    yb = [a.psum([P, 512]) for i in range(2)]
    s_be = [a.sem(f"rows{i}_loaded") for i in range(UN)]
    s_wd = [a.sem(f"wd{i}_loaded") for i in range(UN)]
    s_y = [a.sem(f"y{i}_stored") for i in range(UN)]
    s_tb, s_bt, s_gb, s_sg, s_hh = (a.sem(n) for n in ("rows_flipped", "rowsT_written", "hidden_ready", "silu_written", "hidden_written"))
    s_ht, s_hht, s_yb, s_ys = (a.sem(n) for n in ("hidden_flipped", "hiddenT_written", "y_ready", "y_copied"))
    TURNS = E // UN

    def per_expert(eng, step):
        for i in range(UN):
            step(True, 0, i)
        with eng.Fori(1, TURNS) as t:
            for i in range(UN):
                step(False, t, i)

    with nc.Block() as block:
        @block.sync
        def _(sp):
            def load(first, t, i):
                e = t * UN + i
                if not first:
                    sp.wait_ge(s_tb, e - UN + 1)
                sp.dma_start(be[i][:], buf.rearrange("(e c) n -> e c n", c=CAP)[bass.ds(e, 1)].rearrange("a c n -> (a c) n")).then_inc(s_be[i], 16)

            per_expert(sp, load)

        @block.gpsimd
        def _(pool):
            def load_down(e, i):
                pool.dma_start(wd[i][:], d["w_down"][bass.ds(e, 1)].rearrange("a p k n -> (a p) k n")).then_inc(s_wd[i], 16)

            def store(t, i):
                e = t * UN + i
                pool.wait_ge(s_ys, e + 1)
                pool.dma_start(ybuf.rearrange("(e c) n -> e c n", c=CAP)[bass.ds(e, 1)].rearrange("a c n -> (a c) n"), ys[i][:]).then_inc(s_y[i], 16)

            for i in range(UN):
                load_down(i, i)
            with pool.Fori(0, TURNS - 1) as t:
                for i in range(UN):
                    store(t, i)
                    load_down(t * UN + UN + i, i)
            for i in range(UN):
                store(TURNS - 1, i)
            for s in s_y:
                pool.wait_ge(s, 16 * TURNS)

        @block.tensor
        def _(pe):
            def flip(first, t, i):
                e = t * UN + i
                pe.wait_ge(s_be[i], 16 * t + 16)
                if not (first and i < 2):
                    pe.wait_ge(s_bt, e - 1)
                for kd in range(KD):
                    ins = pe.transpose(tb[i % 2][:, kd], be[i][:, kd * P:(kd + 1) * P], ident[:])
                ins.then_inc(s_tb, 1)

            def hidden(first, t, i):
                e = t * UN + i
                pe.wait_ge(s_bt, e + 1)
                if not (first and i < 2):
                    pe.wait_ge(s_hh, e - 1)
                for kd in range(KD):
                    w = w_gu[:, bass.ds(e, 1), kd].rearrange("p a n -> p (a n)")
                    ins = pe.matmul(gb[i % 2][:, 0:2 * FE], bT[i][:, kd], w, start=kd == 0, stop=kd == KD - 1)
                ins.then_inc(s_gb, 1)

            def output(first, t, i):
                e = t * UN + i
                pe.wait_ge(s_hh, e + 1)
                if not (first and i < 2):
                    pe.wait_ge(s_hht, e - 1)
                    pe.wait_ge(s_ys, e - 1)
                for k in range(2):
                    ins = pe.transpose(ht[i % 2][0:FH, k], hh[i][:, k * FH:(k + 1) * FH], ident[:])
                ins.then_inc(s_ht, 1)
                pe.wait_ge(s_hht, e + 1)
                pe.wait_ge(s_wd[i], 16 * t + 16)
                for k in range(2):
                    ins = pe.matmul(yb[i % 2][:, 0:D], hhT[i][:, k], wd[i][:, k], start=k == 0, stop=k == 1)
                ins.then_inc(s_yb, 1)

            def turn(first, t, last):
                hidden(first, t, 0)
                for i in range(1, UN):
                    hidden(first, t, i)
                    if i == UN - 1 and not last:
                        for k in range(2):
                            flip(False, t + 1, k)
                    output(first, t, i - 1)
                if not last:
                    for k in range(2, UN):
                        flip(False, t + 1, k)
                output(first, t, UN - 1)

            for s in gu_loaded:
                pe.wait_ge(s, 16)
            for i in range(UN):
                flip(True, 0, i)
            turn(True, 0, False)
            with pe.Fori(1, TURNS - 1) as t:
                turn(False, t, False)
            turn(False, TURNS - 1, True)

        @block.vector
        def _(dve):
            def rows_out(first, t, i):
                e = t * UN + i
                dve.wait_ge(s_tb, e + 1)
                if not first:
                    dve.wait_ge(s_gb, e - UN + 1)
                dve.tensor_copy(bT[i][:], tb[i % 2][:, 0:KD]).then_inc(s_bt, 1)

            def hidden(first, t, i):
                e = t * UN + i
                dve.wait_ge(s_sg, e + 1)
                if not first:
                    dve.wait_ge(s_ht, e - UN + 1)
                dve.tensor_tensor(hh[i][:], sg[i][:], gb[i % 2][:, FE:2 * FE], ALU.mult).then_inc(s_hh, 1)

            def y_out(first, t, i):
                e = t * UN + i
                dve.wait_ge(s_yb, e + 1)
                if not first:
                    dve.wait_ge(s_y[i], 16 * t)
                dve.tensor_copy(ys[i][:], yb[i % 2][:, 0:D]).then_inc(s_ys, 1)

            def turn(first, t, last):
                hidden(first, t, 0)
                for i in range(1, UN):
                    hidden(first, t, i)
                    if i == UN - 1 and not last:
                        for k in range(2):
                            rows_out(False, t + 1, k)
                    y_out(first, t, i - 1)
                if not last:
                    for k in range(2, UN):
                        rows_out(False, t + 1, k)
                y_out(first, t, UN - 1)

            for i in range(UN):
                rows_out(True, 0, i)
            turn(True, 0, False)
            with dve.Fori(1, TURNS - 1) as t:
                turn(False, t, False)
            turn(False, TURNS - 1, True)

        @block.scalar
        def _(act):
            def silu(first, t, i):
                e = t * UN + i
                act.wait_ge(s_gb, e + 1)
                if not first:
                    act.wait_ge(s_hh, e - UN + 1)
                act.activation(sg[i][:], gb[i % 2][:, 0:FE], ACT.Silu).then_inc(s_sg, 1)

            def hT_out(first, t, i):
                e = t * UN + i
                act.wait_ge(s_ht, e + 1)
                if not first:
                    act.wait_ge(s_yb, e - UN + 1)
                act.activation(hhT[i][:], ht[i % 2][0:FH, 0:2], ACT.Copy).then_inc(s_hht, 1)

            def turn(first, t):
                silu(first, t, 0)
                for i in range(1, UN):
                    silu(first, t, i)
                    hT_out(first, t, i - 1)
                hT_out(first, t, UN - 1)

            turn(True, 0)
            with act.Fori(1, TURNS) as t:
                turn(False, t)


def combine(nc, a, x, rows, wv, ybuf, out):
    NB = 8
    yg = [a.sb(f"yg{i}", [P, D]) for i in range(NB)]
    s_g = [a.sem(f"gathered{i}") for i in range(NB)]
    s_sum, s_out = a.sem("expert_added"), a.sem("out_written")
    with nc.Block() as block:
        @block.gpsimd
        def _(pool):
            for n in range(NT * TOPK):
                if n >= NB:
                    pool.wait_ge(s_sum, n - NB + 1)
                pool.indirect_dma_start(out=yg[n % NB][:], out_offset=None, in_=ybuf,
                                        in_offset=bass.IndirectOffsetOnAxis(ap=rows[:, n:n + 1], axis=0)).then_inc(s_g[n % NB], 16)

        @block.vector
        def _(dve):
            for n in range(NT * TOPK):
                t = n // TOPK
                dve.wait_ge(s_g[n % NB], 16 * (n // NB + 1))
                if n % TOPK:
                    dve.wait_ge(s_sum, n)
                dve.scalar_tensor_tensor(x[:, t], yg[n % NB][:], wv[:, n:n + 1], x[:, t], ALU.mult, ALU.add).then_inc(s_sum, 1)

        @block.sync
        def _(sp):
            o = out.rearrange("a (t p) n -> p (a t) n", p=P)
            for t in range(NT):
                sp.wait_ge(s_sum, TOPK * (t + 1))
                sp.dma_start(o[:, t], x[:, t]).then_inc(s_out, 16)
            sp.wait_ge(s_out, 16 * NT)


CONSTS = ["ident", "upto", "after", "before", "levels"]


def load_constants(nc, a, d, x, buf, s_zeroed):
    consts = {
        "ident": a.sb("ident", [P, P]),
        "upto": a.sb("upto", [P, P]),
        "after": a.sb("after", [P, P]),
        "before": a.sb("before", [P, P]),
        "levels": a.sb("levels", [P, LEVELS, P]),
    }
    s_x, s_zero = a.sem("x_loaded"), a.sem("zero_row_ready")
    zeros = a.sb("zeros", [P, D])
    s_const = [a.sem(f"const_{n}_loaded") for n in CONSTS]
    with nc.Block() as block:
        @block.sync
        def _(sp):
            sp.dma_start(x[:], d["x"].rearrange("(t p) n -> p t n", p=P)).then_inc(s_x, 16)
            for n, s in zip(CONSTS, s_const):
                sp.dma_start(consts[n][:], d[n]).then_inc(s, 16)
            sp.wait_ge(s_zero, 1)
            sp.dma_start(buf.rearrange("(p r) n -> p r n", p=P),
                         zeros[:].unsqueeze(1).to_broadcast([P, E * CAP // P, D])).then_inc(s_zeroed, 16)
            for s in s_const:
                sp.wait_ge(s, 16)
            sp.wait_ge(s_x, 16)

        @block.gpsimd
        def _(pool):
            pool.memset(zeros[:], 0.0).then_inc(s_zero, 1)

    return consts


def program(nc, d, out, stages=4):
    with ExitStack() as stack:
        a = Alloc(nc, stack, "main")
        Alloc.psum_banks = stack.enter_context(nc.psum_tensor("psum_banks", [P, 8, 512], F32))
        x = a.sb("x", [P, NT, D])
        hT = a.sb("hT", [P, KD, T])
        buf = nc.dram_tensor("expert_rows", (E * CAP, D), F32, kind="Internal").ap()
        ybuf = nc.dram_tensor("expert_out", (E * CAP, D), F32, kind="Internal").ap()
        s_zeroed = a.sem("expert_rows_zeroed")
        consts = load_constants(nc, a, d, x, buf, s_zeroed)
        gated_delta(nc, x, hT, consts, d)
        w_gu = a.sb("w_gu", [P, E, KD, 2 * FE])
        gu_loaded = [a.sem(f"w_gu{i}_loaded") for i in range(4)]

        def load_experts(sp):
            for i, s in enumerate(gu_loaded):
                n = E // len(gu_loaded)
                sp.dma_start(w_gu[:, i * n:(i + 1) * n], d["w_gu"][:, i * n:(i + 1) * n]).then_inc(s, 16)

        if stages >= 2:
            perceptron(nc, x, hT, consts, d, load_experts)
        if stages >= 3:
            attention(nc, x, hT, consts, d)
        if stages >= 4:
            mixture(nc, x, hT, consts, d, w_gu, gu_loaded, buf, ybuf, s_zeroed, out)
            return
        s_out = a.sem("out_written")
        with nc.Block() as block:
            @block.sync
            def _(sp):
                sp.dma_start(out.rearrange("a (t p) n -> p (a t) n", p=P), x[:]).then_inc(s_out, 16)
                sp.wait_ge(s_out, 16)


def shape_constants():
    import numpy as np
    j, i = np.indices((P, P))
    masks = []
    for lv in range(1, LEVELS + 1):
        s = 1 << (lv - 1)
        masks.append((j // (2 * s) == i // (2 * s)) & (j % (2 * s) < s) & (i % (2 * s) >= s))
    f = np.float32
    return {"ident": np.eye(P, dtype=f), "upto": (j <= i).astype(f), "after": (j > i).astype(f), "before": (j < i).astype(f),
            "levels": np.stack(masks, 1).astype(f)}


def layouts(inp):
    import numpy as np

    def rows(w):
        w = np.asarray(w)
        return w.reshape(w.shape[0] // P, P, -1).transpose(1, 0, 2)

    out = {"x": np.asarray(inp["L0_attn_hidden_states"]).reshape(T, D)}
    w = rows(inp["L0_attn_w_qkv"])
    q, k, v = w[..., :2048], w[..., 2048:4096], w[..., 4096:]
    q, k = (m.reshape(P, KD, HK, P) for m in (q, k))
    v = v.reshape(P, KD, HK, 2 * P)
    out["w_in"] = np.concatenate([k, q, v], -1).transpose(2, 0, 1, 3)
    out["w_z"] = rows(inp["L0_attn_w_z"]).reshape(P, KD, HK, 2 * P).transpose(2, 0, 1, 3)
    out["w_o"] = np.asarray(inp["L0_attn_w_out"]).reshape(HK, HD, P, D).transpose(0, 2, 1, 3)
    out["w_ba"] = np.concatenate([rows(inp["L0_attn_w_b"]), rows(inp["L0_attn_w_a"])], -1)
    cw = np.asarray(inp["L0_attn_conv_w"]).reshape(64, P, 4)
    blocks = [[HK + hk, hk, 2 * HK + 2 * hk, 2 * HK + 2 * hk + 1] for hk in range(HK)]
    out["conv_w"] = cw[np.array(blocks)].transpose(2, 0, 1, 3)
    out["dt_bias"] = np.asarray(inp["L0_attn_dt_bias"]).reshape(1, 32)
    out["A_log"] = np.asarray(inp["L0_attn_A_log"]).reshape(1, 32)
    out["gamma"] = np.asarray(inp["L0_attn_norm_gamma"]).reshape(P, 1)

    get = lambda n: np.asarray(inp[n])
    out["mlp_w1"], out["mlp_w2"], out["mlp_w3"] = (rows(get(f"L0_ffn_W{i}").T) for i in (1, 2, 3))
    out["mlp_b12"] = np.stack([get(f"L0_ffn_b{i}").reshape(NF, P).T for i in (1, 2)], 1)
    out["mlp_b3"] = get("L0_ffn_b3").reshape(1, D)
    for n in "qkvo":
        out[f"attn_w{n}"] = rows(get(f"L1_attn_W{n}"))
    out["attn_bqk"] = np.stack([get(f"L1_attn_b{n}").reshape(KD, P).T for n in "qk"], 1)
    out["attn_bv"], out["attn_bo"] = get("L1_attn_bv").reshape(1, D), get("L1_attn_bo").reshape(1, D)
    out["moe_w_norm"] = get("L1_ffn_w_norm").reshape(1, D)
    out["moe_w_r"] = np.concatenate([rows(get("L1_ffn_w_router")), rows(get("L1_ffn_w_shared_gate"))], -1)
    out["moe_iota"] = np.arange(E, dtype=np.float32).reshape(1, E)
    gu = np.concatenate([get("L1_ffn_w_gate"), get("L1_ffn_w_up")], -1)
    out["w_gu"] = gu.reshape(E, KD, P, 2 * FE).transpose(2, 0, 1, 3)
    out["w_down"] = get("L1_ffn_w_down").reshape(E, 2, FH, D).transpose(0, 2, 1, 3)
    out["sw_gu"] = np.stack([rows(get("L1_ffn_sw_gate")), rows(get("L1_ffn_sw_up"))], 1)
    down = get("L1_ffn_sw_down")
    tail = np.zeros((len(SH) * P, D), down.dtype)
    tail[:FS] = down
    out["sw_down"] = rows(tail)
    out.update(shape_constants())
    return {n: np.ascontiguousarray(v) for n, v in out.items()}


def kernel(**inputs):
    import concourse.bacc as _bacc
    from concourse import mybir as _mybir
    from concourse.bass_utils import run_bass_kernel_spmd as _run

    nc = _bacc.Bacc("TRN2", target_bir_lowering=False, num_devices=1)
    arrays = {f"in_{n}": v for n, v in layouts(inputs).items()}
    d = {n[3:]: nc.dram_tensor(n, v.shape, _mybir.dt.from_np(v.dtype), kind="ExternalInput").ap() for n, v in arrays.items()}
    out = nc.dram_tensor("out", (1, T, D), F32, kind="ExternalOutput").ap()
    program(nc, d, out)
    return _run(nc, [arrays], core_ids=[0]).results[0]["out"]
```
